# Optimizing a Trainium2 kernel written in Bass

```python
import numpy as np
import jax
import jax.numpy as jnp

def _softmax(x, axis=-1):
    return jax.nn.softmax(x, axis=axis)

def _gelu(x):
    return jax.nn.gelu(x, approximate=True)

def _silu(x):
    return jax.nn.silu(x)

def _sigmoid(x):
    return jax.nn.sigmoid(x)

def _layernorm(x, axis=-1, eps=1e-05):
    m = jnp.mean(x, axis=axis, keepdims=True)
    v = jnp.var(x, axis=axis, keepdims=True)
    return (x - m) / jnp.sqrt(v + eps)

def _scatter_add(tgt, idx, src, axis=0):
    return tgt.at[idx].add(src)

def _segment_sum(src, seg, n):
    return jax.ops.segment_sum(src, seg, n)
kernel_name = 'mk_gnn_ffn_d4_gnn_r32_e32897'

def setup_inputs(seed: int=0):
    np.random.seed(seed)
    _w = jnp.asarray

    def _rec_inputs():
        import jax
        import jax.numpy as jnp
        _gk = jax.random.key(seed)
        x = -8.776e-05 + 1 * jax.random.normal(jax.random.fold_in(_gk, 1), (625, 256), jnp.float32)
        _s = jax.random.randint(jax.random.fold_in(_gk, 2), (10000,), 0, 625, jnp.int32)
        _d = jax.random.randint(jax.random.fold_in(_gk, 3), (10000,), 0, 625, jnp.int32)
        _loop = jnp.arange(625, dtype=jnp.int32)
        src = jnp.concatenate([_s, _d, _loop])
        dst = jnp.concatenate([_d, _s, _loop])
        _o = jnp.argsort(dst, stable=True)
        src = src[_o]
        dst = dst[_o]
        edge_type_8 = jax.random.randint(jax.random.fold_in(_gk, 13), (20625,), 0, 8, jnp.int32)
        edge_weight1 = jax.random.uniform(jax.random.fold_in(_gk, 14), (20625, 1), jnp.float32, 0.0, 0.999994)
        return (x, src, dst, edge_type_8, edge_weight1)
    x, src, dst, edge_type_8, edge_weight1 = _rec_inputs()

    def _L0_gnn_setup():
        import jax, jax.numpy as jnp
        import numpy as np
        N = 625
        E = 20000
        D = 256
        H = 4
        Dh = 64
        L = 3
        BN_EPS = 1e-05

        def _transformer_conv(x, src, dst, Wq, bq, Wk, bk, Wv, bv, Ws, bs):
            q = (x @ Wq + bq).reshape(N, H, Dh)
            k = (x @ Wk + bk).reshape(N, H, Dh)
            v = (x @ Wv + bv).reshape(N, H, Dh)
            qd = q[dst]
            ks_ = k[src]
            score = jnp.einsum('ehd,ehd->eh', qd, ks_) / np.sqrt(Dh)
            m = jax.ops.segment_max(score, dst, num_segments=N)
            ex = jnp.exp(score - m[dst])
            denom = jax.ops.segment_sum(ex, dst, num_segments=N)
            alpha = ex / denom[dst]
            msg = alpha[:, :, None] * v[src]
            out = jax.ops.segment_sum(msg, dst, num_segments=N)
            out = out.reshape(N, H * Dh)
            return out + x @ Ws + bs

        def _batch_norm(x, gamma, beta):
            mean = jnp.mean(x, axis=0)
            var = jnp.var(x, axis=0)
            return gamma * (x - mean) * jax.lax.rsqrt(var + BN_EPS) + beta
        key = jax.random.key(seed)
        ks = jax.random.split(key, 14)
        s = 1.0 / np.sqrt(D)
        f32 = jnp.float32
        return {'x': jax.random.normal(ks[0], (N, D), f32), 'edge_index': jax.random.randint(ks[1], (2, E), 0, N, dtype=jnp.int32), 'Wq': jax.random.normal(ks[2], (L, D, D), f32) * s, 'bq': jax.random.normal(ks[3], (L, D), f32) * 0.02, 'Wk': jax.random.normal(ks[4], (L, D, D), f32) * s, 'bk': jax.random.normal(ks[5], (L, D), f32) * 0.02, 'Wv': jax.random.normal(ks[6], (L, D, D), f32) * s, 'bv': jax.random.normal(ks[7], (L, D), f32) * 0.02, 'Ws': jax.random.normal(ks[8], (L, D, D), f32) * s, 'bs': jax.random.normal(ks[9], (L, D), f32) * 0.02, 'bn_gamma': 1.0 + 0.1 * jax.random.normal(ks[10], (L - 1, D), f32), 'bn_beta': 0.1 * jax.random.normal(ks[11], (L - 1, D), f32)}
    _L0_gnn_all = _L0_gnn_setup()
    _L0_gnn_in = {k: v for k, v in _L0_gnn_all.items() if k in ('Wq', 'bq', 'Wk', 'bk', 'Wv', 'bv', 'Ws', 'bs', 'bn_gamma', 'bn_beta')}
    del _L0_gnn_all

    def _L0_ffn_setup():
        import jax, jax.numpy as jnp
        import numpy as np
        TOP_K = 2
        LN_EPS = 1e-05
        key = jax.random.key(seed)
        ks = jax.random.split(key, 8)
        B, S, D, E, H = (16, 1024, 256, 8, 1024)
        x = jax.random.normal(ks[0], (B, S, D), dtype=jnp.float32)
        Wr = jax.random.normal(ks[1], (D, E), dtype=jnp.float32) * 0.1
        br = jnp.zeros((E,), dtype=jnp.float32)
        ln_g = jnp.ones((E, D), dtype=jnp.float32)
        ln_b = jnp.zeros((E, D), dtype=jnp.float32)
        W1 = jax.random.normal(ks[2], (E, D, H), dtype=jnp.float32) * (1.0 / np.sqrt(D))
        b1 = jnp.zeros((E, H), dtype=jnp.float32)
        W2 = jax.random.normal(ks[3], (E, H, D), dtype=jnp.float32) * (1.0 / np.sqrt(H))
        b2 = jnp.zeros((E, D), dtype=jnp.float32)
        return {'x': x, 'Wr': Wr, 'br': br, 'ln_g': ln_g, 'ln_b': ln_b, 'W1': W1, 'b1': b1, 'W2': W2, 'b2': b2}
    _L0_ffn_all = _L0_ffn_setup()
    _L0_ffn_in = {k: v for k, v in _L0_ffn_all.items() if k in ('Wr', 'br', 'ln_g', 'ln_b', 'W1', 'b1', 'W2', 'b2')}
    del _L0_ffn_all

    def _L1_gnn_setup():
        import jax, jax.numpy as jnp
        import numpy as np
        N_NODES = 3125
        N_EDGES = 100000
        NFEAT = 256
        NHID = 256
        key = jax.random.key(seed)
        k_x, k_ws, k_wn, k_src, k_dst = jax.random.split(key, 5)
        x = jax.random.normal(k_x, (N_NODES, NFEAT), dtype=jnp.float32)
        W_self = jax.random.normal(k_ws, (NFEAT, NHID), dtype=jnp.float32) * (1.0 / np.sqrt(NFEAT))
        W_neigh = jax.random.normal(k_wn, (NFEAT, NHID), dtype=jnp.float32) * (1.0 / np.sqrt(NFEAT))
        b = jnp.zeros((NHID,), dtype=jnp.float32)
        edge_src = jax.random.randint(k_src, (N_EDGES,), 0, N_NODES, dtype=jnp.int32)
        edge_dst = jax.random.randint(k_dst, (N_EDGES,), 0, N_NODES, dtype=jnp.int32)
        return {'x': x, 'W_self': W_self, 'W_neigh': W_neigh, 'b': b, 'edge_src': edge_src, 'edge_dst': edge_dst}
    _L1_gnn_all = _L1_gnn_setup()
    _L1_gnn_in = {k: v for k, v in _L1_gnn_all.items() if k in ('W_self', 'W_neigh', 'b')}
    del _L1_gnn_all

    def _L1_ffn_setup():
        import math
        import jax, jax.numpy as jnp
        import numpy as np
        CAPACITY_FACTOR = 1.25
        TOP_K = 2
        LN_EPS = 1e-05

        def _layer_norm(x, gamma, beta):
            mu = jnp.mean(x, axis=-1, keepdims=True)
            var = jnp.var(x, axis=-1, keepdims=True)
            return (x - mu) * jax.lax.rsqrt(var + LN_EPS) * gamma + beta
        key = jax.random.key(seed)
        ks = jax.random.split(key, 4)
        B, S, D, F, E = (8, 128, 256, 512, 8)
        x = jax.random.normal(ks[0], (B, S, D), dtype=jnp.float32)
        Wr = jax.random.normal(ks[1], (D, E), dtype=jnp.float32) / np.sqrt(D)
        br = jnp.zeros((E,), jnp.float32)
        W1 = jax.random.normal(ks[2], (E, D, F), dtype=jnp.float32) / np.sqrt(D)
        b1 = jnp.zeros((E, F), jnp.float32)
        W2 = jax.random.normal(ks[3], (E, F, D), dtype=jnp.float32) / np.sqrt(F)
        b2 = jnp.zeros((E, D), jnp.float32)
        gamma = jnp.ones((D,), jnp.float32)
        beta = jnp.zeros((D,), jnp.float32)
        return {'x': x, 'Wr': Wr, 'br': br, 'W1': W1, 'b1': b1, 'W2': W2, 'b2': b2, 'gamma': gamma, 'beta': beta}
    _L1_ffn_all = _L1_ffn_setup()
    _L1_ffn_in = {k: v for k, v in _L1_ffn_all.items() if k in ('Wr', 'br', 'W1', 'b1', 'W2', 'b2', 'gamma', 'beta')}
    del _L1_ffn_all

    def _L2_gnn_setup():
        import jax, jax.numpy as jnp
        import numpy as np
        N_NODES = 625
        N_EDGES = 10000
        D = 256
        R = 8
        B = 8
        L = 2
        key = jax.random.key(seed)
        ks = jax.random.split(key, 8)
        feat = jax.random.normal(ks[0], (N_NODES, D), dtype=jnp.float32)
        norm = jax.random.uniform(ks[1], (N_EDGES, 1), dtype=jnp.float32)
        basis = jax.random.normal(ks[2], (L, B, D, D), dtype=jnp.float32) * 0.02
        coeff = jax.random.normal(ks[3], (L, R, B), dtype=jnp.float32)
        bias = jnp.zeros((L, D), dtype=jnp.float32)
        src = jax.random.randint(ks[4], (N_EDGES,), 0, N_NODES, dtype=jnp.int32)
        dst = jax.random.randint(ks[5], (N_EDGES,), 0, N_NODES, dtype=jnp.int32)
        etype = jax.random.randint(ks[6], (N_EDGES,), 0, R, dtype=jnp.int32)
        return {'feat': feat, 'norm': norm, 'basis': basis, 'coeff': coeff, 'bias': bias, 'src': src, 'dst': dst, 'etype': etype}
    _L2_gnn_all = _L2_gnn_setup()
    _L2_gnn_in = {k: v for k, v in _L2_gnn_all.items() if k in ('basis', 'coeff', 'bias')}
    del _L2_gnn_all

    def _L2_ffn_setup():
        import jax, jax.numpy as jnp
        import numpy as np
        B, T, C = (64, 384, 256)
        NH, NKV = (4, 2)
        HD = C // NH
        NREP = NH // NKV
        NE, TOPK = (8, 2)
        HID = int(8 / 3 * C)
        EPS_RMS = 1e-06

        def _rope_tables(t_len):
            inv_freq = 1.0 / 10000.0 ** (np.arange(0, HD, 2, dtype=np.float32) / HD)
            t = np.arange(t_len, dtype=np.float32)
            freqs = np.outer(t, inv_freq)
            emb = np.concatenate([freqs, freqs], axis=-1)
            return (jnp.asarray(np.cos(emb)), jnp.asarray(np.sin(emb)))

        def _rotate_half(x):
            h = x.shape[-1] // 2
            return jnp.concatenate([-x[..., h:], x[..., :h]], axis=-1)

        def _rmsnorm(v, w):
            return v * jax.lax.rsqrt(jnp.mean(v * v, axis=-1, keepdims=True) + EPS_RMS) * w
        key = jax.random.key(seed)
        ks = jax.random.split(key, 10)
        s = lambda k, shape: jax.random.normal(k, shape, jnp.float32) * 0.02
        return {'x': jax.random.normal(ks[0], (B, T, C), jnp.float32), 'ln1_w': jnp.ones((C,), jnp.float32), 'ln2_w': jnp.ones((C,), jnp.float32), 'wq': s(ks[1], (NH * HD, C)), 'wk': s(ks[2], (NKV * HD, C)), 'wv': s(ks[3], (NKV * HD, C)), 'wo': s(ks[4], (C, C)), 'router_w': s(ks[5], (NE, C)), 'w1': s(ks[6], (NE, HID, C)), 'w2': s(ks[7], (NE, C, HID)), 'w3': s(ks[8], (NE, HID, C))}
    _L2_ffn_all = _L2_ffn_setup()
    _L2_ffn_in = {k: v for k, v in _L2_ffn_all.items() if k in ('ln1_w', 'ln2_w', 'wq', 'wk', 'wv', 'wo', 'router_w', 'w1', 'w2', 'w3')}
    del _L2_ffn_all

    def _L3_gnn_setup():
        import jax, jax.numpy as jnp
        import numpy as np
        N_NODES = 512
        D_FEAT = 256
        N_EDGES = 8192
        HIDDEN = 512
        D_OUT = 256
        key = jax.random.key(seed)
        ks = jax.random.split(key, 5)
        x = jax.random.normal(ks[0], (N_NODES, D_FEAT), dtype=jnp.float32)
        W1 = jax.random.normal(ks[1], (2 * D_FEAT, HIDDEN), dtype=jnp.float32) * (1.0 / np.sqrt(2 * D_FEAT))
        b1 = jnp.zeros((HIDDEN,), dtype=jnp.float32)
        W2 = jax.random.normal(ks[2], (HIDDEN, D_OUT), dtype=jnp.float32) * (1.0 / np.sqrt(HIDDEN))
        b2 = jnp.zeros((D_OUT,), dtype=jnp.float32)
        nn_index = jax.random.randint(ks[3], (2, N_EDGES), 0, N_NODES, dtype=jnp.int64)
        return {'x': x, 'W1': W1, 'b1': b1, 'W2': W2, 'b2': b2, 'nn_index': nn_index, 'k': 16}
    _L3_gnn_all = _L3_gnn_setup()
    _L3_gnn_in = {k: v for k, v in _L3_gnn_all.items() if k in ('W1', 'b1', 'W2', 'b2')}
    del _L3_gnn_all

    def _L3_ffn_setup():
        import jax, jax.numpy as jnp
        import numpy as np
        C = 256
        HID = 1024
        E = 8
        TEMP = 1.0
        key = jax.random.key(seed)
        ks = jax.random.split(key, 7)
        x = jax.random.normal(ks[0], (8, 512, C), dtype=jnp.float32)
        W1 = jax.random.normal(ks[1], (C, HID), dtype=jnp.float32) * 0.02
        b1 = jnp.zeros((HID,), dtype=jnp.float32)
        Wg = jax.random.normal(ks[2], (HID, E), dtype=jnp.float32) * 0.02
        bg = jnp.zeros((E,), dtype=jnp.float32)
        Wd = jax.random.normal(ks[3], (E, HID, C), dtype=jnp.float32) * 0.02
        bd = jnp.zeros((E, C), dtype=jnp.float32)
        return {'x': x, 'W1': W1, 'b1': b1, 'Wg': Wg, 'bg': bg, 'Wd': Wd, 'bd': bd}
    _L3_ffn_all = _L3_ffn_setup()
    _L3_ffn_in = {k: v for k, v in _L3_ffn_all.items() if k in ('W1', 'b1', 'Wg', 'bg', 'Wd', 'bd')}
    del _L3_ffn_all
    return {'x': x, 'src': src, 'dst': dst, 'edge_type_8': edge_type_8, 'edge_weight1': edge_weight1, 'L0_gnn_Wq': _L0_gnn_in['Wq'], 'L0_gnn_bq': _L0_gnn_in['bq'], 'L0_gnn_Wk': _L0_gnn_in['Wk'], 'L0_gnn_bk': _L0_gnn_in['bk'], 'L0_gnn_Wv': _L0_gnn_in['Wv'], 'L0_gnn_bv': _L0_gnn_in['bv'], 'L0_gnn_Ws': _L0_gnn_in['Ws'], 'L0_gnn_bs': _L0_gnn_in['bs'], 'L0_gnn_bn_gamma': _L0_gnn_in['bn_gamma'], 'L0_gnn_bn_beta': _L0_gnn_in['bn_beta'], 'L0_ffn_Wr': _L0_ffn_in['Wr'], 'L0_ffn_br': _L0_ffn_in['br'], 'L0_ffn_ln_g': _L0_ffn_in['ln_g'], 'L0_ffn_ln_b': _L0_ffn_in['ln_b'], 'L0_ffn_W1': _L0_ffn_in['W1'], 'L0_ffn_b1': _L0_ffn_in['b1'], 'L0_ffn_W2': _L0_ffn_in['W2'], 'L0_ffn_b2': _L0_ffn_in['b2'], 'L1_gnn_W_self': _L1_gnn_in['W_self'], 'L1_gnn_W_neigh': _L1_gnn_in['W_neigh'], 'L1_gnn_b': _L1_gnn_in['b'], 'L1_ffn_Wr': _L1_ffn_in['Wr'], 'L1_ffn_br': _L1_ffn_in['br'], 'L1_ffn_W1': _L1_ffn_in['W1'], 'L1_ffn_b1': _L1_ffn_in['b1'], 'L1_ffn_W2': _L1_ffn_in['W2'], 'L1_ffn_b2': _L1_ffn_in['b2'], 'L1_ffn_gamma': _L1_ffn_in['gamma'], 'L1_ffn_beta': _L1_ffn_in['beta'], 'L2_gnn_basis': _L2_gnn_in['basis'], 'L2_gnn_coeff': _L2_gnn_in['coeff'], 'L2_gnn_bias': _L2_gnn_in['bias'], 'L2_ffn_ln1_w': _L2_ffn_in['ln1_w'], 'L2_ffn_ln2_w': _L2_ffn_in['ln2_w'], 'L2_ffn_wq': _L2_ffn_in['wq'], 'L2_ffn_wk': _L2_ffn_in['wk'], 'L2_ffn_wv': _L2_ffn_in['wv'], 'L2_ffn_wo': _L2_ffn_in['wo'], 'L2_ffn_router_w': _L2_ffn_in['router_w'], 'L2_ffn_w1': _L2_ffn_in['w1'], 'L2_ffn_w2': _L2_ffn_in['w2'], 'L2_ffn_w3': _L2_ffn_in['w3'], 'L3_gnn_W1': _L3_gnn_in['W1'], 'L3_gnn_b1': _L3_gnn_in['b1'], 'L3_gnn_W2': _L3_gnn_in['W2'], 'L3_gnn_b2': _L3_gnn_in['b2'], 'L3_ffn_W1': _L3_ffn_in['W1'], 'L3_ffn_b1': _L3_ffn_in['b1'], 'L3_ffn_Wg': _L3_ffn_in['Wg'], 'L3_ffn_bg': _L3_ffn_in['bg'], 'L3_ffn_Wd': _L3_ffn_in['Wd'], 'L3_ffn_bd': _L3_ffn_in['bd']}

def reference(x, src, dst, edge_type_8, edge_weight1, L0_gnn_Wq, L0_gnn_bq, L0_gnn_Wk, L0_gnn_bk, L0_gnn_Wv, L0_gnn_bv, L0_gnn_Ws, L0_gnn_bs, L0_gnn_bn_gamma, L0_gnn_bn_beta, L0_ffn_Wr, L0_ffn_br, L0_ffn_ln_g, L0_ffn_ln_b, L0_ffn_W1, L0_ffn_b1, L0_ffn_W2, L0_ffn_b2, L1_gnn_W_self, L1_gnn_W_neigh, L1_gnn_b, L1_ffn_Wr, L1_ffn_br, L1_ffn_W1, L1_ffn_b1, L1_ffn_W2, L1_ffn_b2, L1_ffn_gamma, L1_ffn_beta, L2_gnn_basis, L2_gnn_coeff, L2_gnn_bias, L2_ffn_ln1_w, L2_ffn_ln2_w, L2_ffn_wq, L2_ffn_wk, L2_ffn_wv, L2_ffn_wo, L2_ffn_router_w, L2_ffn_w1, L2_ffn_w2, L2_ffn_w3, L3_gnn_W1, L3_gnn_b1, L3_gnn_W2, L3_gnn_b2, L3_ffn_W1, L3_ffn_b1, L3_ffn_Wg, L3_ffn_bg, L3_ffn_Wd, L3_ffn_bd):
    import jax
    import jax.numpy as jnp

    def _L0_gnn_ref(x, edge_index, Wq, bq, Wk, bk, Wv, bv, Ws, bs, bn_gamma, bn_beta):
        import jax, jax.numpy as jnp
        import numpy as np
        N = 625
        E = 20000
        D = 256
        H = 4
        Dh = 64
        L = 3
        BN_EPS = 1e-05

        def _transformer_conv(x, src, dst, Wq, bq, Wk, bk, Wv, bv, Ws, bs):
            q = (x @ Wq + bq).reshape(N, H, Dh)
            k = (x @ Wk + bk).reshape(N, H, Dh)
            v = (x @ Wv + bv).reshape(N, H, Dh)
            qd = q[dst]
            ks_ = k[src]
            score = jnp.einsum('ehd,ehd->eh', qd, ks_) / np.sqrt(Dh)
            m = jax.ops.segment_max(score, dst, num_segments=N)
            ex = jnp.exp(score - m[dst])
            denom = jax.ops.segment_sum(ex, dst, num_segments=N)
            alpha = ex / denom[dst]
            msg = alpha[:, :, None] * v[src]
            out = jax.ops.segment_sum(msg, dst, num_segments=N)
            out = out.reshape(N, H * Dh)
            return out + x @ Ws + bs

        def _batch_norm(x, gamma, beta):
            mean = jnp.mean(x, axis=0)
            var = jnp.var(x, axis=0)
            return gamma * (x - mean) * jax.lax.rsqrt(var + BN_EPS) + beta
        src, dst = (edge_index[0], edge_index[1])
        for i in range(L):
            x = _transformer_conv(x, src, dst, Wq[i], bq[i], Wk[i], bk[i], Wv[i], bv[i], Ws[i], bs[i])
            if i < L - 1:
                x = jax.nn.relu(_batch_norm(x, bn_gamma[i], bn_beta[i]))
        return x

    def _L0_ffn_ref(x, Wr, br, ln_g, ln_b, W1, b1, W2, b2):
        import jax, jax.numpy as jnp
        import numpy as np
        TOP_K = 2
        LN_EPS = 1e-05
        B, S, D = x.shape
        N = B * S
        xt = x.reshape(N, D)
        logits = xt @ Wr + br
        probs = jax.nn.softmax(logits, axis=-1)
        top_p, top_idx = jax.lax.top_k(probs, TOP_K)
        weights = top_p / top_p.sum(axis=-1, keepdims=True)
        mu = xt.mean(axis=-1, keepdims=True)
        var = ((xt - mu) ** 2).mean(axis=-1, keepdims=True)
        xn = (xt - mu) * jax.lax.rsqrt(var + LN_EPS)
        xe = xn[None, :, :] * ln_g[:, None, :] + ln_b[:, None, :]
        h = jax.nn.gelu(jnp.einsum('end,edh->enh', xe, W1) + b1[:, None, :], approximate=False)
        y = jnp.einsum('enh,ehd->end', h, W2) + b2[:, None, :]
        y_tok = jnp.transpose(y, (1, 0, 2))
        sel = jnp.take_along_axis(y_tok, top_idx[:, :, None], axis=1)
        out = (weights[:, :, None] * sel).sum(axis=1)
        return out.reshape(B, S, D)

    def _L1_gnn_ref(x, W_self, W_neigh, b, edge_src, edge_dst):
        import jax, jax.numpy as jnp
        import numpy as np
        N_NODES = 3125
        N_EDGES = 100000
        NFEAT = 256
        NHID = 256
        n = x.shape[0]
        msg = x[edge_src]
        agg = jax.ops.segment_sum(msg, edge_dst, num_segments=n)
        deg = jax.ops.segment_sum(jnp.ones_like(edge_dst, dtype=x.dtype), edge_dst, num_segments=n)
        h_neigh = agg / jnp.maximum(deg, 1.0)[:, None]
        out = x @ W_self + h_neigh @ W_neigh + b
        return jax.nn.relu(out)

    def _L1_ffn_ref(x, Wr, br, W1, b1, W2, b2, gamma, beta):
        import math
        import jax, jax.numpy as jnp
        import numpy as np
        CAPACITY_FACTOR = 1.25
        TOP_K = 2
        LN_EPS = 1e-05

        def _layer_norm(x, gamma, beta):
            mu = jnp.mean(x, axis=-1, keepdims=True)
            var = jnp.var(x, axis=-1, keepdims=True)
            return (x - mu) * jax.lax.rsqrt(var + LN_EPS) * gamma + beta
        B, S, D = x.shape
        E = Wr.shape[1]
        N = B * S
        K = TOP_K
        logits = jnp.mean(x, axis=1) @ Wr + br
        routing_weights = jax.nn.softmax(logits, axis=-1)
        capacity = float(math.ceil(N * CAPACITY_FACTOR / E))
        expected_loads = routing_weights.sum(axis=0) * (N / B)
        scale = jnp.where(expected_loads > capacity, capacity / expected_loads, 1.0)
        routing_weights = jax.nn.softmax(routing_weights * scale, axis=-1)
        rw_tok = jnp.broadcast_to(routing_weights[:, None, :], (B, S, E)).reshape(N, E)
        top_w, top_i = jax.lax.top_k(rw_tok, K)
        top_w = jax.nn.softmax(top_w, axis=-1)
        xf = x.reshape(N, D)
        h = jax.nn.gelu(jnp.einsum('nd,edf->enf', xf, W1) + b1[:, None, :], approximate=False)
        y = jnp.einsum('enf,efd->end', h, W2) + b2[:, None, :]
        w_dense = jnp.zeros((N, E), x.dtype).at[jnp.arange(N)[:, None], top_i].add(top_w)
        out = jnp.einsum('ne,end->nd', w_dense, y).reshape(B, S, D)
        out = _layer_norm(out + x, gamma, beta)
        return out

    def _L2_gnn_ref(feat, norm, basis, coeff, bias, src, dst, etype):
        import jax, jax.numpy as jnp
        import numpy as np
        N_NODES = 625
        N_EDGES = 10000
        D = 256
        R = 8
        B = 8
        L = 2
        'Stacked RelGraphConv (basis regularizer, self_loop=False, bias=True),\n            ReLU between layers, none after the last layer.'
        h = feat
        for l in range(L):
            W = jnp.einsum('rb,bio->rio', coeff[l], basis[l])
            all_h = jnp.einsum('ni,rio->rno', h, W)
            msg = all_h[etype, src] * norm
            agg = jax.ops.segment_sum(msg, dst, num_segments=N_NODES)
            h = agg + bias[l]
            if l < L - 1:
                h = jax.nn.relu(h)
        return h

    def _L2_ffn_ref(x, ln1_w, ln2_w, wq, wk, wv, wo, router_w, w1, w2, w3):
        import jax, jax.numpy as jnp
        import numpy as np
        B, T, C = (64, 384, 256)
        NH, NKV = (4, 2)
        HD = C // NH
        NREP = NH // NKV
        NE, TOPK = (8, 2)
        HID = int(8 / 3 * C)
        EPS_RMS = 1e-06

        def _rope_tables(t_len):
            inv_freq = 1.0 / 10000.0 ** (np.arange(0, HD, 2, dtype=np.float32) / HD)
            t = np.arange(t_len, dtype=np.float32)
            freqs = np.outer(t, inv_freq)
            emb = np.concatenate([freqs, freqs], axis=-1)
            return (jnp.asarray(np.cos(emb)), jnp.asarray(np.sin(emb)))

        def _rotate_half(x):
            h = x.shape[-1] // 2
            return jnp.concatenate([-x[..., h:], x[..., :h]], axis=-1)

        def _rmsnorm(v, w):
            return v * jax.lax.rsqrt(jnp.mean(v * v, axis=-1, keepdims=True) + EPS_RMS) * w
        Bx, Tx, Cx = x.shape
        h = _rmsnorm(x, ln1_w)
        q = (h @ wq.T).reshape(Bx, Tx, NH, HD).transpose(0, 2, 1, 3)
        k = (h @ wk.T).reshape(Bx, Tx, NKV, HD).transpose(0, 2, 1, 3)
        v = (h @ wv.T).reshape(Bx, Tx, NKV, HD).transpose(0, 2, 1, 3)
        cos, sin = _rope_tables(Tx)
        cos, sin = (cos[None, None], sin[None, None])
        q = q * cos + _rotate_half(q) * sin
        k = k * cos + _rotate_half(k) * sin
        k = jnp.repeat(k, NREP, axis=1)
        v = jnp.repeat(v, NREP, axis=1)
        scores = jnp.einsum('bhtd,bhsd->bhts', q, k) / jnp.sqrt(jnp.float32(HD))
        causal = jnp.tril(jnp.ones((Tx, Tx), dtype=bool))
        scores = jnp.where(causal[None, None], scores, jnp.float32(-1e+30))
        att = jax.nn.softmax(scores, axis=-1)
        y = jnp.einsum('bhts,bhsd->bhtd', att, v).transpose(0, 2, 1, 3).reshape(Bx, Tx, Cx)
        x = x + y @ wo.T
        flat = _rmsnorm(x, ln2_w).reshape(-1, Cx)
        probs = jax.nn.softmax(flat @ router_w.T, axis=-1)
        tp, ti = jax.lax.top_k(probs, TOPK)
        tp = tp / (jnp.sum(tp, axis=-1, keepdims=True) + 1e-09)
        weights = jnp.sum(tp[..., None] * jax.nn.one_hot(ti, NE, dtype=flat.dtype), axis=1)
        out = jnp.zeros_like(flat)
        for e in range(NE):
            hh = jax.nn.silu(flat @ w1[e].T) * (flat @ w3[e].T)
            out = out + weights[:, e:e + 1] * (hh @ w2[e].T)
        return x + out.reshape(Bx, Tx, Cx)

    def _L3_gnn_ref(x, W1, b1, W2, b2, nn_index, k):
        import jax, jax.numpy as jnp
        import numpy as np
        N_NODES = 512
        D_FEAT = 256
        N_EDGES = 8192
        HIDDEN = 512
        D_OUT = 256
        num_nodes = x.shape[0]
        src = nn_index[0]
        tgt = nn_index[1]
        x_i = x[tgt]
        x_j = x[src]
        feat = jnp.concatenate([x_i, x_j - x_i], axis=-1)
        h = jax.nn.relu(feat @ W1 + b1)
        msg = h @ W2 + b2
        out = jax.ops.segment_sum(msg, tgt, num_segments=num_nodes)
        deg = jax.ops.segment_sum(jnp.ones((msg.shape[0], 1), dtype=msg.dtype), tgt, num_segments=num_nodes)
        return out / (deg + 1e-08)

    def _L3_ffn_ref(x, W1, b1, Wg, bg, Wd, bd):
        import jax, jax.numpy as jnp
        import numpy as np
        C = 256
        HID = 1024
        E = 8
        TEMP = 1.0
        orig_shape = x.shape
        xf = x.reshape(-1, orig_shape[-1])
        H = jax.nn.gelu(xf @ W1 + b1, approximate=False)
        probs = jax.nn.softmax((H @ Wg + bg) / TEMP, axis=-1)
        assign = jnp.argmax(probs, axis=-1)
        out = jnp.zeros_like(xf)
        for e in range(Wd.shape[0]):
            y = H @ Wd[e] + bd[e]
            sel = (assign == e)[:, None]
            out = out + jnp.where(sel, probs[:, e:e + 1] * y, 0.0)
        return out.reshape(orig_shape)
    edge_index = jnp.stack([src, dst])
    x = x + _L0_gnn_ref(_layernorm(x, axis=-1), edge_index, L0_gnn_Wq, L0_gnn_bq, L0_gnn_Wk, L0_gnn_bk, L0_gnn_Wv, L0_gnn_bv, L0_gnn_Ws, L0_gnn_bs, L0_gnn_bn_gamma, L0_gnn_bn_beta)
    x = x + _L0_ffn_ref(_layernorm(x, axis=-1)[None], L0_ffn_Wr, L0_ffn_br, L0_ffn_ln_g, L0_ffn_ln_b, L0_ffn_W1, L0_ffn_b1, L0_ffn_W2, L0_ffn_b2)[0]
    x = x + _L1_gnn_ref(_layernorm(x, axis=-1), L1_gnn_W_self, L1_gnn_W_neigh, L1_gnn_b, src, dst)
    x = x + _L1_ffn_ref(_layernorm(x, axis=-1)[None], L1_ffn_Wr, L1_ffn_br, L1_ffn_W1, L1_ffn_b1, L1_ffn_W2, L1_ffn_b2, L1_ffn_gamma, L1_ffn_beta)[0]
    x = x + _L2_gnn_ref(_layernorm(x, axis=-1), edge_weight1, L2_gnn_basis, L2_gnn_coeff, L2_gnn_bias, src, dst, edge_type_8)
    x = x + _L2_ffn_ref(_layernorm(x, axis=-1)[None], L2_ffn_ln1_w, L2_ffn_ln2_w, L2_ffn_wq, L2_ffn_wk, L2_ffn_wv, L2_ffn_wo, L2_ffn_router_w, L2_ffn_w1, L2_ffn_w2, L2_ffn_w3)[0]
    x = x + _L3_gnn_ref(_layernorm(x, axis=-1), L3_gnn_W1, L3_gnn_b1, L3_gnn_W2, L3_gnn_b2, edge_index, 16)
    x = x + _L3_ffn_ref(_layernorm(x, axis=-1)[None], L3_ffn_W1, L3_ffn_b1, L3_ffn_Wg, L3_ffn_bg, L3_ffn_Wd, L3_ffn_bd)[0]
    return x

_drawn_inputs = setup_inputs


def setup_inputs(seed=0):
    import zlib

    import numpy as np

    out = dict(_drawn_inputs(seed))
    spreads = {'L0_ffn_br': (0.0, 0.1),
     'L0_ffn_ln_g': (1.0, 0.2),
     'L0_ffn_ln_b': (0.0, 0.1),
     'L0_ffn_b1': (0.0, 0.1),
     'L0_ffn_b2': (0.0, 0.1),
     'L1_gnn_b': (0.0, 0.1),
     'L1_ffn_br': (0.0, 0.1),
     'L1_ffn_b1': (0.0, 0.356),
     'L1_ffn_b2': (0.0, 0.1),
     'L1_ffn_gamma': (1.0, 0.2),
     'L1_ffn_beta': (0.0, 0.1),
     'L2_gnn_bias': (0.0, 0.314),
     'L2_ffn_ln1_w': (1.0, 0.6),
     'L2_ffn_ln2_w': (1.0, 0.6),
     'L3_gnn_b1': (0.0, 2.0),
     'L3_gnn_b2': (0.0, 2.0),
     'L3_ffn_b1': (0.0, 0.8),
     'L3_ffn_bg': (0.0, 0.8),
     'L3_ffn_bd': (0.0, 2.0)}
    factors = {'L0_gnn_bq': 8.0,
     'L0_gnn_bk': 64.0,
     'L2_ffn_wq': 8.0,
     'L2_ffn_wk': 8.0,
     'L2_ffn_wv': 8.0,
     'L2_ffn_wo': 8.0,
     'L2_ffn_router_w': 8.0,
     'L2_ffn_w1': 8.0,
     'L2_ffn_w2': 8.0,
     'L2_ffn_w3': 8.0,
     'L3_ffn_W1': 8.0,
     'L3_ffn_Wg': 8.0,
     'L3_ffn_Wd': 8.0,
     'L3_gnn_W1': 3.397}
    for name, (base, spread) in spreads.items():
        noise = np.random.default_rng([zlib.crc32(name.encode()), seed]).standard_normal(out[name].shape)
        drawn = base * np.exp(spread * noise) if base else spread * noise
        out[name] = jnp.asarray(drawn.astype(out[name].dtype))
    for name, factor in factors.items():
        out[name] = (out[name] * factor).astype(out[name].dtype)
    return out
```

```python
import numpy as np
import concourse.bass as bass
from concourse import mybir
from contextlib import ExitStack

F32 = mybir.dt.float32
BF16 = mybir.dt.bfloat16
F16 = mybir.dt.float16
I32 = mybir.dt.int32
U32 = mybir.dt.uint32
ALU = mybir.AluOpType
ACT = mybir.ActivationFunctionType
AX = mybir.AxisListType

NODES = 625
NB = 5
NP = NODES // NB
NC = NODES + 1
HC = NC // 2
D = 256
KD = D // 128
EDGES = 20625
EP = 125
EC = EDGES // EP
LANES = 128
ET = -(-((EDGES + NB * (LANES - 1)) // LANES) // 4) * 4
AHEAD = 4
EXPERTS = 8
NEG = -1e30
LN_EPS = 1e-5

C_ID = 0
C_TRI = C_ID + 128
C_IOTA = C_TRI + 128
C_RANK = C_IOTA + NC
C_ROW = C_RANK + EXPERTS * EXPERTS
C_END = C_ROW + NB


def constants():
    c = np.zeros((128, C_END), np.float32)
    c[:, C_ID:C_ID + 128] = np.eye(128)
    c[:, C_TRI:C_TRI + 128] = np.triu(np.ones((128, 128)), 1)
    c[:, C_IOTA:C_IOTA + NC] = np.arange(NC)
    c[:, C_ROW:C_END] = np.arange(128)[:, None] + NP * np.arange(NB)
    c[:, C_RANK:C_ROW] = np.tril(np.ones((EXPERTS, EXPERTS)), -1).reshape(-1)
    return c


COLS = {"conv_bias": 3 * 3 * KD, "bn_gamma": 2 * KD, "bn_beta": 2 * KD, "moe0_ln_g": KD * (EXPERTS + 1),
        "moe0_ln_b": KD * (EXPERTS + 1), "moe0_b1": EXPERTS * 8, "moe3_b1": 8, "ln1_w": KD, "ln2_w": KD,
        "moe0_router": KD * EXPERTS, "moe1_router": KD * EXPERTS, "moe2_router": KD * EXPERTS,
        "moe3_router": 8 * EXPERTS}


def col(k, name, first=0, count=1):
    at = sum(w for n, w in COLS.items() if list(COLS).index(n) < list(COLS).index(name))
    if isinstance(first, int):
        return k.col[:, at + first:at + first + count]
    return k.col[:, bass.ds(first + at, count)]


class Kernel:

    def __init__(self, nc, ins, out):
        self.nc, self.ins, self.out = nc, ins, out
        self.all = ExitStack()
        self.layer_sems = []
        self.stack = self.all

    def sb(self, name, shape, dt=F32):
        return self.stack.enter_context(self.nc.sbuf_tensor(name, shape, dt))

    def sem(self, name):
        self.layer_sems.append(self.nc.alloc_semaphore(name))
        return self.layer_sems[-1]

    def end_layer(self):
        self.nc.clear_and_free_semaphores(self.layer_sems)
        self.nc.all_engine_barrier()
        self.layer_sems = []


class Chain:

    def __init__(self, eng, sem):
        self.eng, self.sem, self.n = eng, sem, 0

    def __call__(self, ins):
        ins.then_inc(self.sem, 1)
        self.n = self.n + 1
        self.eng.wait_ge(self.sem, self.n)


def open_slots(eng, *sems):
    for s in sems:
        eng.sem_inc(s, 1)


def edges(k):
    nc, P = k.nc, k.psum
    with ExitStack() as st:
        k.stack = st
        ints = k.sb("edge_ints", [EP, 3, EC], I32)
        flt = k.sb("edge_floats", [EP, 3, EC])
        ge = k.sb("edge_ge", [EP, NB + 1, EC])
        member = k.sb("edge_member", [EP, NB, EC])
        count = k.sb("edge_count", [EP, NB, EC])
        ones = k.sb("edge_ones", [EP, EC])
        tot = k.sb("edge_tot", [128, 4, NB + 1])
        toti = k.sb("edge_toti", [128, NB], I32)
        ldst = k.sb("edge_ldst", [EP, EC])
        blk = k.sb("edge_blk", [EP, EC])
        pos = k.sb("edge_pos", [EP, EC])
        posi = k.sb("edge_posi", [EP, 2, EC], I32)
        lane = k.sb("edge_lane", [EP, 2, EC])
        field = k.sb("edge_field", [EP, 2, EC])
        hot = [k.sb(f"edge_hot{s}", [EP, LANES]) for s in range(3)]
        put = [k.sb(f"edge_put{s}", [EP, 2, ET]) for s in range(3)]
        keyi = k.sb("edge_keyi", [LANES, 4, ET], I32)
        tb = k.sb("edge_tb", [1, ET + AHEAD])
        dhot = [k.sb(f"edge_dhot{s}", [LANES, NP], BF16) for s in range(2)]
        shot = [k.sb(f"edge_shot{s}", [LANES, NODES], BF16) for s in range(2)]
        iota = k.const[:, C_IOTA:C_IOTA + NC]

        loaded = k.sem("edges_loaded")
        step = k.sem("edges_step")
        rows = k.sem("edge_row_totals")
        prefix = k.sem("edge_prefix")
        put_ready = [k.sem(f"edge_put_ready{s}") for s in range(3)]
        put_used = [k.sem(f"edge_put_used{s}") for s in range(3)]
        sorted_ = k.sem("edges_sorted")
        unpacked = k.sem("edges_unpacked")
        hot_ready = [k.sem(f"edge_hot_ready{s}") for s in range(2)]
        hot_used = [k.sem(f"edge_hot_used{s}") for s in range(2)]
        counted = k.sem("edges_counted")
        c_ready = k.sem("c_ready")
        turned = k.sem("c_turned")
        ct_half = k.sem("ct_half_copied")
        with nc.Block() as block:

            @block.sync
            def _(sp):
                sp.dma_start(k.const[:, :], k.ins["const"]).then_inc(loaded, 16)
                sp.dma_start(ints[:, 0, :], k.ins["dst"]).then_inc(loaded, 16)
                sp.dma_start(ints[:, 1, :], k.ins["src"]).then_inc(loaded, 16)
                sp.dma_start(ints[:, 2, :], k.ins["edge_type_8"]).then_inc(loaded, 16)
                sp.dma_start(field[:, 1, :], k.ins["edge_weight1"]).then_inc(loaded, 16)
                sp.dma_start(k.x[:, :, :], k.ins["x"]).then_inc(loaded, 16)
                sp.dma_start(k.col[:, :], k.ins["cols"]).then_inc(loaded, 16)
                for i in range(3):
                    for n, m in enumerate(("Wq", "Wk", "Ws", "Wv")):
                        sp.dma_start(k.wconv[:, i, :, n * D:(n + 1) * D],
                                     k.ins[f"L0_gnn_{m}"][i].rearrange("(a p) n -> p a n", p=128)
                                     ).then_inc(k.wconv_loaded, 16)

            @block.vector
            def _(dve):
                c = Chain(dve, step)
                v = nc.vector
                c(v.memset(ones[:, :], 1.0))
                c(v.memset(tot[:, :, :], 0.0))
                c(v.memset(k.ones[:, :], 1.0))
                c(v.memset(k.zeros[:, :], 0.0))
                c(v.memset(k.C[:, :, NODES:NC], 0.0))
                c(v.memset(k.CT[:, :, NODES:NC], 0.0))
                c(v.memset(k.xT[:, :, NODES:NC], 0.0))
                c(v.memset(k.oT_padded[:, :, :], 0.0))
                c(v.memset(k.qT[:, :, NC:NODES + NP], 0.0))
                dve.wait_ge(loaded, 16 * 7)
                c(v.tensor_copy(flt[:, :, :], ints[:, :, :]))
                for b in range(NB + 1):
                    c(v.tensor_scalar(ge[:, b, :], flt[:, 0, :], float(b * NP), None, ALU.is_ge))
                c(v.tensor_tensor(member[:, :, :], ge[:, 0:NB, :], ge[:, 1:NB + 1, :], ALU.subtract))
                for b in range(NB):
                    c(v.tensor_tensor_scan(count[:, b, :], ones[:, :], member[:, b, :], 0.0, ALU.mult, ALU.add))
                v.tensor_copy(tot[0:EP, 0, 0:NB], count[:, :, EC - 1]).then_inc(rows, 1)
                c(v.tensor_tensor(blk[:, :], ge[:, 1, :], ge[:, 2, :], ALU.add))
                c(v.tensor_tensor(blk[:, :], blk[:, :], ge[:, 3, :], ALU.add))
                c(v.tensor_tensor(blk[:, :], blk[:, :], ge[:, 4, :], ALU.add))
                c(v.scalar_tensor_tensor(ldst[:, :], blk[:, :], float(-NP), flt[:, 0, :], ALU.mult, ALU.add))
                c(v.scalar_tensor_tensor(field[:, 0, :], flt[:, 1, :], 8.0, flt[:, 2, :], ALU.mult, ALU.add))
                c(v.scalar_tensor_tensor(field[:, 0, :], field[:, 0, :], 128.0, ldst[:, :], ALU.mult, ALU.add))
                c(v.tensor_scalar(field[:, 0, :], field[:, 0, :], 1.0, None, ALU.add))
                dve.wait_ge(prefix, 1)
                c(v.tensor_scalar(tot[:, 1, 0:NB], P[:, 1, 0:NB], float(LANES - 1), None, ALU.add))
                c(v.tensor_copy(toti[:, :], tot[:, 1, 0:NB]))
                c(v.tensor_scalar(toti[:, :], toti[:, :], 7, None, ALU.logical_shift_right))
                c(v.tensor_copy(tot[:, 1, 0:NB], toti[:, :]))
                c(v.tensor_tensor_scan(tot[:, 2, 1:NB + 1], k.ones[:, 0:NB], tot[:, 1, 0:NB], 0.0, ALU.mult, ALU.add))
                c(v.scalar_tensor_tensor(tot[0:EP, 3, 0:NB], tot[0:EP, 2, 0:NB], float(LANES), P[0:EP, 0, 0:NB],
                                         ALU.mult, ALU.add))
                c(v.tensor_scalar(tot[0:EP, 3, 0:NB], tot[0:EP, 3, 0:NB], -1.0, None, ALU.add))
                for b in range(NB):
                    c(v.scalar_tensor_tensor(count[:, b, :], count[:, b, :], tot[0:EP, 3, b:b + 1], member[:, b, :],
                                             ALU.add, ALU.mult))
                c(v.tensor_tensor(pos[:, :], count[:, 0, :], count[:, 1, :], ALU.add))
                for b in range(2, NB):
                    c(v.tensor_tensor(pos[:, :], pos[:, :], count[:, b, :], ALU.add))
                c(v.tensor_copy(posi[:, 0, :], pos[:, :]))
                c(v.tensor_scalar(posi[:, 1, :], posi[:, 0, :], 7, None, ALU.logical_shift_right))
                c(v.tensor_scalar(posi[:, 0, :], posi[:, 0, :], LANES - 1, None, ALU.bitwise_and))
                c(v.tensor_copy(lane[:, :, :], posi[:, :, :]))
                with dve.Fori(0, EC // 3) as i:
                    for s in range(3):
                        col = i * 3 + s
                        dve.wait_ge(put_used[s], i + 1)
                        v.tensor_scalar(hot[s][:, :], iota[0:EP, 0:LANES], lane[:, 0, bass.ds(col, 1)], None,
                                        ALU.is_equal)
                        v.tensor_scalar(put[s][:, 0, :], iota[0:EP, 0:ET], lane[:, 1, bass.ds(col, 1)],
                                        field[:, 0, bass.ds(col, 1)], ALU.is_equal, ALU.mult)
                        v.tensor_scalar(put[s][:, 1, :], iota[0:EP, 0:ET], lane[:, 1, bass.ds(col, 1)],
                                        field[:, 1, bass.ds(col, 1)], ALU.is_equal,
                                        ALU.mult).then_inc(put_ready[s], 1)
                dve.wait_ge(sorted_, 1)
                c(v.tensor_copy(keyi[:, 0, :], P[:, 0, 0:ET]))
                c(v.tensor_copy(k.e_w[:, :], P[:, 0, ET:2 * ET]))
                c(v.tensor_scalar(keyi[:, 1, :], keyi[:, 0, :], LANES - 1, None, ALU.bitwise_and))
                c(v.tensor_scalar(keyi[:, 2, :], keyi[:, 0, :], 7, None, ALU.logical_shift_right))
                c(v.tensor_scalar(keyi[:, 3, :], keyi[:, 0, :], 10, None, ALU.logical_shift_right))
                c(v.memset(k.e_ldst[:, ET:ET + AHEAD], 0.0))
                c(v.tensor_copy(k.e_ldst[:, 0:ET], keyi[:, 1, :]))
                c(v.tensor_scalar(k.e_ldst[:, :], k.e_ldst[:, :], -1.0, None, ALU.add))
                c(v.tensor_copy(k.e_row[:, :], keyi[:, 2, :]))
                c(v.tensor_copy(k.e_srci[:, :], keyi[:, 3, :]))
                c(v.tensor_copy(k.e_src[:, :], keyi[:, 3, :]))
                c(v.tensor_scalar(tb[:, :], iota[0:1, 0:ET + AHEAD], tot[0:1, 2, 1:2], None, ALU.is_ge))
                for b in range(2, NB):
                    c(v.scalar_tensor_tensor(tb[:, :], iota[0:1, 0:ET + AHEAD], tot[0:1, 2, b:b + 1], tb[:, :],
                                             ALU.is_ge, ALU.add))
                c(v.tensor_copy(k.e_blk[:, :], tb[:, :]))
                v.tensor_scalar(tb[:, :], tb[:, :], 0.0, None, ALU.add).then_inc(unpacked, 1)
                with dve.Fori(0, ET // 2) as i:
                    for s in range(2):
                        t = i * 2 + s
                        dve.wait_ge(hot_used[s], i + 1)
                        v.tensor_scalar(dhot[s][:, :], iota[:, 0:NP], k.e_ldst[:, bass.ds(t, 1)], None, ALU.is_equal)
                        v.tensor_scalar(shot[s][:, :], iota[:, 0:NODES], k.e_src[:, bass.ds(t, 1)], None,
                                        ALU.is_equal).then_inc(hot_ready[s], 1)
                dve.wait_ge(counted, 1)
                for b in range(NB):
                    c(v.tensor_copy(k.C[:, b, 0:4 * NP], P[0:NP, b, 0:4 * NP]))
                c(v.tensor_copy(k.C[:, 0:4, 4 * NP:NODES],
                                P[0:NP, 5, :].rearrange("p (b n) -> p b n", b=4)[:, :, 0:NP]))
                v.tensor_copy(k.C[:, 4, 4 * NP:NODES], P[0:NP, 6, 0:NP]).then_inc(c_ready, 1)
                dve.wait_ge(c_ready, 1)
                c(v.tensor_reduce(k.deg[:, :], k.C[:, :, 0:NODES], AX.X, ALU.add))
                c(v.memset(k.negC[:, NB, :], 0.0))
                c(v.tensor_scalar(k.negC[:, 0:NB, :], k.C[:, :, :], 0.0, NEG, ALU.is_equal, ALU.mult))
                c(v.tensor_copy(k.ident16[:, :], k.const[:, C_ID:C_ID + 128]))
                for j in range(NB):
                    dve.wait_ge(turned, j + 1)
                    q = j % 4
                    v.tensor_copy(k.CT[:, j, 0:4 * NP], P[0:NP, 2 * q, 0:4 * NP])
                    v.tensor_copy(k.CT[:, j, 4 * NP:NODES], P[0:NP, 2 * q + 1, 0:NP]).then_inc(ct_half, 1)

            @block.tensor
            def _(pe):
                t = nc.tensor
                open_slots(pe, *put_used, *hot_used)
                pe.wait_ge(rows, 1)
                t.matmul(P[0:EP, 0, 0:NB], k.const[0:EP, C_TRI:C_TRI + EP], tot[0:EP, 0, 0:NB], start=True, stop=True)
                t.matmul(P[:, 1, 0:NB], k.ones[0:EP, 0:128], tot[0:EP, 0, 0:NB], start=True,
                         stop=True).then_inc(prefix, 1)
                pe.wait_ge(put_ready[0], 1)
                t.matmul(P[:, 0, 0:2 * ET], k.zeros[0:1, 0:128], k.zeros[0:1, 0:2 * ET], start=True, stop=False)
                with pe.Fori(0, EC // 3) as i:
                    for s in range(3):
                        pe.wait_ge(put_ready[s], i + 1)
                        t.matmul(P[:, 0, 0:2 * ET], hot[s][:, :], put[s][:, :, :], start=False, stop=False,
                                 skip_group_check=True).then_inc(put_used[s], 1)
                t.matmul(P[:, 0, 0:2 * ET], k.zeros[0:1, 0:128], k.zeros[0:1, 0:2 * ET], start=False,
                         stop=True).then_inc(sorted_, 1)
                pe.wait_ge(unpacked, 1)
                for b in range(7):
                    t.matmul(P[0:NP, b, :], k.zeros[0:1, 0:NP], k.zeros[0:1, 0:512], start=True, stop=False)
                with pe.Fori(0, ET // 2) as i:
                    for s in range(2):
                        b = pe.value_load(k.e_blk[0:1, bass.ds(i * 2 + s, 1)], min_val=0, max_val=NB - 1)
                        pe.wait_ge(hot_ready[s], i + 1)
                        t.matmul(k.psum_flat[0:NP, bass.ds(b * 512, 4 * NP)], dhot[s][:, :], shot[s][:, 0:4 * NP],
                                 start=False, stop=False, skip_group_check=True)
                        t.matmul(k.psum_flat[0:NP, bass.ds(b * 128 + 5 * 512, NP)], dhot[s][:, :],
                                 shot[s][:, 4 * NP:NODES], start=False, stop=False,
                                 skip_group_check=True).then_inc(hot_used[s], 1)
                for b in range(7):
                    m = t.matmul(P[0:NP, b, :], k.zeros[0:1, 0:NP], k.zeros[0:1, 0:512], start=False, stop=True)
                m.then_inc(counted, 1)
                pe.wait_ge(c_ready, 1)
                for j in range(NB):
                    q = j % 4
                    if j >= 4:
                        pe.wait_ge(ct_half, j - 3)
                    for b in range(NB):
                        m = t.transpose(P[0:NP, 2 * q + b // 4, (b % 4) * NP:(b % 4 + 1) * NP],
                                        k.C[:, b, j * NP:(j + 1) * NP], k.const[0:NP, C_ID:C_ID + NP])
                    m.then_inc(turned, 1)
    k.stack = k.all




def turn(k, pe, src, bank):
    for m in range(KD):
        for b in range(NB):
            last = k.nc.tensor.transpose(k.psum[:, bank + 2 * m + b // 4, (b % 4) * NP:(b % 4 + 1) * NP],
                                         src[:, b, m * 128:(m + 1) * 128], k.const[0:NP, C_ID:C_ID + NP])
    return last


def normalize(k, name, x, xn, xT, rms=False, weight=None, pre=None):
    nc, P = k.nc, k.psum
    with ExitStack() as st:
        k.stack = st
        stats = k.sb(f"{name}_stats", [NP, NB, 6])
        mv = k.sb(f"{name}_mv", [NP, NB, 2])
        rs = k.sb(f"{name}_rs", [NP, 2, NB])
        sq = k.sb(f"{name}_sq", [NP, D])
        step, spread, root, normed, turned = (k.sem(f"{name}_{s}") for s in (
            "step", "var_ready", "root_ready", "normed", "turned"))
        eps = 1e-6 if rms else LN_EPS
        with nc.Block() as block:

            @block.vector
            def _(dve):
                c, v = Chain(dve, step), nc.vector
                if pre is not None:
                    pre(dve, c)
                for b in range(NB):
                    if rms:
                        c(v.tensor_tensor_reduce(out=sq[:, :], in0=x[:, b, :], in1=x[:, b, :], scale=1.0, scalar=0.0,
                                                 op0=ALU.mult, op1=ALU.add, accum_out=mv[:, b, 1:2]))
                    else:
                        c(v.bn_stats(stats[:, b, :], x[:, b, :]))
                        c(v.bn_aggr(mv[:, b, :], stats[:, b, :]))
                v.tensor_scalar(rs[:, 0, :], mv[:, :, 1], 1.0 / D if rms else 1.0, eps, ALU.mult,
                                ALU.add).then_inc(spread, 1)
                dve.wait_ge(root, 1)
                c(v.reciprocal(rs[:, 0, :], rs[:, 1, :]))
                for b in range(NB):
                    if rms:
                        v.tensor_scalar(xn[:, b, :], x[:, b, :], rs[:, 0, b:b + 1], None,
                                        ALU.mult).then_inc(normed, 1)
                    else:
                        v.tensor_scalar(xn[:, b, :], x[:, b, :], mv[:, b, 0:1], rs[:, 0, b:b + 1], ALU.subtract,
                                        ALU.mult).then_inc(normed, 1)

            @block.tensor
            def _(pe):
                pe.wait_ge(normed, NB)
                turn(k, pe, xn, 0).then_inc(turned, 1)

            @block.scalar
            def _(act):
                a = nc.scalar
                act.wait_ge(spread, 1)
                a.activation(rs[:, 1, :], rs[:, 0, :], ACT.Sqrt).then_inc(root, 1)
                act.wait_ge(turned, 1)
                for m in range(KD):
                    scale = 1.0 if weight is None else weight[:, m:m + 1]
                    a.activation(xT[:, m, 0:4 * NP], P[:, 2 * m, 0:4 * NP], ACT.Copy, scale=scale)
                    a.activation(xT[:, m, 4 * NP:NODES], P[:, 2 * m + 1, 0:NP], ACT.Copy, scale=scale)
    k.stack = k.all


def attention(k, name, qT, kT, v, vcols, oT, neg, times):
    nc, P = k.nc, k.psum
    H, HD = 4, 64
    SC = HD ** -0.5
    with ExitStack() as st:
        k.stack = st
        qs = k.sb(f"{name}_q_block", [128, 2, KD, NP])
        top = k.sb(f"{name}_top", [NP, 2, 2])
        e = [k.sb(f"{name}_exp{s}", [NP, NC]) for s in range(2)]
        w = [k.sb(f"{name}_weights{s}", [NP, NC]) for s in range(2)]
        wT = [k.sb(f"{name}_weightsT{s}", [NP, NB, NP]) for s in range(2)]
        den = k.sb(f"{name}_den", [NP, 2, 3])
        wT_cleared = k.sem(f"{name}_wT_cleared")
        q_cleared, q_copied, top_ready, exped, weighed, divided, turned, wT_ready, step = (
            k.sem(f"{name}_{s}") for s in ("q_cleared", "q_copied", "top_ready", "exped", "weighed", "divided", "turned",
                                           "wT_ready", "attn_step"))
        scored, mixed, taken = ([k.sem(f"{name}_{n}{s}") for s in range(2)] for n in ("scored", "mixed", "taken"))
        with nc.Block() as block:

            @block.gpsimd
            def _(pool):
                nc.gpsimd.memset(qs[:, :, :, :], 0.0).then_inc(q_cleared, 1)
                pool.wait_ge(q_cleared, 1)
                for a in range(2):
                    nc.gpsimd.tensor_copy(qs[a * HD:(a + 1) * HD, a], qT[a * HD:(a + 1) * HD, :, 0:NP]
                                          ).then_inc(q_copied, 1)
                with pool.Fori(0, NB) as d:
                    pool.wait_ge(scored[1], d * 2 + 2)
                    for a in range(2):
                        nc.gpsimd.tensor_copy(qs[a * HD:(a + 1) * HD, a],
                                              qT[a * HD:(a + 1) * HD, :, bass.ds(d * NP + NP, NP)]
                                              ).then_inc(q_copied, 1)

            @block.tensor
            def _(pe):
                t = nc.tensor

                def score(d, h):
                    s = h % 2
                    for half in range(2):
                        t.matmul(P[0:NP, 2 * s + half, 0:HC], qs[:, s, h // 2, :],
                                 kT[:, h // 2, half * HC:(half + 1) * HC], start=True, stop=False)
                        m = t.matmul(P[0:NP, 2 * s + half, 0:HC], k.ident16[0:NP, 0:NP],
                                     neg[:, d, half * HC:(half + 1) * HC], start=False, stop=True)
                    m.then_inc(scored[s], 1)

                def mix(h):
                    s = h % 2
                    for j in range(NB):
                        m = t.matmul(P[s * HD:(s + 1) * HD, 6 + s, 0:NP], v[:, j, vcols[h]:vcols[h] + HD],
                                     wT[s][:, j, :], start=(j == 0), stop=(j == NB - 1))
                    m.then_inc(mixed[s], 1)

                open_slots(pe, mixed[0])
                pe.wait_ge(q_copied, 2)
                score(0, 0)
                score(0, 1)
                pe.wait_ge(wT_cleared, 1)
                with pe.Fori(0, NB) as d:
                    for h in range(H):
                        pe.wait_ge(exped, d * H + h + 1)
                        if h == 2:
                            pe.wait_ge(q_copied, d * 2 + 4)
                        score(d + (h + 2) // H, (h + 2) % H)
                        pe.wait_ge(divided, d * H + h + 1)
                        pe.wait_ge(wT_ready, d * H + h + 1)
                        for j in range(NB):
                            m = t.transpose(P[0:NP, 4 + j // 4, (j % 4) * NP:(j % 4 + 1) * NP],
                                            w[h % 2][:, j * NP:(j + 1) * NP], k.const[0:NP, C_ID:C_ID + NP])
                        m.then_inc(turned, 1)
                        pe.wait_ge(taken[(h + 1) % 2], d * 2 + h // 2 + 1)
                        mix((h + 3) % H)
                pe.wait_ge(wT_ready, NB * H + 1)
                pe.wait_ge(taken[1], 2 * NB + 1)
                mix(3)

            @block.scalar
            def _(act):
                a = nc.scalar

                def exps(u, s):
                    act.wait_ge(top_ready, u + 1)
                    a.activation(e[s][:, :].rearrange("p (a n) -> p a n", a=2), P[0:NP, 2 * s:2 * s + 2, 0:HC],
                                 ACT.Exp, bias=top[:, s, 1:2], scale=SC).then_inc(exped, 1)

                open_slots(act, wT_ready)
                exps(0, 0)
                with act.Fori(0, NB) as d:
                    for h in range(H):
                        exps(d * H + h + 1, (h + 1) % 2)
                        act.wait_ge(turned, d * H + h + 1)
                        act.wait_ge(mixed[h % 2], d * 2 + h // 2 + 1)
                        a.activation(wT[h % 2][:, 0:4, :], P[0:NP, 4, 0:4 * NP].rearrange("p (j n) -> p j n", j=4),
                                     ACT.Copy)
                        a.activation(wT[h % 2][:, 4, :], P[0:NP, 5, 0:NP], ACT.Copy).then_inc(wT_ready, 1)

            @block.vector
            def _(dve):
                vec = nc.vector

                def find_top(j, s, n):
                    dve.wait_ge(scored[s], j + 1)
                    vec.tensor_reduce(top[:, s, 0:1], P[0:NP, 2 * s:2 * s + 2, 0:HC], AX.XY,
                                      ALU.max).then_inc(step, 1)
                    dve.wait_ge(step, n + 1)
                    vec.tensor_scalar(top[:, s, 1:2], top[:, s, 0:1], -SC, None, ALU.mult).then_inc(top_ready, 1)

                def add(block_, h, n):
                    s = h % 2
                    dve.wait_ge(mixed[s], n)
                    at = bass.ds(block_ * NP, NP) if not isinstance(block_, int) else \
                        slice(block_ * NP, block_ * NP + NP)
                    to = oT[s * HD:(s + 1) * HD, h // 2, at]
                    vec.tensor_tensor(to, P[s * HD:(s + 1) * HD, 6 + s, 0:NP], to, ALU.add).then_inc(taken[s], 1)

                vec.memset(wT[1][:, :, :], 0.0).then_inc(wT_cleared, 1)
                open_slots(dve, *taken)
                find_top(0, 0, 0)
                steps = 3
                with dve.Fori(0, NB) as d:
                    for h in range(H):
                        s = h % 2
                        n = d * (H * steps) + (h * steps + 1)
                        dve.wait_ge(exped, d * H + h + 1)
                        vec.scalar_tensor_tensor(w[s][:, :], e[s][:, :], 1.0, times[:, d, :], ALU.mult, ALU.mult,
                                                 accum_out=den[:, s, 0:1]).then_inc(weighed, 1)
                        dve.wait_ge(weighed, d * H + h + 1)
                        vec.tensor_scalar(den[:, s, 1:2], den[:, s, 0:1], 1e-30, None, ALU.max).then_inc(step, 1)
                        dve.wait_ge(step, n + 1)
                        vec.reciprocal(den[:, s, 2:3], den[:, s, 1:2]).then_inc(step, 1)
                        dve.wait_ge(step, n + 2)
                        vec.tensor_scalar(w[s][:, :], w[s][:, :], den[:, s, 2:3], None,
                                          ALU.mult).then_inc(divided, 1)
                        find_top(d * 2 + (h + 1) // 2, 1 - s, n + 2)
                        if h == 0:
                            add(d, 3, d * 2 + 1)
                        else:
                            add(d + 1, h - 1, d * 2 + (h - 1) // 2 + 2)
                add(NB, 3, 2 * NB + 1)
    k.stack = k.all


def conv_project(k, i):
    nc, P = k.nc, k.psum
    name = f"conv{i}"
    loaded, product, copied, values = (k.sem(f"{name}_{s}") for s in ("bias_loaded", "product", "copied", "values"))
    w = k.wconv[:, i, :, :]
    with nc.Block() as block:

        @block.tensor
        def _(pe):
            t = nc.tensor
            pe.wait_ge(k.wconv_loaded, 16 * 12)
            pe.wait_ge(loaded, 16)
            for g in range(6):
                if g >= 4:
                    pe.wait_ge(copied, g - 3)
                for half in range(2):
                    for kk in range(KD):
                        m = t.matmul(P[:, 2 * (g % 4) + half, 0:HC], w[:, kk, g * 128:(g + 1) * 128],
                                     k.xT[:, kk, half * HC:(half + 1) * HC], start=(kk == 0), stop=(kk == KD - 1))
                m.then_inc(product, 1)
            for b in range(NB):
                pe.wait_ge(copied, 4 if b < 4 else 5)
                bank = (4 + b) % 8
                for kk in range(KD):
                    t.matmul(P[0:NP, bank, 0:D], k.xT[:, kk, b * NP:(b + 1) * NP], w[:, kk, 3 * D:4 * D],
                             start=(kk == 0), stop=False)
                t.matmul(P[0:NP, bank, 0:D], k.ones[0:1, 0:NP], k.brow[0:1, 0:D], start=False,
                         stop=True).then_inc(values, 1)

        @block.sync
        def _(sp):
            sp.dma_start(k.brow[0:1, 0:D], k.ins["L0_gnn_bv"][i:i + 1]).then_inc(loaded, 16)

        @block.scalar
        def _(act):
            for g in range(6):
                act.wait_ge(product, g + 1)
                to = (k.qT, k.kT, k.oT)[g // KD][:, g % KD, 0:NC]
                nc.scalar.activation(to.rearrange("p (a n) -> p a n", a=2), P[:, 2 * (g % 4):2 * (g % 4) + 2, 0:HC],
                                     ACT.Identity, bias=col(k, "conv_bias", 6 * i + g)).then_inc(copied, 1)

        @block.vector
        def _(dve):
            for b in range(NB):
                dve.wait_ge(values, b + 1)
                nc.vector.tensor_copy(k.v[:, b, :], P[0:NP, (4 + b) % 8, 0:D])


def batch_norm(k, i):
    nc, P = k.nc, k.psum
    name = f"bn{i}"
    with ExitStack() as st:
        k.stack = st
        stats = k.sb(f"{name}_stats", [128, KD, 2, 6])
        mv = k.sb(f"{name}_mv", [128, KD, 2])
        f = k.sb(f"{name}_f", [128, 4, KD])
        spread, root, step, ready = (k.sem(f"{name}_{s}") for s in (
            "var_ready", "root_ready", "step", "affine_ready"))
        with nc.Block() as block:

            @block.vector
            def _(dve):
                c, v = Chain(dve, step), nc.vector
                for m in range(KD):
                    v.bn_stats(stats[:, m, 0, :], k.oT[:, m, 0:HC])
                    c(v.bn_stats(stats[:, m, 1, :], k.oT[:, m, HC:NODES]))
                    c(v.bn_aggr(mv[:, m, :], stats[:, m, :, :]))
                v.tensor_scalar(f[:, 0, :], mv[:, :, 1], LN_EPS, None, ALU.add).then_inc(spread, 1)
                dve.wait_ge(root, 1)
                c(v.reciprocal(f[:, 2, :], f[:, 1, :]))
                c(v.tensor_tensor(f[:, 2, :], f[:, 2, :], col(k, "bn_gamma", KD * i, KD), ALU.mult))
                c(v.tensor_tensor(f[:, 3, :], f[:, 2, :], mv[:, :, 0], ALU.mult))
                v.tensor_tensor(f[:, 3, :], col(k, "bn_beta", KD * i, KD), f[:, 3, :], ALU.subtract).then_inc(ready, 1)

            @block.scalar
            def _(act):
                a = nc.scalar
                act.wait_ge(spread, 1)
                a.activation(f[:, 1, :], f[:, 0, :], ACT.Sqrt).then_inc(root, 1)
                act.wait_ge(ready, 1)
                for m in range(KD):
                    a.activation(k.xT[:, m, 0:NODES], k.oT[:, m, 0:NODES], ACT.Relu, bias=f[:, 3, m:m + 1],
                                 scale=f[:, 2, m:m + 1])
    k.stack = k.all


def conv_layers(k):
    normalize(k, "ln_conv", k.x, k.xn, k.xT)
    for i in range(3):
        conv_project(k, i)
        attention(k, f"conv{i}", k.qT, k.kT, k.v, [0, 64, 128, 192], k.oT_padded, k.negC, k.C)
        if i < 2:
            batch_norm(k, i)
    turned = k.sem("conv_out_turned")
    with k.nc.Block() as block:

        @block.tensor
        def _(pe):
            for b in range(NB):
                for m in range(KD):
                    ins = k.nc.tensor.transpose(k.psum[0:NP, b, m * 128:(m + 1) * 128],
                                                k.oT[:, m, b * NP:(b + 1) * NP], k.const[:, C_ID:C_ID + 128])
                ins.then_inc(turned, 1)

        @block.vector
        def _(dve):
            for b in range(NB):
                dve.wait_ge(turned, b + 1)
                k.nc.vector.tensor_tensor(k.x[:, b, :], k.x[:, b, :], k.psum[0:NP, b, 0:D], ALU.add)


def add_to_x(k, name, what):
    done = k.sem(f"{name}_added")
    with k.nc.Block() as block:

        @block.vector
        def _(dve):
            k.nc.vector.tensor_tensor(k.x[:, :, :], k.x[:, :, :], what[:, :, :], ALU.add).then_inc(done, 1)


def softmax8(k, c, v, p, small, exp_to, exp_done, exp_wait):
    n = p.shape[1]
    wide = lambda s: s.unsqueeze(2).to_broadcast([NP, n, EXPERTS])
    c(v.tensor_reduce(small[:, 0, :], p, AX.X, ALU.max))
    v.tensor_tensor(p, p, wide(small[:, 0, :]), ALU.subtract).then_inc(exp_to, 1)
    c.eng.wait_ge(exp_done, exp_wait)
    c(v.tensor_reduce(small[:, 0, :], p, AX.X, ALU.add))
    c(v.reciprocal(small[:, 1, :], small[:, 0, :]))
    c(v.tensor_tensor(p, p, wide(small[:, 1, :]), ALU.mult))


def rank8(k, c, v, p, rank, pair, tie):
    n = p.shape[1]
    tri = k.const[0:NP, C_RANK:C_ROW].rearrange("p (e f) -> p e f", e=EXPERTS)
    for i in range(n):
        mine = p[:, i, :].unsqueeze(2).to_broadcast([NP, EXPERTS, EXPERTS])
        other = p[:, i, :].unsqueeze(1).to_broadcast([NP, EXPERTS, EXPERTS])
        c(v.tensor_tensor(tie[:, i], other, mine, ALU.is_equal))
        c(v.tensor_tensor(tie[:, i], tie[:, i], tri, ALU.mult))
        c(v.tensor_tensor(pair[:, i], other, mine, ALU.is_gt))
        c(v.tensor_tensor(pair[:, i], pair[:, i], tie[:, i], ALU.add))
    c(v.tensor_reduce(rank, pair[:, :, :, :], AX.X, ALU.add))


def route(k, name, xT, tiles, router, bias, top, floor):
    nc, P = k.nc, k.psum
    with ExitStack() as st:
        k.stack = st
        small = k.sb(f"{name}_small", [NP, 2, NB])
        rank = k.sb(f"{name}_rank", [NP, NB, EXPERTS])
        pair = k.sb(f"{name}_pair", [NP, NB, EXPERTS, EXPERTS])
        tie = k.sb(f"{name}_tie", [NP, NB, EXPERTS, EXPERTS])
        brow = k.sb(f"{name}_bias", [1, EXPERTS])
        loaded, logits, step, to_exp, exped = (k.sem(f"{name}_{s}") for s in (
            "bias_loaded", "logits", "step", "to_exp", "exped"))
        g = k.gate
        with nc.Block() as block:

            @block.sync
            def _(sp):
                if bias is not None:
                    sp.dma_start(brow[:, :], k.ins[bias].rearrange("(a n) -> a n", a=1)).then_inc(loaded, 16)

            @block.tensor
            def _(pe):
                t = nc.tensor
                if bias is not None:
                    pe.wait_ge(loaded, 16)
                for b in range(NB):
                    for kk in range(tiles):
                        m = t.matmul(P[0:NP, 0, b * EXPERTS:(b + 1) * EXPERTS], xT[:, kk, b * NP:(b + 1) * NP],
                                     col(k, router, kk * EXPERTS, EXPERTS), start=(kk == 0),
                                     stop=(kk == tiles - 1 and bias is None))
                    if bias is not None:
                        m = t.matmul(P[0:NP, 0, b * EXPERTS:(b + 1) * EXPERTS], k.ones[0:1, 0:NP], brow[:, :],
                                     start=False, stop=True)
                m.then_inc(logits, 1)

            @block.scalar
            def _(act):
                act.wait_ge(to_exp, 1)
                nc.scalar.activation(g[:, :, :], g[:, :, :], ACT.Exp).then_inc(exped, 1)

            @block.vector
            def _(dve):
                c, v = Chain(dve, step), nc.vector
                dve.wait_ge(logits, 1)
                c(v.tensor_copy(g[:, :, :], P[0:NP, 0, 0:NB * EXPERTS].rearrange("p (b e) -> p b e", b=NB)))
                softmax8(k, c, v, g[:, :, :], small, to_exp, exped, 1)
                rank8(k, c, v, g, rank[:, :, :], pair, tie)
                c(v.tensor_scalar(rank[:, :, :], rank[:, :, :], float(top), None, ALU.is_lt))
                c(v.tensor_tensor(g[:, :, :], g[:, :, :], rank[:, :, :], ALU.mult))
                if floor is not None:
                    c(v.tensor_reduce(small[:, 0, :], g[:, :, :], AX.X, ALU.add))
                    c(v.tensor_scalar(small[:, 0, :], small[:, 0, :], floor, None, ALU.add))
                    c(v.reciprocal(small[:, 1, :], small[:, 0, :]))
                    c(v.tensor_tensor(g[:, :, :], g[:, :, :],
                                      small[:, 1, :].unsqueeze(2).to_broadcast([NP, NB, EXPERTS]), ALU.mult))
    k.stack = k.all


def down(k, pe, hT, w, brow, tiles, rows, i, s, given, taken):
    P, t = k.psum, k.nc.tensor
    for b in range(NB):
        q = (NB * s + b) % 2
        pe.wait_ge(taken[q], i * NB + ((NB * s + b) // 2 + 1))
        for kk in range(tiles):
            m = t.matmul(P[0:NP, 6 + q, 0:D], hT[0:rows, kk, b * NP:(b + 1) * NP], w[0:rows, kk, :],
                         start=(kk == 0), stop=(brow is None and kk == tiles - 1))
        if brow is not None:
            m = t.matmul(P[0:NP, 6 + q, 0:D], k.ones[0:1, 0:NP], brow, start=False, stop=True)
        m.then_inc(given[q], 1)


def gather_outputs(k, dve, acc, i, s, given, taken):
    for b in range(NB):
        q = (NB * s + b) % 2
        dve.wait_ge(given[q], i * NB + (NB * s + b) // 2 + 1)
        k.nc.vector.scalar_tensor_tensor(acc[:, b, :], k.psum[0:NP, 6 + q, 0:D],
                                         k.gate[:, b, bass.ds(i * 2 + s, 1)], acc[:, b, :], ALU.mult,
                                         ALU.add).then_inc(taken[q], 1)


def experts_gelu(k, name, w1_of, w2_of, b2_of, tiles, pairs, b1, affine, acc, before=None):
    nc, P = k.nc, k.psum
    hidden = tiles * 128
    with ExitStack() as st:
        k.stack = st
        w1 = [k.sb(f"{name}_w1_{s}", [128, KD, hidden]) for s in range(2)]
        w2 = [k.sb(f"{name}_w2_{s}", [128, tiles, D]) for s in range(2)]
        b2 = [k.sb(f"{name}_b2_{s}", [1, D]) for s in range(2)]
        xe = [k.sb(f"{name}_x_{s}", [128, KD, NC]) if affine else k.xT for s in range(2)]
        hT = k.sb(f"{name}_hT", [128, tiles, NC])
        two = lambda n: [k.sem(f"{name}_{n}{s}") for s in range(2)]
        w1_loaded, w2_loaded, w1_used, w2_used, x_ready, up_given, up_taken, given, taken = (two(n) for n in (
            "w1_loaded", "w2_loaded", "w1_used", "w2_used", "x_ready", "up_given", "up_taken", "down_given",
            "down_taken"))
        cleared = k.sem(f"{name}_cleared")
        half = tiles // 2
        with nc.Block() as block:

            @block.sync
            def _(sp):
                if before is not None:
                    before(sp)
                with sp.Fori(0, pairs) as i:
                    for s in range(2):
                        e = i * 2 + s
                        sp.wait_ge(w1_used[s], i + 1)
                        sp.dma_start(w1[s][:, :, :], w1_of(sp, e)).then_inc(w1_loaded[s], 16)
                        sp.wait_ge(w2_used[s], i + 1)
                        sp.dma_start(w2[s][:, :, :], w2_of(sp, e)).then_inc(w2_loaded[s], 16)
                        sp.dma_start(b2[s][:, :], b2_of(sp, e)).then_inc(w2_loaded[s], 16)

            @block.tensor
            def _(pe):
                t = nc.tensor
                open_slots(pe, *w1_used, *w2_used)
                with pe.Fori(0, pairs) as i:
                    for s in range(2):
                        pe.wait_ge(w1_loaded[s], i * 16 + 16)
                        if affine:
                            pe.wait_ge(x_ready[s], i + 1)
                        for m in range(tiles):
                            q = m % 2
                            pe.wait_ge(up_taken[q], (i * 2 + s) * half + (m // 2 + 1))
                            for a in range(2):
                                for kk in range(KD):
                                    ins = t.matmul(P[:, 2 * q + a, 0:HC], w1[s][:, kk, m * 128:(m + 1) * 128],
                                                   xe[s][:, kk, a * HC:(a + 1) * HC], start=(kk == 0),
                                                   stop=(kk == KD - 1))
                            ins.then_inc(up_given[q], 1)
                        t.matmul(P[:, 5, 0:1], k.zeros[0:1, 0:128], k.zeros[0:1, 0:1], start=True,
                                 stop=True).then_inc(w1_used[s], 1)
                        for q in range(2):
                            pe.wait_ge(up_taken[q], (i * 2 + s + 1) * half + 1)
                        pe.wait_ge(w2_loaded[s], i * 32 + 32)
                        down(k, pe, hT, w2[s], b2[s][:, :], tiles, 128, i, s, given, taken)
                        t.matmul(P[:, 5, 0:1], k.zeros[0:1, 0:128], k.zeros[0:1, 0:1], start=True,
                                 stop=True).then_inc(w2_used[s], 1)

            @block.scalar
            def _(act):
                open_slots(act, *up_taken)
                with act.Fori(0, pairs) as i:
                    for s in range(2):
                        for m in range(tiles):
                            act.wait_ge(up_given[m % 2], (i * 2 + s) * half + m // 2 + 1)
                            nc.scalar.activation(hT[:, m, :].rearrange("p (a n) -> p a n", a=2),
                                                 P[:, 2 * (m % 2):2 * (m % 2) + 2, 0:HC], ACT.Gelu,
                                                 bias=b1(i * 2 + s, m)).then_inc(up_taken[m % 2], 1)

            @block.vector
            def _(dve):
                v = nc.vector

                def make_x(e, s):
                    for kk in range(KD):
                        ins = v.tensor_scalar(xe[s][:, kk, :], k.xT[:, kk, :],
                                              col(k, affine[0], e + kk * (EXPERTS + 1)),
                                              col(k, affine[1], e + kk * (EXPERTS + 1)), ALU.mult, ALU.add)
                    ins.then_inc(x_ready[s], 1)

                open_slots(dve, *taken)
                v.memset(acc[:, :, :], 0.0).then_inc(cleared, 1)
                dve.wait_ge(cleared, 1)
                if affine:
                    make_x(0, 0)
                with dve.Fori(0, pairs) as i:
                    for s in range(2):
                        if affine:
                            dve.wait_ge(w1_used[1 - s], i + (s + 1))
                            make_x(i * 2 + s + 1, 1 - s)
                        gather_outputs(k, dve, acc, i, s, given, taken)
    k.stack = k.all


def moe0(k):
    normalize(k, "ln_moe0", k.x, k.xn, k.xT)
    route(k, "moe0_route", k.xT, KD, "moe0_router", "L0_ffn_br", 2, 0.0)
    normalize(k, "ln_moe0_inner", k.xn, k.xn, k.xT)
    experts_gelu(k, "moe0",
                 lambda sp, e: k.ins["L0_ffn_W1"][bass.ds(e, 1)].rearrange("o (a p) n -> p (o a) n", p=128),
                 lambda sp, e: k.ins["L0_ffn_W2"][bass.ds(e, 1)].rearrange("o (a p) n -> p (o a) n", p=128),
                 lambda sp, e: k.ins["L0_ffn_b2"][bass.ds(e, 1), :],
                 8, EXPERTS // 2, lambda e, m: col(k, "moe0_b1", e * 8 + m), ("moe0_ln_g", "moe0_ln_b"), k.o)
    add_to_x(k, "moe0", k.o)


def sage(k):
    nc, P = k.nc, k.psum
    normalize(k, "ln_sage", k.x, k.xn, k.xT)
    with ExitStack() as st:
        k.stack = st
        w = k.sb("sage_w", [128, 2, KD, D])
        brow = k.sb("sage_b", [1, D])
        aggT = k.sb("sage_aggT", [128, KD, NC])
        rdeg = k.sb("sage_rdeg", [NP, 2, NB])
        z = k.sb("sage_z", [NP, NB, D])
        loaded, agg, agg_ready, own, neigh, step = (k.sem(f"sage_{s}") for s in (
            "loaded", "agg", "agg_copied", "own_products", "neighbour_products", "step"))
        with nc.Block() as block:

            @block.sync
            def _(sp):
                for n, m in enumerate(("W_self", "W_neigh")):
                    sp.dma_start(w[:, n], k.ins[f"L1_gnn_{m}"].rearrange("(a p) n -> p a n", p=128)
                                 ).then_inc(loaded, 16)
                sp.dma_start(brow[:, :], k.ins["L1_gnn_b"].rearrange("(a n) -> a n", a=1)).then_inc(loaded, 16)

            @block.tensor
            def _(pe):
                t = nc.tensor
                for m in range(KD):
                    for a in range(2):
                        for j in range(NB):
                            ins = t.matmul(P[:, 2 * m + a, 0:HC], k.xn[:, j, m * 128:(m + 1) * 128],
                                           k.CT[:, j, a * HC:(a + 1) * HC], start=(j == 0), stop=(j == NB - 1))
                    ins.then_inc(agg, 1)
                pe.wait_ge(loaded, 16 * 3)
                for b in range(NB):
                    q = b % 2
                    if b >= 2:
                        pe.wait_ge(step, b - 1)
                    for kk in range(KD):
                        t.matmul(P[0:NP, 4 + q, 0:D], k.xT[:, kk, b * NP:(b + 1) * NP], w[:, 0, kk, :],
                                 start=(kk == 0), stop=False)
                    t.matmul(P[0:NP, 4 + q, 0:D], k.ones[0:1, 0:NP], brow[:, :], start=False,
                             stop=True).then_inc(own, 1)
                    pe.wait_ge(agg_ready, KD)
                    for kk in range(KD):
                        ins = t.matmul(P[0:NP, 6 + q, 0:D], aggT[:, kk, b * NP:(b + 1) * NP], w[:, 1, kk, :],
                                       start=(kk == 0), stop=(kk == KD - 1))
                    ins.then_inc(neigh, 1)

            @block.scalar
            def _(act):
                for m in range(KD):
                    act.wait_ge(agg, m + 1)
                    nc.scalar.activation(aggT[:, m, :].rearrange("p (a n) -> p a n", a=2),
                                         P[:, 2 * m:2 * m + 2, 0:HC], ACT.Copy).then_inc(agg_ready, 1)

            @block.vector
            def _(dve):
                v = nc.vector
                c = Chain(dve, k.sem("sage_chain"))
                c(v.tensor_scalar(rdeg[:, 0, :], k.deg[:, :], 1.0, None, ALU.max))
                c(v.reciprocal(rdeg[:, 1, :], rdeg[:, 0, :]))
                for b in range(NB):
                    dve.wait_ge(neigh, b + 1)
                    dve.wait_ge(own, b + 1)
                    c(v.tensor_scalar(z[:, b, :], P[0:NP, 6 + b % 2, 0:D], rdeg[:, 1, b:b + 1], None, ALU.mult))
                    v.tensor_tensor(z[:, b, :], z[:, b, :], P[0:NP, 4 + b % 2, 0:D], ALU.add).then_inc(step, 1)
                    dve.wait_ge(step, b + 1)
                    v.scalar_tensor_tensor(k.x[:, b, :], z[:, b, :], 0.0, k.x[:, b, :], ALU.max, ALU.add)
    k.stack = k.all


def route_graph(k):
    nc, P = k.nc, k.psum
    CAPACITY = -(-NODES * 5 // (4 * EXPERTS))
    with ExitStack() as st:
        k.stack = st
        mean = k.sb("moe1_mean", [128, KD])
        means = k.sb("moe1_means", [128, KD, NP])
        p = k.sb("moe1_p", [NP, 1, EXPERTS])
        f = k.sb("moe1_f", [NP, 1, EXPERTS])
        small = k.sb("moe1_small", [NP, 2, 1])
        rank = k.sb("moe1_rank", [NP, 1, EXPERTS])
        pair = k.sb("moe1_pair", [NP, 1, EXPERTS, EXPERTS])
        tie = k.sb("moe1_tie", [NP, 1, EXPERTS, EXPERTS])
        pick = k.sb("moe1_pick", [NP, EXPERTS])
        junk = k.sb("moe1_junk", [NP, EXPERTS])
        val = k.sb("moe1_val", [NP, 6])
        brow = k.sb("moe1_brow", [1, EXPERTS])
        loaded, mean_ready, logits, step, to_exp, exped, picked, bias_loaded = (k.sem(f"moe1_{s}") for s in (
            "loaded", "mean_ready", "logits", "step", "to_exp", "exped", "picked", "picked_bias_loaded"))
        with nc.Block() as block:

            @block.sync
            def _(sp):
                sp.dma_start(brow[:, :], k.ins["L1_ffn_br"].rearrange("(a n) -> a n", a=1)).then_inc(loaded, 16)
                sp.wait_ge(picked, 1)
                for s in range(2):
                    e = sp.value_load(k.picked[0:1, s:s + 1], min_val=0, max_val=EXPERTS - 1)
                    sp.dma_start(k.picked_b1[:, s * 4:(s + 1) * 4],
                                 k.ins["moe1_b1"][bass.ds(e, 1)].rearrange("o p m -> p (o m)")
                                 ).then_inc(bias_loaded, 16)
                sp.wait_ge(bias_loaded, 32)

            @block.tensor
            def _(pe):
                t = nc.tensor
                pe.wait_ge(mean_ready, 1)
                pe.wait_ge(loaded, 16)
                for kk in range(KD):
                    t.matmul(P[0:NP, 0, 0:EXPERTS], means[:, kk, :], col(k, "moe1_router", kk * EXPERTS, EXPERTS),
                             start=(kk == 0), stop=False)
                t.matmul(P[0:NP, 0, 0:EXPERTS], k.ones[0:1, 0:NP], brow[:, :], start=False,
                         stop=True).then_inc(logits, 1)

            @block.scalar
            def _(act):
                a = nc.scalar
                for n in range(2):
                    act.wait_ge(to_exp, n + 1)
                    a.activation(p[:, 0, :], p[:, 0, :], ACT.Exp).then_inc(exped, 1)
                act.wait_ge(to_exp, 3)
                a.activation(val[:, 3:4], val[:, 2:3], ACT.Exp).then_inc(exped, 1)

            @block.vector
            def _(dve):
                c, v = Chain(dve, step), nc.vector
                c(v.tensor_reduce(mean[:, :], k.xT[:, :, 0:NODES], AX.X, ALU.add))
                c(v.tensor_scalar(mean[:, :], mean[:, :], 1.0 / NODES, None, ALU.mult))
                for kk in range(KD):
                    ins = v.tensor_scalar(means[:, kk, :], k.ones[:, 0:NP], mean[:, kk:kk + 1], None, ALU.mult)
                    c(ins)
                v.memset(junk[:, :], 0.0).then_inc(mean_ready, 1)
                dve.wait_ge(mean_ready, 1)
                dve.wait_ge(logits, 1)
                c(v.tensor_copy(p[:, 0, :], P[0:NP, 0, 0:EXPERTS]))
                softmax8(k, c, v, p[:, :, :], small, to_exp, exped, 1)
                c(v.tensor_scalar(f[:, 0, :], p[:, 0, :], float(NODES), 1e-30, ALU.mult, ALU.max))
                c(v.reciprocal(f[:, 0, :], f[:, 0, :]))
                c(v.tensor_scalar(f[:, 0, :], f[:, 0, :], float(CAPACITY), 1.0, ALU.mult, ALU.min))
                c(v.tensor_tensor(p[:, 0, :], p[:, 0, :], f[:, 0, :], ALU.mult))
                softmax8(k, c, v, p[:, :, :], small, to_exp, exped, 2)
                rank8(k, c, v, p, rank[:, :, :], pair, tie)
                for s in range(2):
                    c(v.tensor_scalar(pick[:, :], rank[:, 0, :], float(s), None, ALU.is_equal))
                    for n, what in enumerate((p[:, 0, :], k.const[0:NP, C_IOTA:C_IOTA + EXPERTS])):
                        c(v.tensor_tensor(junk[:, :], pick[:, :], what, ALU.mult))
                        c(v.tensor_reduce(val[:, s + 4 * n:s + 4 * n + 1], junk[:, :], AX.X, ALU.add))
                v.tensor_copy(k.picked[0:1, :], val[0:1, 4:6]).then_inc(picked, 1)
                v.tensor_tensor(val[:, 2:3], val[:, 1:2], val[:, 0:1], ALU.subtract).then_inc(to_exp, 1)
                dve.wait_ge(exped, 3)
                c(v.tensor_scalar(val[:, 2:3], val[:, 3:4], 1.0, None, ALU.add))
                c(v.reciprocal(val[:, 0:1], val[:, 2:3]))
                c(v.tensor_tensor(val[:, 1:2], val[:, 3:4], val[:, 0:1], ALU.mult))
                c(v.tensor_copy(k.gate[:, :, 0:2], val[:, 0:2].unsqueeze(1).to_broadcast([NP, NB, 2])))
    k.stack = k.all


def moe1(k):
    nc = k.nc
    normalize(k, "ln_moe1", k.x, k.xn, k.xT)
    route_graph(k)
    hidden = 4

    def expert(sp, e):
        return sp.value_load(k.picked[0:1, bass.ds(e, 1)], min_val=0, max_val=EXPERTS - 1)

    experts_gelu(k, "moe1",
                 lambda sp, e: k.ins["L1_ffn_W1"][bass.ds(expert(sp, e), 1)].rearrange("o (a p) n -> p (o a) n", p=128),
                 lambda sp, e: k.ins["L1_ffn_W2"][bass.ds(expert(sp, e), 1)].rearrange("o (a p) n -> p (o a) n", p=128),
                 lambda sp, e: k.ins["L1_ffn_b2"][bass.ds(expert(sp, e), 1), :],
                 hidden, 1, lambda e, m: k.picked_b1[:, bass.ds(e * hidden + m, 1)], None, k.o)

    def add_tokens(dve, c):
        c(nc.vector.tensor_tensor(k.o[:, :, :], k.o[:, :, :], k.xn[:, :, :], ALU.add))

    normalize(k, "ln_moe1_out", k.o, k.o, k.xT, pre=add_tokens)
    with ExitStack() as st:
        k.stack = st
        par = k.sb("moe1_par", [NP, 2, D])
        loaded, step = k.sem("moe1_par_loaded"), k.sem("moe1_out_step")
        with nc.Block() as block:

            @block.sync
            def _(sp):
                sp.dma_start(par[:, 0, :], k.ins["moe1_gamma"]).then_inc(loaded, 16)
                sp.dma_start(par[:, 1, :], k.ins["moe1_beta"]).then_inc(loaded, 16)

            @block.vector
            def _(dve):
                c, v = Chain(dve, step), nc.vector
                wide = lambda n: par[:, n, :].unsqueeze(1).to_broadcast([NP, NB, D])
                dve.wait_ge(loaded, 32)
                c(v.tensor_tensor(k.o[:, :, :], k.o[:, :, :], wide(0), ALU.mult))
                c(v.tensor_tensor(k.o[:, :, :], k.o[:, :, :], wide(1), ALU.add))
                c(v.tensor_tensor(k.x[:, :, :], k.x[:, :, :], k.o[:, :, :], ALU.add))
    k.stack = k.all


RELS = 8


def rgcn_layer(k, l):
    nc, P = k.nc, k.psum
    name = f"rgcn{l}"
    with ExitStack() as st:
        k.stack = st
        basis = k.sb(f"{name}_basis", [128, RELS, KD, D])
        w = k.sb(f"{name}_w", [128, KD, RELS, D])
        coeff = k.sb(f"{name}_coeff", [128, RELS * RELS])
        ah = [k.sb(f"{name}_all_h{s}", [NP, RELS * D]) for s in range(2)]
        brow = k.sb(f"{name}_bias", [1, 2 * D])
        idx = [k.sb(f"{name}_idx{s}", [LANES, 1], U32) for s in range(4)]
        rows = [k.sb(f"{name}_rows{s}", [LANES, D]) for s in range(4)]
        hot = [k.sb(f"{name}_hot{s}", [LANES, NP]) for s in range(4)]
        loaded, step, w_ready, products, copied, whole = (k.sem(f"{name}_{s}") for s in (
            "loaded", "step", "w_ready", "products", "copied", "summed"))
        idx_seen = k.sem(f"{name}_idx_seen")
        stored = [k.sem(f"{name}_stored{s}") for s in range(2)]
        four = lambda n: [k.sem(f"{name}_{n}{s}") for s in range(4)]
        idx_ready, gathered, hot_ready, used = (four(n) for n in ("idx_ready", "gathered", "hot_ready", "used"))
        table = k.tables[:, 0:RELS * D]
        with nc.Block() as block:

            @block.sync
            def _(sp):
                sp.dma_start(coeff[:, :], k.ins["coeff_rows"][:, l * RELS * RELS:(l + 1) * RELS * RELS]
                             ).then_inc(loaded, 16)
                sp.dma_start(brow[0:1, 0:D], k.ins["L2_gnn_bias"][l:l + 1]).then_inc(loaded, 16)
                sp.dma_start(brow[0:1, D:2 * D], k.ins["L2_gnn_bias"][l:l + 1]).then_inc(loaded, 16)
                for b in range(RELS):
                    sp.dma_start(basis[:, b], k.ins["L2_gnn_basis"][l, b].rearrange("(a p) n -> p a n", p=128)
                                 ).then_inc(loaded, 16)
                for b in range(NB):
                    sp.wait_ge(copied, 4 * (b + 1))
                    sp.dma_start(table[b * NP:(b + 1) * NP, :], ah[b % 2][:, :]).then_inc(stored[b % 2], 16)

            @block.gpsimd
            def _(pool):
                pool.wait_ge(stored[0], 16 * 3)
                pool.wait_ge(stored[1], 16 * 2)
                with pool.Fori(0, ET // 4) as i:
                    for s in range(4):
                        pool.wait_ge(used[s], i + 1)
                        nc.gpsimd.tensor_copy(idx[s][:, :], k.e_row[:, bass.ds(i * 4 + s, 1)]).then_inc(idx_ready[s], 1)
                        pool.wait_ge(idx_ready[s], i + 1)
                        pool.sem_inc(idx_seen, 1)
                        nc.gpsimd.indirect_dma_start(
                            out=rows[s][:, :], out_offset=None, in_=k.table_rows,
                            in_offset=bass.IndirectOffsetOnAxis(ap=idx[s][:, 0:1], axis=0)).then_inc(gathered[s], 16)

            @block.vector
            def _(dve):
                c, v = Chain(dve, step), nc.vector
                dve.wait_ge(loaded, 16 * 11)
                for r in range(RELS):
                    c(v.tensor_scalar(w[:, :, r, :], basis[:, 0], coeff[:, r * RELS:r * RELS + 1], None, ALU.mult))
                    for b in range(1, RELS):
                        ins = v.scalar_tensor_tensor(w[:, :, r, :], basis[:, b],
                                                     coeff[:, r * RELS + b:r * RELS + b + 1], w[:, :, r, :],
                                                     ALU.mult, ALU.add)
                        if b < RELS - 1:
                            c(ins)
                        else:
                            ins.then_inc(w_ready, 1)
                for b in range(NB):
                    if b >= 2:
                        dve.wait_ge(stored[b % 2], 16 * (b // 2))
                    for q in range(4):
                        dve.wait_ge(products, 4 * b + q + 1)
                        v.tensor_copy(ah[b % 2][:, q * 2 * D:(q + 1) * 2 * D], P[0:NP, q, :]).then_inc(copied, 1)
                with dve.Fori(0, ET // 4) as i:
                    for s in range(4):
                        t = i * 4 + s
                        dve.wait_ge(used[s], i + 1)
                        v.tensor_scalar(hot[s][:, :], k.const[:, C_IOTA:C_IOTA + NP], k.e_ldst[:, bass.ds(t, 1)],
                                        k.e_w[:, bass.ds(t, 1)], ALU.is_equal, ALU.mult).then_inc(hot_ready[s], 1)
                dve.wait_ge(whole, 1)
                for b in range(NB):
                    sums = P[0:NP, 4 + b // 2, (b % 2) * D:(b % 2 + 1) * D]
                    if l == 0:
                        v.tensor_scalar(k.o[:, b, :], sums, 0.0, None, ALU.max)
                    else:
                        v.tensor_tensor(k.x[:, b, :], k.x[:, b, :], sums, ALU.add)

            @block.tensor
            def _(pe):
                t = nc.tensor
                open_slots(pe, *used)
                for b in range(NB):
                    for q in range(4):
                        pe.wait_ge(w_ready, 2 * q + 2)
                        if b:
                            pe.wait_ge(copied, 4 * (b - 1) + q + 1)
                        for kk in range(KD):
                            m = t.matmul(P[0:NP, q, :], k.xT[:, kk, b * NP:(b + 1) * NP],
                                         w[:, kk, 2 * q:2 * q + 2, :], start=(kk == 0), stop=(kk == KD - 1))
                        m.then_inc(products, 1)
                pe.wait_ge(loaded, 16 * 11)
                for q in range(3):
                    t.matmul(P[0:NP, 4 + q, :], k.ones[0:1, 0:NP], brow[0:1, :], start=True, stop=False)
                with pe.Fori(0, ET // 4) as i:
                    for s in range(4):
                        b = pe.value_load(k.e_blk[0:1, bass.ds(i * 4 + s, 1)], min_val=0, max_val=NB - 1)
                        pe.wait_ge(hot_ready[s], i + 1)
                        pe.wait_ge(gathered[s], i * 16 + 16)
                        t.matmul(k.psum_flat[0:NP, bass.ds(b * D + 4 * 512, D)], hot[s][:, :], rows[s][:, :],
                                 start=False, stop=False, skip_group_check=True).then_inc(used[s], 1)
                for q in range(3):
                    m = t.matmul(P[0:NP, 4 + q, :], k.zeros[0:1, 0:NP], k.zeros[0:1, 0:512], start=False, stop=True)
                m.then_inc(whole, 1)
    k.stack = k.all


def turn_o(k, name, src, weight=None):
    nc, P = k.nc, k.psum
    turned = k.sem(f"{name}_turned")
    with nc.Block() as block:

        @block.tensor
        def _(pe):
            turn(k, pe, src, 0).then_inc(turned, 1)

        @block.scalar
        def _(act):
            act.wait_ge(turned, 1)
            for m in range(KD):
                nc.scalar.activation(k.xT[:, m, 0:4 * NP], P[:, 2 * m, 0:4 * NP], ACT.Copy)
                nc.scalar.activation(k.xT[:, m, 4 * NP:NODES], P[:, 2 * m + 1, 0:NP], ACT.Copy)


def rgcn(k):
    normalize(k, "ln_rgcn", k.x, k.xn, k.xT)
    rgcn_layer(k, 0)
    turn_o(k, "rgcn_mid", k.o)
    rgcn_layer(k, 1)


def moe2_attention(k):
    nc, P = k.nc, k.psum
    normalize(k, "ln_moe2", k.x, k.xn, k.xT)
    normalize(k, "rms1", k.xn, k.o, k.xT, rms=True, weight=col(k, "ln1_w", 0, KD))
    with ExitStack() as outer:
        k.stack = outer
        causal = k.sb("causal", [NP, NB, NC])
        neg = k.sb("causal_neg", [NP, NB + 1, NC], BF16)
        with ExitStack() as st:
            k.stack = st
            w = k.sb("rope_w", [128, 4, KD, D])
            wv = k.sb("rope_wv", [128, KD, D // 2])
            rope = k.sb("rope_tables", [128, 2, NC])
            part = k.sb("rope_part", [128, 2, NC])
            loaded, raw, raw_taken, step, vs = (k.sem(f"rope_{s}") for s in (
                "loaded", "products", "products_taken", "step", "v_products"))
            with nc.Block() as block:

                @block.sync
                def _(sp):
                    sp.dma_start(rope[:, :, :], k.ins["rope"]).then_inc(loaded, 16)
                    for n, m in enumerate(("rope_wq", "rope_wq_swapped", "rope_wk", "rope_wk_swapped")):
                        sp.dma_start(w[:, n], k.ins[m].rearrange("(a p) n -> p a n", p=128)).then_inc(loaded, 16)
                    sp.dma_start(wv[:, :, :], k.ins["moe2_wv"].rearrange("(a p) n -> p a n", p=128)
                                 ).then_inc(loaded, 16)

                @block.tensor
                def _(pe):
                    t = nc.tensor
                    pe.wait_ge(loaded, 16 * 6)
                    for g in range(4):
                        at = 4 * (g % 2)
                        if g >= 2:
                            pe.wait_ge(raw_taken, g - 1)
                        for n in range(2):
                            for a in range(2):
                                for kk in range(KD):
                                    m = t.matmul(P[:, at + 2 * n + a, 0:HC],
                                                 w[:, 2 * (g // 2) + n, kk, (g % 2) * 128:(g % 2 + 1) * 128],
                                                 k.xT[:, kk, a * HC:(a + 1) * HC], start=(kk == 0),
                                                 stop=(kk == KD - 1))
                        m.then_inc(raw, 1)
                    pe.wait_ge(raw_taken, 4)
                    for b in range(NB):
                        for kk in range(KD):
                            m = t.matmul(P[0:NP, b, 0:D // 2], k.xT[:, kk, b * NP:(b + 1) * NP], wv[:, kk, :],
                                         start=(kk == 0), stop=(kk == KD - 1))
                    m.then_inc(vs, 1)

                @block.vector
                def _(dve):
                    c, v = Chain(dve, step), nc.vector
                    iota = k.const[0:NP, C_IOTA:C_IOTA + NC]
                    c(v.memset(k.oT[:, :, :], 0.0))
                    c(v.memset(neg[:, NB, :], 0.0))
                    for b in range(NB):
                        c(v.tensor_scalar(causal[:, b, :], iota, k.const[0:NP, C_ROW + b:C_ROW + b + 1], None,
                                          ALU.is_le))
                        c(v.tensor_scalar(neg[:, b, :], iota, k.const[0:NP, C_ROW + b:C_ROW + b + 1], NEG,
                                          ALU.is_gt, ALU.mult))
                    dve.wait_ge(loaded, 16 * 6)
                    for g in range(4):
                        dve.wait_ge(raw, g + 1)
                        at = 4 * (g % 2)
                        for n in range(2):
                            c(v.tensor_tensor(part[:, n, :].rearrange("p (a n) -> p a n", a=2),
                                              P[:, at + 2 * n:at + 2 * n + 2, 0:HC],
                                              rope[:, n, :].rearrange("p (a n) -> p a n", a=2), ALU.mult))
                        to = (k.qT if g < 2 else k.kT)[:, g % 2, 0:NC]
                        c(v.tensor_tensor(to, part[:, 0, :], part[:, 1, :], ALU.add))
                        v.tensor_scalar(to, to, 1.0, None, ALU.mult).then_inc(raw_taken, 1)
                        dve.wait_ge(raw_taken, g + 1)
                    dve.wait_ge(vs, 1)
                    v.tensor_copy(k.v[:, :, 0:D // 2], P[0:NP, 0:NB, 0:D // 2])
        attention(k, "causal", k.qT, k.kT, k.v, [0, 0, 64, 64], k.oT_padded, neg, causal)
    with ExitStack() as st:
        k.stack = st
        wo = k.sb("wo", [128, KD, D])
        loaded, out = k.sem("wo_loaded"), k.sem("wo_products")
        with nc.Block() as block:

            @block.sync
            def _(sp):
                sp.dma_start(wo[:, :, :], k.ins["moe2_wo"].rearrange("(a p) n -> p a n", p=128)).then_inc(loaded, 16)

            @block.tensor
            def _(pe):
                pe.wait_ge(loaded, 16)
                for b in range(NB):
                    for kk in range(KD):
                        m = nc.tensor.matmul(P[0:NP, b, 0:D], k.oT[:, kk, b * NP:(b + 1) * NP], wo[:, kk, :],
                                             start=(kk == 0), stop=(kk == KD - 1))
                    m.then_inc(out, 1)

            @block.vector
            def _(dve):
                for b in range(NB):
                    dve.wait_ge(out, b + 1)
                    nc.vector.tensor_tensor(k.z[:, b, :], k.xn[:, b, :], P[0:NP, b, 0:D], ALU.add)
    k.stack = k.all


HID = int(8 / 3 * D)
HT = 6
HR = -(-HID // HT)


def experts_swiglu(k, acc):
    nc, P = k.nc, k.psum
    with ExitStack() as st:
        k.stack = st
        w13 = [k.sb(f"moe2_w13_{s}", [128, 2, KD, HT * HR]) for s in range(2)]
        w2 = [k.sb(f"moe2_w2_{s}", [HR, HT, D]) for s in range(2)]
        act1 = [k.sb(f"moe2_silu{s}", [HR, NC]) for s in range(2)]
        hT = k.sb("moe2_hT", [HR, HT, NC])
        two = lambda n: [k.sem(f"moe2_{n}{s}") for s in range(2)]
        w13_loaded, w13_used, w2_loaded, w2_used, up_given, silu_ready, given, taken = (two(n) for n in (
            "w13_loaded", "w13_used", "w2_loaded", "w2_used", "up_given", "silu_ready", "down_given", "down_taken"))
        gate_given, gate_taken, cleared = (k.sem(f"moe2_{n}") for n in ("gate_given", "gate_taken", "cleared"))
        half = HT // 2
        with nc.Block() as block:

            @block.sync
            def _(sp):
                with sp.Fori(0, EXPERTS // 2) as i:
                    for s in range(2):
                        e = i * 2 + s
                        sp.wait_ge(w13_used[s], i + 1)
                        for n, m in enumerate(("moe2_w1", "moe2_w3")):
                            sp.dma_start(w13[s][:, n], k.ins[m][bass.ds(e, 1)].rearrange(
                                "o (a p) n -> p (o a) n", p=128)).then_inc(w13_loaded[s], 16)
                        sp.wait_ge(w2_used[s], i + 1)
                        sp.dma_start(w2[s][:, :, :], k.ins["moe2_w2"][bass.ds(e, 1)].rearrange(
                            "o (a p) n -> p (o a) n", p=HR)).then_inc(w2_loaded[s], 16)

            @block.tensor
            def _(pe):
                t = nc.tensor

                def up(s, n, m, bank):
                    for a in range(2):
                        for kk in range(KD):
                            ins = t.matmul(P[0:HR, bank + a, 0:HC], w13[s][:, n, kk, m * HR:(m + 1) * HR],
                                           k.xT[:, kk, a * HC:(a + 1) * HC], start=(kk == 0), stop=(kk == KD - 1))
                    return ins

                open_slots(pe, *w13_used, *w2_used)
                with pe.Fori(0, EXPERTS // 2) as i:
                    for s in range(2):
                        pe.wait_ge(w13_loaded[s], i * 32 + 32)
                        for m in range(HT):
                            pe.wait_ge(silu_ready[m % 2], (i * 2 + s) * half + (m // 2 + 1))
                            up(s, 0, m, 2 * (m % 2)).then_inc(up_given[m % 2], 1)
                            pe.wait_ge(gate_taken, (i * 2 + s) * HT + (m + 1))
                            up(s, 1, m, 4).then_inc(gate_given, 1)
                        pe.wait_ge(gate_taken, (i * 2 + s + 1) * HT + 1)
                        t.matmul(P[:, 4, 0:1], k.zeros[0:1, 0:128], k.zeros[0:1, 0:1], start=True,
                                 stop=True).then_inc(w13_used[s], 1)
                        pe.wait_ge(w2_loaded[s], i * 16 + 16)
                        down(k, pe, hT, w2[s], None, HT, HR, i, s, given, taken)
                        t.matmul(P[:, 4, 0:1], k.zeros[0:1, 0:128], k.zeros[0:1, 0:1], start=True,
                                 stop=True).then_inc(w2_used[s], 1)

            @block.scalar
            def _(act):
                open_slots(act, *silu_ready)
                with act.Fori(0, EXPERTS // 2) as i:
                    for s in range(2):
                        for m in range(HT):
                            act.wait_ge(up_given[m % 2], (i * 2 + s) * half + m // 2 + 1)
                            act.wait_ge(gate_taken, (i * 2 + s) * HT + max(m, 1))
                            nc.scalar.activation(act1[m % 2][:, :].rearrange("p (a n) -> p a n", a=2),
                                                 P[0:HR, 2 * (m % 2):2 * (m % 2) + 2, 0:HC],
                                                 ACT.Silu).then_inc(silu_ready[m % 2], 1)

            @block.vector
            def _(dve):
                v = nc.vector
                open_slots(dve, gate_taken, *taken)
                v.memset(acc[:, :, :], 0.0).then_inc(cleared, 1)
                dve.wait_ge(cleared, 1)
                with dve.Fori(0, EXPERTS // 2) as i:
                    for s in range(2):
                        for m in range(HT):
                            dve.wait_ge(silu_ready[m % 2], (i * 2 + s) * half + (m // 2 + 2))
                            dve.wait_ge(gate_given, (i * 2 + s) * HT + m + 1)
                            v.tensor_tensor(hT[:, m, :].rearrange("p (a n) -> p a n", a=2), P[0:HR, 4:6, 0:HC],
                                            act1[m % 2][:, :].rearrange("p (a n) -> p a n", a=2),
                                            ALU.mult).then_inc(gate_taken, 1)
                        gather_outputs(k, dve, acc, i, s, given, taken)
    k.stack = k.all


def moe2(k):
    moe2_attention(k)
    normalize(k, "rms2", k.z, k.xn, k.xT, rms=True, weight=col(k, "ln2_w", 0, KD))
    route(k, "moe2_route", k.xT, KD, "moe2_router", None, 2, 1e-9)
    experts_swiglu(k, k.o)
    add_to_x(k, "moe2_z", k.z)
    add_to_x(k, "moe2", k.o)


def edge_conv(k):
    nc, P = k.nc, k.psum
    normalize(k, "ln_edge", k.x, k.xn, k.xT)
    W = 2 * D
    with ExitStack() as st:
        k.stack = st
        own = k.sb("edge_own", [NP, NB, W])
        sums = k.sb("edge_sums", [NP, NB, W])
        with ExitStack() as st2:
            k.stack = st2
            w1 = k.sb("edge_w1", [128, 4, W])
            brow = k.sb("edge_b1", [1, W])
            other = k.sb("edge_other", [NP, NB, W])
            loaded, products, copied, stored, taken = (k.sem(f"edge_node_{s}") for s in (
                "loaded", "products", "copied", "stored", "taken"))
            with nc.Block() as block:

                @block.sync
                def _(sp):
                    sp.dma_start(w1[:, :, :], k.ins["L3_gnn_W1"].rearrange("(a p) n -> p a n", p=128)
                                 ).then_inc(loaded, 16)
                    sp.dma_start(brow[:, :], k.ins["L3_gnn_b1"].rearrange("(a n) -> a n", a=1)).then_inc(loaded, 16)
                    for b in range(NB):
                        sp.wait_ge(copied, b + 1)
                        sp.dma_start(k.node_tables[b * NP:(b + 1) * NP, :], other[:, b, :]).then_inc(stored, 16)
                    sp.wait_ge(stored, 16 * NB)

                @block.tensor
                def _(pe):
                    t = nc.tensor
                    pe.wait_ge(loaded, 32)
                    for b in range(NB):
                        q = 2 * (b % 2)
                        if b >= 2:
                            pe.wait_ge(taken, b - 1)
                        for kk in range(KD):
                            t.matmul(P[0:NP, q, :], k.xT[:, kk, b * NP:(b + 1) * NP], w1[:, KD + kk, :],
                                     start=(kk == 0), stop=(kk == KD - 1))
                        for kk in range(KD):
                            t.matmul(P[0:NP, q + 1, :], k.xT[:, kk, b * NP:(b + 1) * NP], w1[:, kk, :],
                                     start=(kk == 0), stop=False)
                        t.matmul(P[0:NP, q + 1, :], k.ones[0:1, 0:NP], brow[:, :], start=False,
                                 stop=True).then_inc(products, 1)

                @block.vector
                def _(dve):
                    v = nc.vector
                    for b in range(NB):
                        q = 2 * (b % 2)
                        dve.wait_ge(products, b + 1)
                        v.tensor_copy(other[:, b, :], P[0:NP, q, :]).then_inc(copied, 1)
                        dve.wait_ge(copied, b + 1)
                        v.tensor_tensor(own[:, b, :], P[0:NP, q + 1, :], other[:, b, :],
                                        ALU.subtract).then_inc(taken, 1)
        with ExitStack() as st2:
            k.stack = st2
            four = lambda n: [k.sem(f"edge_{n}{s}") for s in range(4)]
            idx_ready, gathered, hot_ready, hotT_given, hotT_ready, mine, rows_free, hid_ready, used = (
                four(n) for n in ("idx_ready", "rows_gathered", "onehot_ready", "onehotT_given", "onehotT_ready",
                                  "own_given", "rows_free", "hidden_ready", "hidden_used"))
            idx_seen, whole, summed = k.sem("edge_idx_seen"), k.sem("edge_whole"), k.sem("edge_summed")
            idx = [k.sb(f"edge_idx{s}", [LANES, 1], U32) for s in range(4)]
            rows = [k.sb(f"edge_rows{s}", [LANES, W]) for s in range(4)]
            pre = [k.sb(f"edge_pre{s}", [LANES, W]) for s in range(4)]
            hid = [k.sb(f"edge_hid{s}", [LANES, W]) for s in range(4)]
            hot = [k.sb(f"edge_hot_{s}", [LANES, NP]) for s in range(4)]
            hotT = [k.sb(f"edge_hotT{s}", [NP, LANES]) for s in range(4)]
            with nc.Block() as block:

                @block.gpsimd
                def _(pool):
                    with pool.Fori(0, ET // 4) as i:
                        for s in range(4):
                            pool.wait_ge(rows_free[s], i + 1)
                            nc.gpsimd.tensor_copy(idx[s][:, :], k.e_srci[:, bass.ds(i * 4 + s, 1)]
                                                  ).then_inc(idx_ready[s], 1)
                            pool.wait_ge(idx_ready[s], i + 1)
                            pool.sem_inc(idx_seen, 1)
                            nc.gpsimd.indirect_dma_start(
                                out=rows[s][:, :], out_offset=None, in_=k.node_rows,
                                in_offset=bass.IndirectOffsetOnAxis(ap=idx[s][:, 0:1], axis=0)
                            ).then_inc(gathered[s], 16)

                @block.tensor
                def _(pe):
                    t = nc.tensor

                    def onehotT(s, n, m=None):
                        pe.wait_ge(hot_ready[s], n + 1)
                        if m is not None:
                            pe.wait_ge(hotT_ready[(s + 3) % 4], m + 1)
                        t.transpose(P[0:NP, 5, s * 128:(s + 1) * 128], hot[s][:, :],
                                    k.const[:, C_ID:C_ID + 128]).then_inc(hotT_given[s], 1)

                    def own_rows(i, s, n, free):
                        b = pe.value_load(k.e_blk[0:1, bass.ds(i * 4 + s, 1)] if not isinstance(i, int) else
                                          k.e_blk[0:1, i * 4 + s:i * 4 + s + 1], min_val=0, max_val=NB - 1)
                        pe.wait_ge(hotT_ready[s % 4], n + 1)
                        for sem, val in free:
                            pe.wait_ge(sem, val)
                        t.matmul(P[:, 6 + s % 2, :], hotT[s % 4][:, :], own[:, bass.ds(b, 1), :],
                                 start=True, stop=True).then_inc(mine[s % 4], 1)

                    open_slots(pe, *mine, *used)
                    for b in range(NB):
                        t.matmul(P[0:NP, b, :], k.zeros[0:1, 0:NP], k.zeros[0:1, 0:512], start=True, stop=False)
                    onehotT(0, 0)
                    own_rows(0, 0, 0, [])
                    onehotT(1, 0, 0)
                    with pe.Fori(0, ET // 4) as i:
                        for s in range(4):
                            onehotT((s + 2) % 4, i + (s + 2) // 4, i + (s + 1) // 4)
                            free = [(rows_free[s - 1], i + 2)] if s >= 1 else [(rows_free[3], i + 1)]
                            own_rows(i, s + 1, i + (s + 1) // 4, free)
                            b = pe.value_load(k.e_blk[0:1, bass.ds(i * 4 + s, 1)], min_val=0, max_val=NB - 1)
                            pe.wait_ge(hid_ready[s], i + 2)
                            t.matmul(k.psum_flat[0:NP, bass.ds(b * 512, 512)], hot[s][:, :], hid[s][:, :],
                                     start=False, stop=False, skip_group_check=True).then_inc(used[s], 1)
                    for b in range(NB):
                        m = t.matmul(P[0:NP, b, :], k.zeros[0:1, 0:NP], k.zeros[0:1, 0:512], start=False, stop=True)
                    m.then_inc(whole, 1)

                @block.scalar
                def _(act):
                    a = nc.scalar

                    def copy_onehotT(s, n):
                        act.wait_ge(hotT_given[s], n + 1)
                        act.wait_ge(mine[s], n + 1)
                        a.activation(hotT[s][:, :], P[0:NP, 5, s * 128:(s + 1) * 128],
                                     ACT.Copy).then_inc(hotT_ready[s], 1)

                    open_slots(act, *hid_ready)
                    copy_onehotT(0, 0)
                    copy_onehotT(1, 0)
                    with act.Fori(0, ET // 4) as i:
                        for s in range(4):
                            copy_onehotT((s + 2) % 4, i + (s + 2) // 4)
                            act.wait_ge(rows_free[s], i + 2)
                            act.wait_ge(used[s], i + 1)
                            a.activation(hid[s][:, :], pre[s][:, :], ACT.Relu).then_inc(hid_ready[s], 1)

                @block.vector
                def _(dve):
                    v = nc.vector

                    def onehot(t, s, n):
                        dve.wait_ge(used[s], n + 1)
                        at = bass.ds(t, 1) if not isinstance(t, int) else slice(t, t + 1)
                        v.tensor_scalar(hot[s][:, :], k.const[:, C_IOTA:C_IOTA + NP], k.e_ldst[:, at], None,
                                        ALU.is_equal).then_inc(hot_ready[s], 1)

                    open_slots(dve, *rows_free)
                    onehot(0, 0, 0)
                    onehot(1, 1, 0)
                    with dve.Fori(0, ET // 4) as i:
                        for s in range(4):
                            onehot(i * 4 + (s + 2), (s + 2) % 4, i + (s + 2) // 4)
                            dve.wait_ge(mine[s], i + 2)
                            dve.wait_ge(gathered[s], i * 16 + 16)
                            dve.wait_ge(hid_ready[s], i + 1)
                            v.tensor_tensor(pre[s][:, :], P[:, 6 + s % 2, :], rows[s][:, :],
                                            ALU.add).then_inc(rows_free[s], 1)
                    dve.wait_ge(whole, 1)
                    v.tensor_copy(sums[:, :, :], P[0:NP, 0:NB, :])
        with ExitStack() as st2:
            k.stack = st2
            w2 = k.sb("edge_w2", [128, 4, D])
            b2 = k.sb("edge_b2", [NP, D])
            sumsT = k.sb("edge_sumsT", [128, 4, NC])
            rdeg = k.sb("edge_rdeg", [NP, 2, NB])
            y = k.sb("edge_y", [NP, NB, D])
            loaded, turned, copied, out, step = (k.sem(f"edge_out_{s}") for s in (
                "loaded", "turned", "copied", "products", "step"))
            with nc.Block() as block:

                @block.sync
                def _(sp):
                    sp.dma_start(w2[:, :, :], k.ins["L3_gnn_W2"].rearrange("(a p) n -> p a n", p=128)
                                 ).then_inc(loaded, 16)
                    sp.dma_start(b2[:, :], k.ins["edge_b2"]).then_inc(loaded, 16)

                @block.tensor
                def _(pe):
                    t = nc.tensor
                    for m in range(4):
                        for b in range(NB):
                            ins = t.transpose(P[:, 2 * m + b // 4, (b % 4) * NP:(b % 4 + 1) * NP],
                                              sums[:, b, m * 128:(m + 1) * 128], k.const[0:NP, C_ID:C_ID + NP])
                        ins.then_inc(turned, 1)
                    pe.wait_ge(loaded, 32)
                    pe.wait_ge(copied, 4)
                    for b in range(NB):
                        for kk in range(4):
                            ins = t.matmul(P[0:NP, b, 0:D], sumsT[:, kk, b * NP:(b + 1) * NP], w2[:, kk, :],
                                           start=(kk == 0), stop=(kk == 3))
                        ins.then_inc(out, 1)

                @block.scalar
                def _(act):
                    for m in range(4):
                        act.wait_ge(turned, m + 1)
                        nc.scalar.activation(sumsT[:, m, 0:4 * NP], P[:, 2 * m, 0:4 * NP], ACT.Copy)
                        nc.scalar.activation(sumsT[:, m, 4 * NP:NODES], P[:, 2 * m + 1, 0:NP],
                                             ACT.Copy).then_inc(copied, 1)

                @block.vector
                def _(dve):
                    c, v = Chain(dve, step), nc.vector
                    c(v.tensor_scalar(rdeg[:, 0, :], k.deg[:, :], 1e-8, None, ALU.add))
                    c(v.reciprocal(rdeg[:, 1, :], rdeg[:, 0, :]))
                    dve.wait_ge(loaded, 32)
                    for b in range(NB):
                        dve.wait_ge(out, b + 1)
                        c(v.scalar_tensor_tensor(y[:, b, :], b2[:, :], k.deg[:, b:b + 1], P[0:NP, b, 0:D], ALU.mult,
                                                 ALU.add))
                        c(v.scalar_tensor_tensor(k.x[:, b, :], y[:, b, :], rdeg[:, 1, b:b + 1], k.x[:, b, :],
                                                 ALU.mult, ALU.add))
    k.stack = k.all


def moe3(k):
    nc, P = k.nc, k.psum
    tiles = 8
    normalize(k, "ln_moe3", k.x, k.xn, k.xT)
    with ExitStack() as outer:
        k.stack = outer
        hT = k.sb("moe3_hT", [128, tiles, NC])
        with ExitStack() as st:
            k.stack = st
            w1 = k.sb("moe3_w1", [128, KD, tiles * 128])
            loaded = k.sem("moe3_w1_loaded")
            given, taken = ([k.sem(f"moe3_up_{n}{s}") for s in range(2)] for n in ("given", "taken"))
            with nc.Block() as block:

                @block.sync
                def _(sp):
                    sp.dma_start(w1[:, :, :], k.ins["L3_ffn_W1"].rearrange("(a p) n -> p a n", p=128)
                                 ).then_inc(loaded, 16)

                @block.tensor
                def _(pe):
                    pe.wait_ge(loaded, 16)
                    for m in range(tiles):
                        q = m % 2
                        if m >= 2:
                            pe.wait_ge(taken[q], m // 2)
                        for a in range(2):
                            for kk in range(KD):
                                ins = nc.tensor.matmul(P[:, 2 * q + a, 0:HC], w1[:, kk, m * 128:(m + 1) * 128],
                                                       k.xT[:, kk, a * HC:(a + 1) * HC], start=(kk == 0),
                                                       stop=(kk == KD - 1))
                        ins.then_inc(given[q], 1)

                @block.scalar
                def _(act):
                    for m in range(tiles):
                        act.wait_ge(given[m % 2], m // 2 + 1)
                        nc.scalar.activation(hT[:, m, :].rearrange("p (a n) -> p a n", a=2),
                                             P[:, 2 * (m % 2):2 * (m % 2) + 2, 0:HC], ACT.Gelu,
                                             bias=col(k, "moe3_b1", m)).then_inc(taken[m % 2], 1)
        route(k, "moe3_route", hT, tiles, "moe3_router", "L3_ffn_bg", 1, None)
        with ExitStack() as st:
            k.stack = st
            wd = [k.sb(f"moe3_wd{s}", [128, tiles, D]) for s in range(2)]
            bd = [k.sb(f"moe3_bd{s}", [1, D]) for s in range(2)]
            w_loaded, w_used, given, taken = ([k.sem(f"moe3_{n}{s}") for s in range(2)] for n in (
                "wd_loaded", "wd_used", "down_given", "down_taken"))
            cleared = k.sem("moe3_cleared")
            with nc.Block() as block:

                @block.sync
                def _(sp):
                    with sp.Fori(0, EXPERTS // 2) as i:
                        for s in range(2):
                            e = i * 2 + s
                            sp.wait_ge(w_used[s], i + 1)
                            sp.dma_start(wd[s][:, :, :], k.ins["L3_ffn_Wd"][bass.ds(e, 1)].rearrange(
                                "o (a p) n -> p (o a) n", p=128)).then_inc(w_loaded[s], 16)
                            sp.dma_start(bd[s][:, :], k.ins["L3_ffn_bd"][bass.ds(e, 1), :]).then_inc(w_loaded[s], 16)

                @block.tensor
                def _(pe):
                    open_slots(pe, *w_used)
                    with pe.Fori(0, EXPERTS // 2) as i:
                        for s in range(2):
                            pe.wait_ge(w_loaded[s], i * 32 + 32)
                            down(k, pe, hT, wd[s], bd[s][:, :], tiles, 128, i, s, given, taken)
                            nc.tensor.matmul(P[:, 4, 0:1], k.zeros[0:1, 0:128], k.zeros[0:1, 0:1], start=True,
                                             stop=True).then_inc(w_used[s], 1)

                @block.vector
                def _(dve):
                    open_slots(dve, *taken)
                    nc.vector.memset(k.o[:, :, :], 0.0).then_inc(cleared, 1)
                    dve.wait_ge(cleared, 1)
                    with dve.Fori(0, EXPERTS // 2) as i:
                        for s in range(2):
                            gather_outputs(k, dve, k.o, i, s, given, taken)
    k.stack = k.all
    add_to_x(k, "moe3", k.o)


def store(k):
    done = k.sem("stored")
    with k.nc.Block() as block:

        @block.sync
        def _(sp):
            sp.dma_start(k.out.rearrange("(b p) d -> p b d", b=NB), k.x[:, :, :]).then_inc(done, 16)
            sp.wait_ge(done, 16)
STAGES = [edges, conv_layers, moe0, sage, moe1, rgcn, moe2, edge_conv, moe3, store]


def build(nc, ins, out, stages=None):
    k = Kernel(nc, ins, out)
    with k.all:
        k.const = k.sb("const", [128, C_END])
        k.ones = k.sb("ones", [128, 512])
        k.zeros = k.sb("zeros", [128, 512])
        k.x = k.sb("x_res", [NP, NB, D])
        k.xn = k.sb("xn", [NP, NB, D])
        k.xT = k.sb("xT", [128, KD, NC])
        k.C = k.sb("C", [NP, NB, NC])
        k.CT = k.sb("CT", [NP, NB, NC])
        k.deg = k.sb("deg", [NP, NB])
        k.e_ldst = k.sb("e_ldst", [LANES, ET + AHEAD])
        k.e_src = k.sb("e_src", [LANES, ET])
        k.e_w = k.sb("e_w", [LANES, ET])
        k.e_row = k.sb("e_row", [LANES, ET], U32)
        k.e_srci = k.sb("e_srci", [LANES, ET], U32)
        k.e_blk = k.sb("e_blk", [1, ET + AHEAD], I32)
        k.negC = k.sb("negC", [NP, NB + 1, NC], BF16)
        k.ident16 = k.sb("ident16", [128, 128], BF16)
        k.wconv = k.sb("wconv", [128, 3, KD, 4 * D])
        k.wconv_loaded = k.all.enter_context(nc.semaphore("wconv_loaded"))
        k.col = k.sb("columns", [128, sum(COLS.values())])
        k.brow = k.sb("brow", [1, 2 * D])
        k.qT = k.sb("qT", [128, KD, NODES + NP])
        k.kT = k.sb("kT", [128, KD, NC])
        k.v = k.sb("v", [NP, NB, D])
        k.o = k.sb("o", [NP, NB, D])
        k.oT_padded = k.sb("oT", [128, KD, NP + NC])
        k.oT = k.oT_padded[:, :, NP:NP + NC]
        k.gate = k.sb("gate", [NP, NB, EXPERTS])
        k.z = k.sb("z", [NP, NB, D])
        k.picked = k.sb("picked", [1, 2], I32)
        k.picked_b1 = k.sb("picked_b1", [128, 8])
        k.tables = nc.dram_tensor("edge_tables", (NODES, RELS * D), F32).ap()
        k.table_rows = k.tables.rearrange("n (r d) -> (n r) d", d=D)
        k.node_tables = nc.dram_tensor("node_tables", (NODES, 2 * D), F32).ap()
        k.node_rows = k.node_tables
        k.psum = k.all.enter_context(nc.psum_tensor("psum", [128, 8, 512], F32))
        k.psum_flat = k.psum[:, :, :].rearrange("p b n -> p (b n)")
        for s in (stages or STAGES):
            s(k)
            k.end_layer()
    return k


def layout(i):
    a = {"const": constants()}
    a["x"] = i["x"].reshape(NB, NP, D).transpose(1, 0, 2)
    for n in ("src", "dst", "edge_type_8", "edge_weight1"):
        a[n] = i[n].reshape(EP, EC)

    def tiles(v):
        v = v.reshape(*v.shape[:-1], -1, 128)
        return np.moveaxis(v, -1, 0).reshape(128, -1)

    def padded(v):
        v = np.concatenate([v, np.zeros_like(v[:1])]).reshape(EXPERTS + 1, KD, 128)
        return v.transpose(2, 1, 0).reshape(128, -1)

    def router(w):
        return w.reshape(-1, 128, EXPERTS).transpose(1, 0, 2).reshape(128, -1)

    c = {"conv_bias": tiles(np.stack([i["L0_gnn_bq"], i["L0_gnn_bk"], i["L0_gnn_bs"]], 1)),
         "bn_gamma": tiles(i["L0_gnn_bn_gamma"]), "bn_beta": tiles(i["L0_gnn_bn_beta"]),
         "moe0_ln_g": padded(i["L0_ffn_ln_g"]), "moe0_ln_b": padded(i["L0_ffn_ln_b"]),
         "moe0_b1": tiles(i["L0_ffn_b1"]), "moe3_b1": tiles(i["L3_ffn_b1"]),
         "ln1_w": tiles(i["L2_ffn_ln1_w"]), "ln2_w": tiles(i["L2_ffn_ln2_w"]),
         "moe0_router": router(i["L0_ffn_Wr"]), "moe1_router": router(i["L1_ffn_Wr"]),
         "moe2_router": router(i["L2_ffn_router_w"].T), "moe3_router": router(i["L3_ffn_Wg"])}
    a["cols"] = np.concatenate([c[n] for n in COLS], 1)
    a["coeff_rows"] = np.broadcast_to(i["L2_gnn_coeff"].reshape(1, -1), (128, i["L2_gnn_coeff"].size))
    a["moe1_b1"] = i["L1_ffn_b1"].reshape(EXPERTS, -1, 128).transpose(0, 2, 1)
    for n in ("gamma", "beta"):
        a[f"moe1_{n}"] = np.broadcast_to(i[f"L1_ffn_{n}"].reshape(1, D), (NP, D))
    a["edge_b2"] = np.broadcast_to(i["L3_gnn_b2"].reshape(1, D), (NP, D))
    swap = np.arange(D).reshape(-1, 2, 32)[:, ::-1].reshape(-1)
    wq = i["L2_ffn_wq"]
    wk = i["L2_ffn_wk"].reshape(2, 1, 64, D).repeat(2, 1).reshape(D, D)
    a["rope_wq"], a["rope_wq_swapped"] = wq.T, wq[swap].T
    a["rope_wk"], a["rope_wk_swapped"] = wk.T, wk[swap].T
    a["moe2_wv"], a["moe2_wo"] = i["L2_ffn_wv"].T, i["L2_ffn_wo"].T
    a["rope"] = rope_tables()
    wide = lambda w: np.concatenate([w, np.zeros((EXPERTS, HT * HR - HID, D), np.float32)], 1)
    for n, m in (("moe2_w1", "L2_ffn_w1"), ("moe2_w3", "L2_ffn_w3")):
        a[n] = wide(i[m]).transpose(0, 2, 1)
    a["moe2_w2"] = wide(i["L2_ffn_w2"].transpose(0, 2, 1))
    for n in i:
        if n not in a:
            a[n] = i[n]
    return {n: np.ascontiguousarray(v) for n, v in a.items()}


def rope_tables():
    hd = 64
    inv = 1.0 / 10000.0 ** (np.arange(0, hd, 2, dtype=np.float32) / hd)
    f = np.outer(np.arange(NC, dtype=np.float32), inv)
    e = np.concatenate([f, f], -1).T
    sign = np.where(np.arange(hd) < hd // 2, -1.0, 1.0)[:, None]
    both = np.stack([np.cos(e), np.sin(e) * sign], 1)
    return np.concatenate([both, both]).astype(np.float32)


def kernel(**inputs):
    import concourse.bacc as bacc
    from concourse.bass_utils import run_bass_kernel_spmd

    arrays = layout({n: np.asarray(v) for n, v in inputs.items()})
    nc = bacc.Bacc("TRN2", target_bir_lowering=False, num_devices=1)
    ins = {n: nc.dram_tensor(f"in_{n}", a.shape, mybir.dt.from_np(a.dtype), kind="ExternalInput").ap()
           for n, a in arrays.items()}
    out = nc.dram_tensor("out", (NODES, D), F32, kind="ExternalOutput").ap()
    build(nc, ins, out)
    r = run_bass_kernel_spmd(nc, [{f"in_{n}": a for n, a in arrays.items()}], core_ids=[0])
    return r.results[0]["out"]
```

```python
import numpy as np
import concourse.bass as bass
from concourse import mybir
from contextlib import ExitStack

F32 = mybir.dt.float32
BF16 = mybir.dt.bfloat16
F32R = mybir.dt.float32r
F16 = mybir.dt.float16
I32 = mybir.dt.int32
U32 = mybir.dt.uint32
ALU = mybir.AluOpType
ACT = mybir.ActivationFunctionType
AX = mybir.AxisListType

NODES = 625
NB = 5
NP = NODES // NB
NC = NODES + 1
HC = NC // 2
D = 256
KD = D // 128
EDGES = 20625
EP = 125
EC = EDGES // EP
LANES = 128
ET = -(-((EDGES + NB * (LANES - 1)) // LANES) // 4) * 4
AHEAD = 4
EXPERTS = 8
RELS = 8
BASIS_LOADS = 16 * (1 + RELS)
NEG = -1e30
LN_EPS = 1e-5

C_ID = 0
C_TRI = C_ID + 128
C_IOTA = C_TRI + 128
C_RANK = C_IOTA + NC
C_ROW = C_RANK + EXPERTS * EXPERTS
C_END = C_ROW + NB


def constants():
    c = np.zeros((128, C_END), np.float32)
    c[:, C_ID:C_ID + 128] = np.eye(128)
    c[:, C_TRI:C_TRI + 128] = np.triu(np.ones((128, 128)), 1)
    c[:, C_IOTA:C_IOTA + NC] = np.arange(NC)
    c[:, C_ROW:C_END] = np.arange(128)[:, None] + NP * np.arange(NB)
    c[:, C_RANK:C_ROW] = np.tril(np.ones((EXPERTS, EXPERTS)), -1).reshape(-1)
    return c


COLS = {"conv_bias": 3 * 3 * KD, "bn_gamma": 2 * KD, "bn_beta": 2 * KD, "moe0_ln_g": KD * (EXPERTS + 1),
        "moe0_ln_b": KD * (EXPERTS + 1), "moe0_b1": EXPERTS * 8, "moe3_b1": 8, "ln1_w": KD, "ln2_w": KD,
        "moe0_router": KD * EXPERTS, "moe1_router": KD * EXPERTS, "moe2_router": KD * EXPERTS,
        "moe3_router": 8 * EXPERTS}


def col(k, name, first=0, count=1):
    at = sum(w for n, w in COLS.items() if list(COLS).index(n) < list(COLS).index(name))
    if isinstance(first, int):
        return k.col[:, at + first:at + first + count]
    return k.col[:, bass.ds(first + at, count)]


class Kernel:

    def __init__(self, nc, ins, out):
        self.nc, self.ins, self.out = nc, ins, out
        self.all = ExitStack()
        self.layer_sems = []
        self.stack = self.all

    def sb(self, name, shape, dt=F32):
        return self.stack.enter_context(self.nc.sbuf_tensor(name, shape, dt))

    def sem(self, name):
        self.layer_sems.append(self.nc.alloc_semaphore(name))
        return self.layer_sems[-1]

    def end_layer(self):
        self.nc.clear_and_free_semaphores(self.layer_sems)
        self.nc.all_engine_barrier()
        self.layer_sems = []


class Chain:

    def __init__(self, eng, sem):
        self.eng, self.sem, self.n = eng, sem, 0

    def __call__(self, ins):
        ins.then_inc(self.sem, 1)
        self.n = self.n + 1
        self.eng.wait_ge(self.sem, self.n)


def open_slots(eng, *sems):
    for s in sems:
        eng.sem_inc(s, 1)


def tile_blocks(k, pe, i):
    word = pe.value_load(k.e_blk[0:1, bass.ds(i, 1)], min_val=0, max_val=8 ** 8 - 1)
    of = []
    for _ in range(8):
        of.append(k.nc.s_assert_within(word % 8, min_val=0, max_val=NB - 1, skip_runtime_bounds_check_because=(
            "every digit counts which of the blocks 1 to NB - 1 start at its tile or before it")))
        word = word // 8
    return of


def load_basis(k, eng, l):
    for b in range(RELS):
        eng.dma_start(k.basis[:, b], k.ins["L2_gnn_basis"][l, b].rearrange("(a p) n -> p a n", p=128)
                      ).then_inc(k.basis_loaded, 16)


def mix_basis(k, v, w, l, r, b):
    at = bass.ds(r * RELS + b, 1)
    to = w[:, :, bass.ds(r, 1), :] if not isinstance(r, int) else w[:, :, r:r + 1, :]
    base = k.basis[:, b:b + 1].rearrange("p o a n -> p a o n")
    if b == 0:
        return v.tensor_scalar(to, base, k.coeff[:, l, at], None, ALU.mult)
    return v.scalar_tensor_tensor(to, base, k.coeff[:, l, at], to, ALU.mult, ALU.add)


def edges(k):
    nc, P = k.nc, k.psum
    with ExitStack() as st:
        k.stack = st
        ints = k.sb("edge_ints", [EP, 3, EC], I32)
        flt = k.sb("edge_floats", [EP, 3, EC])
        ge = k.sb("edge_ge", [EP, NB + 1, EC])
        member = k.sb("edge_member", [EP, NB, EC])
        count = k.sb("edge_count", [EP, NB, EC])
        ones = k.sb("edge_ones", [EP, EC])
        tot = k.sb("edge_tot", [128, 4, NB + 1])
        toti = k.sb("edge_toti", [128, NB], I32)
        ldst = k.sb("edge_ldst", [EP, EC])
        blk = k.sb("edge_blk", [EP, EC])
        pos = k.sb("edge_pos", [EP, EC])
        posi = k.sb("edge_posi", [EP, 2, EC], I32)
        lane = k.sb("edge_lane", [EP, 2, EC])
        field = k.sb("edge_field", [EP, 2, EC])
        hot = [k.sb(f"edge_hot{s}", [EP, 5, LANES]) for s in range(3)]
        put = [k.sb(f"edge_put{s}", [EP, 2, ET]) for s in range(5)]
        keyi = k.sb("edge_keyi", [LANES, 4, ET], I32)
        tb = k.sb("edge_tb", [1, ET + 2 * AHEAD])
        tbw = k.sb("edge_tb_words", [1, ET // 4])
        dhot = [k.sb(f"edge_dhot{s}", [LANES, 4, NP], BF16) for s in range(2)]
        shot = [k.sb(f"edge_shot{s}", [LANES, NC], BF16) for s in range(4)]
        iota16 = k.sb("iota16", [128, NC], F16)
        iota = k.const[:, C_IOTA:C_IOTA + NC]

        loaded = k.sem("edges_loaded")
        step = k.sem("edges_step")
        rows = k.sem("edge_row_totals")
        prefix = k.sem("edge_prefix")
        put_ready = [k.sem(f"edge_put_ready{s}") for s in range(5)]
        put_used = [k.sem(f"edge_put_used{s}") for s in range(5)]
        lanes_ready, lanes_used = ([k.sem(f"edge_{n}{s}") for s in range(3)] for n in ("lanes_ready", "lanes_used"))
        lanes_far = [k.sem(f"edge_lanes_far{s}") for s in range(3)]
        dhot_far = [k.sem(f"edge_dhot_far{s}") for s in range(2)]
        squared = k.sem("edge_squared")
        laned = k.sem("edge_laned")
        sorted_ = k.sem("edges_sorted")
        unpacked = k.sem("edges_unpacked")
        blocks_known = k.sem("edge_blocks_known")
        dhot_ready, dhot_used = ([k.sem(f"edge_{n}{s}") for s in range(2)] for n in ("dhot_ready", "dhot_used"))
        shot_ready, shot_used = ([k.sem(f"edge_{n}{s}") for s in range(4)] for n in ("shot_ready", "shot_used"))
        counted = k.sem("edges_counted")
        c_ready = k.sem("c_ready")
        turned = k.sem("c_turned")
        ct_half = k.sem("ct_half_copied")
        with nc.Block() as block:

            @block.sync
            def _(sp):
                sp.dma_start(k.const[:, :], k.ins["const"]).then_inc(loaded, 16)
                sp.dma_start(ints[:, 0, :], k.ins["dst"]).then_inc(loaded, 16)
                sp.dma_start(ints[:, 1, :], k.ins["src"]).then_inc(loaded, 16)
                sp.dma_start(ints[:, 2, :], k.ins["edge_type_8"]).then_inc(loaded, 16)
                sp.dma_start(field[:, 1, :], k.ins["edge_weight1"]).then_inc(loaded, 16)
                sp.dma_start(k.x[:, :, :], k.ins["x"]).then_inc(loaded, 16)
                sp.dma_start(k.col[:, :], k.ins["cols"]).then_inc(loaded, 16)
                for i in range(3):
                    for n, m in enumerate(("Wq", "Wk", "Ws", "Wv")):
                        sp.dma_start(k.wconv[:, i, :, n * D:(n + 1) * D],
                                     k.ins[f"L0_gnn_{m}"][i].rearrange("(a p) n -> p a n", p=128)
                                     ).then_inc(k.wconv_loaded, 16)
                sp.dma_start(k.coeff[:, :, :], k.ins["coeff_rows"].rearrange("p (l n) -> p l n", l=2)
                             ).then_inc(k.basis_loaded, 16)
                load_basis(k, sp, 0)

            @block.vector
            def _(dve):
                c = Chain(dve, step)
                v = nc.vector
                c(v.memset(ones[:, :], 1.0))
                c(v.memset(tot[:, :, :], 0.0))
                c(v.memset(k.ones[:, :], 1.0))
                c(v.memset(k.zeros[:, :], 0.0))
                c(v.memset(k.C[:, :, NODES:NC], 0.0))
                c(v.memset(k.CT[:, :, NODES:NC], 0.0))
                c(v.memset(k.xT[:, :, NODES:NC], 0.0))
                c(v.memset(k.oT_padded[:, :, :], 0.0))
                c(v.memset(k.qT[:, :, NC:NODES + NP], 0.0))
                dve.wait_ge(loaded, 16 * 7)
                c(v.tensor_copy(iota16[:, :], iota))
                c(v.tensor_copy(flt[:, :, :], ints[:, :, :]))
                for b in range(NB + 1):
                    c(v.tensor_scalar(ge[:, b, :], flt[:, 0, :], float(b * NP), None, ALU.is_ge))
                c(v.tensor_tensor(member[:, :, :], ge[:, 0:NB, :], ge[:, 1:NB + 1, :], ALU.subtract))
                for b in range(NB):
                    c(v.tensor_tensor_scan(count[:, b, :], ones[:, :], member[:, b, :], 0.0, ALU.mult, ALU.add))
                v.tensor_copy(tot[0:EP, 0, 0:NB], count[:, :, EC - 1]).then_inc(rows, 1)
                c(v.tensor_tensor(blk[:, :], ge[:, 1, :], ge[:, 2, :], ALU.add))
                c(v.tensor_tensor(blk[:, :], blk[:, :], ge[:, 3, :], ALU.add))
                c(v.tensor_tensor(blk[:, :], blk[:, :], ge[:, 4, :], ALU.add))
                c(v.scalar_tensor_tensor(ldst[:, :], blk[:, :], float(-NP), flt[:, 0, :], ALU.mult, ALU.add))
                c(v.scalar_tensor_tensor(field[:, 0, :], flt[:, 1, :], 8.0, flt[:, 2, :], ALU.mult, ALU.add))
                c(v.scalar_tensor_tensor(field[:, 0, :], field[:, 0, :], 128.0, ldst[:, :], ALU.mult, ALU.add))
                c(v.tensor_scalar(field[:, 0, :], field[:, 0, :], 1.0, None, ALU.add))
                dve.wait_ge(prefix, 1)
                c(v.tensor_scalar(tot[:, 1, 0:NB], P[:, 1, 0:NB], float(LANES - 1), None, ALU.add))
                c(v.tensor_copy(toti[:, :], tot[:, 1, 0:NB]))
                c(v.tensor_scalar(toti[:, :], toti[:, :], 7, None, ALU.logical_shift_right))
                c(v.tensor_copy(tot[:, 1, 0:NB], toti[:, :]))
                c(v.tensor_tensor_scan(tot[:, 2, 1:NB + 1], k.ones[:, 0:NB], tot[:, 1, 0:NB], 0.0, ALU.mult, ALU.add))
                c(v.scalar_tensor_tensor(tot[0:EP, 3, 0:NB], tot[0:EP, 2, 0:NB], float(LANES), P[0:EP, 0, 0:NB],
                                         ALU.mult, ALU.add))
                c(v.tensor_scalar(tot[0:EP, 3, 0:NB], tot[0:EP, 3, 0:NB], -1.0, None, ALU.add))
                for b in range(NB):
                    c(v.scalar_tensor_tensor(count[:, b, :], count[:, b, :], tot[0:EP, 3, b:b + 1], member[:, b, :],
                                             ALU.add, ALU.mult))
                c(v.tensor_tensor(pos[:, :], count[:, 0, :], count[:, 1, :], ALU.add))
                for b in range(2, NB):
                    c(v.tensor_tensor(pos[:, :], pos[:, :], count[:, b, :], ALU.add))
                c(v.tensor_copy(posi[:, 0, :], pos[:, :]))
                c(v.tensor_scalar(posi[:, 1, :], posi[:, 0, :], 7, None, ALU.logical_shift_right))
                c(v.tensor_scalar(posi[:, 0, :], posi[:, 0, :], LANES - 1, None, ALU.bitwise_and))
                v.tensor_copy(lane[:, :, :], posi[:, :, :]).then_inc(laned, 1)
                dve.wait_ge(laned, 1)
                c(v.tensor_scalar(tb[:, :], iota[0:1, 0:ET + 2 * AHEAD], tot[0:1, 2, 1:2], None, ALU.is_ge))
                for b in range(2, NB):
                    c(v.scalar_tensor_tensor(tb[:, :], iota[0:1, 0:ET + 2 * AHEAD], tot[0:1, 2, b:b + 1], tb[:, :],
                                             ALU.is_ge, ALU.add))
                fours = lambda j: tb[:, j:j + ET].rearrange("o (i q) -> o i q", q=4)[:, :, 0]
                c(v.tensor_copy(tbw[:, :], fours(0)))
                for j in range(1, 8):
                    c(v.scalar_tensor_tensor(tbw[:, :], fours(j), float(8 ** j), tbw[:, :], ALU.mult, ALU.add))
                v.tensor_copy(k.e_blk[:, :], tbw[:, :]).then_inc(blocks_known, 1)
                with dve.Fori(0, EC // 15) as i:
                    for n in range(15):
                        col, s = i * 15 + n, n % 5
                        dve.wait_ge(put_used[s], i * 3 + n // 5 + 1)
                        v.tensor_scalar(put[s][:, 0, :], iota[0:EP, 0:ET], lane[:, 1, bass.ds(col, 1)],
                                        field[:, 0, bass.ds(col, 1)], ALU.is_equal, ALU.mult)
                        v.tensor_scalar(put[s][:, 1, :], iota[0:EP, 0:ET], lane[:, 1, bass.ds(col, 1)],
                                        field[:, 1, bass.ds(col, 1)], ALU.is_equal,
                                        ALU.mult).then_inc(put_ready[s], 1)
                dve.wait_ge(sorted_, 1)
                c(v.tensor_copy(keyi[:, 0, :], P[:, 0, 0:ET]))
                c(v.tensor_copy(k.e_w[:, :], P[:, 0, ET:2 * ET]))
                c(v.tensor_scalar(keyi[:, 1, :], keyi[:, 0, :], LANES - 1, None, ALU.bitwise_and))
                c(v.tensor_scalar(keyi[:, 2, :], keyi[:, 0, :], 7, None, ALU.logical_shift_right))
                c(v.tensor_scalar(keyi[:, 3, :], keyi[:, 0, :], 10, None, ALU.logical_shift_right))
                c(v.memset(k.e_ldst[:, ET:ET + AHEAD], 0.0))
                c(v.tensor_copy(k.e_ldst[:, 0:ET], keyi[:, 1, :]))
                v.tensor_copy(k.e_src[:, :], keyi[:, 3, :])
                v.tensor_scalar(k.e_ldst[:, :], k.e_ldst[:, :], -1.0, None, ALU.add).then_inc(unpacked, 1)
                v.tensor_copy(k.e_row[:, :], keyi[:, 2, :])
                v.tensor_copy(k.e_srci[:, :], keyi[:, 3, :])
                dve.wait_ge(unpacked, 1)
                with dve.Fori(0, ET // 4) as i:
                    for s in range(4):
                        dve.wait_ge(shot_used[s], i + 1)
                        v.tensor_scalar(shot[s][:, :], iota16[:, :], k.e_src[:, bass.ds(i * 4 + s, 1)], None,
                                        ALU.is_equal).then_inc(shot_ready[s], 1)
                dve.wait_ge(counted, 1)
                for b in range(NB):
                    c(v.tensor_copy(k.C[:, b, 0:4 * NP], P[0:NP, b, 0:4 * NP]))
                c(v.tensor_copy(k.C[:, 0:4, 4 * NP:NODES],
                                P[0:NP, 5, :].rearrange("p (b n) -> p b n", b=4)[:, :, 0:NP]))
                v.tensor_copy(k.C[:, 4, 4 * NP:NODES], P[0:NP, 6, 0:NP]).then_inc(c_ready, 1)
                dve.wait_ge(c_ready, 1)
                c(v.tensor_reduce(k.deg[:, :], k.C[:, :, 0:NODES], AX.X, ALU.add))
                c(v.memset(k.negC[:, NB, :], 0.0))
                c(v.tensor_scalar(k.negC[:, 0:NB, :], k.C[:, :, :], 0.0, NEG, ALU.is_equal, ALU.mult))
                c(v.tensor_copy(k.ident16[:, :], k.const[:, C_ID:C_ID + 128]))
                for j in range(NB):
                    dve.wait_ge(turned, j + 1)
                    q = j % 4
                    v.tensor_copy(k.CT[:, j, 0:4 * NP], P[0:NP, 2 * q, 0:4 * NP])
                    v.tensor_copy(k.CT[:, j, 4 * NP:NODES], P[0:NP, 2 * q + 1, 0:NP]).then_inc(ct_half, 1)

            @block.gpsimd
            def _(pool):
                pool.wait_ge(laned, 1)
                with pool.Fori(0, EC // 15) as i:
                    for g in range(3):
                        pool.wait_ge(lanes_used[g], i + 1)
                        nc.gpsimd.tensor_tensor(
                            hot[g][:, :, :], iota[0:EP, 0:LANES].unsqueeze(1).to_broadcast([EP, 5, LANES]),
                            lane[:, 0, bass.ds(i * 15 + g * 5, 5)].unsqueeze(2).to_broadcast([EP, 5, LANES]),
                            ALU.subtract).then_inc(lanes_far[g], 1)
                pool.wait_ge(unpacked, 1)
                with pool.Fori(0, ET // 8) as i:
                    for g in range(2):
                        pool.wait_ge(dhot_used[g], i + 1)
                        nc.gpsimd.tensor_tensor(
                            dhot[g][:, :, :], iota[:, 0:NP].unsqueeze(1).to_broadcast([LANES, 4, NP]),
                            k.e_ldst[:, bass.ds(i * 8 + g * 4, 4)].unsqueeze(2).to_broadcast([LANES, 4, NP]),
                            ALU.subtract).then_inc(dhot_far[g], 1)

            @block.scalar
            def _(act):

                def one_hot(x, ready, n):
                    nc.scalar.activation(x, x, ACT.Square).then_inc(squared, 1)
                    act.wait_ge(squared, n)
                    nc.scalar.activation(x, x, ACT.Relu, bias=1.0, scale=-1.0).then_inc(ready, 1)

                with act.Fori(0, EC // 15) as i:
                    for g in range(3):
                        act.wait_ge(lanes_far[g], i + 1)
                        one_hot(hot[g][:, :, :], lanes_ready[g], i * 3 + g + 1)
                with act.Fori(0, ET // 8) as i:
                    for g in range(2):
                        act.wait_ge(dhot_far[g], i + 1)
                        one_hot(dhot[g][:, :, :], dhot_ready[g], i * 2 + (EC // 5 + g + 1))

            @block.tensor
            def _(pe):
                t = nc.tensor
                open_slots(pe, *put_used, *lanes_used, *dhot_used, *shot_used)
                pe.wait_ge(rows, 1)
                t.matmul(P[0:EP, 0, 0:NB], k.const[0:EP, C_TRI:C_TRI + EP], tot[0:EP, 0, 0:NB], start=True, stop=True)
                t.matmul(P[:, 1, 0:NB], k.ones[0:EP, 0:128], tot[0:EP, 0, 0:NB], start=True,
                         stop=True).then_inc(prefix, 1)
                pe.wait_ge(put_ready[0], 1)
                t.matmul(P[:, 0, 0:2 * ET], k.zeros[0:1, 0:128], k.zeros[0:1, 0:2 * ET], start=True, stop=False)
                with pe.Fori(0, EC // 15) as i:
                    for n in range(15):
                        s, g = n % 5, n // 5
                        if n % 5 == 0:
                            pe.wait_ge(lanes_ready[g], i + 1)
                        pe.wait_ge(put_ready[s], i * 3 + n // 5 + 1)
                        t.matmul(P[:, 0, 0:2 * ET], hot[g][:, n % 5, :], put[s][:, :, :], start=False, stop=False,
                                 skip_group_check=True).then_inc(put_used[s], 1)
                        if n % 5 == 4:
                            pe.wait_ge(put_used[s], i * 3 + n // 5 + 2)
                            pe.sem_inc(lanes_used[g], 1)
                t.matmul(P[:, 0, 0:2 * ET], k.zeros[0:1, 0:128], k.zeros[0:1, 0:2 * ET], start=False,
                         stop=True).then_inc(sorted_, 1)
                pe.wait_ge(unpacked, 1)
                for b in range(7):
                    t.matmul(P[0:NP, b, :], k.zeros[0:1, 0:NP], k.zeros[0:1, 0:512], start=True, stop=False)
                pe.wait_ge(blocks_known, 1)
                with pe.Fori(0, ET // 8) as i:
                    of = tile_blocks(k, pe, i * 2)
                    for n in range(8):
                        g, s = n // 4, n % 4
                        b = of[n]
                        if s == 0:
                            pe.wait_ge(dhot_ready[g], i + 1)
                        pe.wait_ge(shot_ready[s], i * 2 + g + 1)
                        t.matmul(k.psum_flat[0:NP, bass.ds(b * 512, 4 * NP)], dhot[g][:, s, :], shot[s][:, 0:4 * NP],
                                 start=False, stop=False, skip_group_check=True)
                        t.matmul(k.psum_flat[0:NP, bass.ds(b * 128 + 5 * 512, NP)], dhot[g][:, s, :],
                                 shot[s][:, 4 * NP:NODES], start=False, stop=False,
                                 skip_group_check=True).then_inc(shot_used[s], 1)
                        if s == 3:
                            pe.wait_ge(shot_used[3], i * 2 + g + 2)
                            pe.sem_inc(dhot_used[g], 1)
                for b in range(7):
                    m = t.matmul(P[0:NP, b, :], k.zeros[0:1, 0:NP], k.zeros[0:1, 0:512], start=False, stop=True)
                m.then_inc(counted, 1)
                pe.wait_ge(c_ready, 1)
                for j in range(NB):
                    q = j % 4
                    if j >= 4:
                        pe.wait_ge(ct_half, j - 3)
                    for b in range(NB):
                        m = t.transpose(P[0:NP, 2 * q + b // 4, (b % 4) * NP:(b % 4 + 1) * NP],
                                        k.C[:, b, j * NP:(j + 1) * NP], k.const[0:NP, C_ID:C_ID + NP])
                    m.then_inc(turned, 1)
    k.stack = k.all




def turn(k, pe, src, bank):
    for m in range(KD):
        for b in range(NB):
            last = k.nc.tensor.transpose(k.psum[:, bank + 2 * m + b // 4, (b % 4) * NP:(b % 4 + 1) * NP],
                                         src[:, b, m * 128:(m + 1) * 128], k.const[0:NP, C_ID:C_ID + NP])
    return last


def normalize(k, name, x, xn, xT, rms=False, weight=None, pre=None):
    nc, P = k.nc, k.psum
    with ExitStack() as st:
        k.stack = st
        stats = k.sb(f"{name}_stats", [NP, NB, 6])
        mv = k.sb(f"{name}_mv", [NP, NB, 2])
        rs = k.sb(f"{name}_rs", [NP, 2, NB])
        sq = k.sb(f"{name}_sq", [NP, D])
        step, spread, root, normed, turned = (k.sem(f"{name}_{s}") for s in (
            "step", "var_ready", "root_ready", "normed", "turned"))
        eps = 1e-6 if rms else LN_EPS
        with nc.Block() as block:

            @block.vector
            def _(dve):
                c, v = Chain(dve, step), nc.vector
                if pre is not None:
                    pre(dve, c)
                for b in range(NB):
                    if rms:
                        c(v.tensor_tensor_reduce(out=sq[:, :], in0=x[:, b, :], in1=x[:, b, :], scale=1.0, scalar=0.0,
                                                 op0=ALU.mult, op1=ALU.add, accum_out=mv[:, b, 1:2]))
                    else:
                        c(v.bn_stats(stats[:, b, :], x[:, b, :]))
                        c(v.bn_aggr(mv[:, b, :], stats[:, b, :]))
                v.tensor_scalar(rs[:, 0, :], mv[:, :, 1], 1.0 / D if rms else 1.0, eps, ALU.mult,
                                ALU.add).then_inc(spread, 1)
                dve.wait_ge(root, 1)
                c(v.reciprocal(rs[:, 0, :], rs[:, 1, :]))
                for b in range(NB):
                    if rms:
                        v.tensor_scalar(xn[:, b, :], x[:, b, :], rs[:, 0, b:b + 1], None,
                                        ALU.mult).then_inc(normed, 1)
                    else:
                        v.tensor_scalar(xn[:, b, :], x[:, b, :], mv[:, b, 0:1], rs[:, 0, b:b + 1], ALU.subtract,
                                        ALU.mult).then_inc(normed, 1)

            @block.tensor
            def _(pe):
                pe.wait_ge(normed, NB)
                turn(k, pe, xn, 0).then_inc(turned, 1)

            @block.scalar
            def _(act):
                a = nc.scalar
                act.wait_ge(spread, 1)
                a.activation(rs[:, 1, :], rs[:, 0, :], ACT.Sqrt).then_inc(root, 1)
                act.wait_ge(turned, 1)
                for m in range(KD):
                    scale = 1.0 if weight is None else weight[:, m:m + 1]
                    a.activation(xT[:, m, 0:4 * NP], P[:, 2 * m, 0:4 * NP], ACT.Copy, scale=scale)
                    a.activation(xT[:, m, 4 * NP:NODES], P[:, 2 * m + 1, 0:NP], ACT.Copy, scale=scale)
    k.stack = k.all


def attention(k, name, qT, kT, v, vcols, oT, neg, times, meanwhile=None):
    nc, P = k.nc, k.psum
    H, HD = 4, 64
    SC = HD ** -0.5
    with ExitStack() as st:
        k.stack = st
        qs = k.sb(f"{name}_q_block", [128, 2, KD, NP])
        top = k.sb(f"{name}_top", [NP, 2, 2])
        e = [k.sb(f"{name}_exp{s}", [NP, NC]) for s in range(2)]
        w = [k.sb(f"{name}_weights{s}", [NP, NC]) for s in range(2)]
        wT = [k.sb(f"{name}_weightsT{s}", [NP, NB, NP]) for s in range(2)]
        den = k.sb(f"{name}_den", [NP, 2, 3])
        wT_cleared = k.sem(f"{name}_wT_cleared")
        q_cleared, q_copied, top_ready, exped, weighed, divided, turned, wT_ready, step = (
            k.sem(f"{name}_{s}") for s in ("q_cleared", "q_copied", "top_ready", "exped", "weighed", "divided", "turned",
                                           "wT_ready", "attn_step"))
        scored, mixed, taken = ([k.sem(f"{name}_{n}{s}") for s in range(2)] for n in ("scored", "mixed", "taken"))
        with nc.Block() as block:

            @block.gpsimd
            def _(pool):
                nc.gpsimd.memset(qs[:, :, :, :], 0.0).then_inc(q_cleared, 1)
                pool.wait_ge(q_cleared, 1)
                for a in range(2):
                    nc.gpsimd.tensor_copy(qs[a * HD:(a + 1) * HD, a], qT[a * HD:(a + 1) * HD, :, 0:NP]
                                          ).then_inc(q_copied, 1)
                for d in range(NB):
                    pool.wait_ge(scored[1], d * 2 + 2)
                    for a in range(2):
                        nc.gpsimd.tensor_copy(qs[a * HD:(a + 1) * HD, a],
                                              qT[a * HD:(a + 1) * HD, :, (d + 1) * NP:(d + 2) * NP]
                                              ).then_inc(q_copied, 1)
                    if meanwhile is not None:
                        pool.wait_ge(q_copied, 2 * d + 4)
                        meanwhile(pool, d)

            @block.tensor
            def _(pe):
                t = nc.tensor

                def score(d, h):
                    s = h % 2
                    for half in range(2):
                        t.matmul(P[0:NP, 2 * s + half, 0:HC], qs[:, s, h // 2, :],
                                 kT[:, h // 2, half * HC:(half + 1) * HC], start=True, stop=False)
                        m = t.matmul(P[0:NP, 2 * s + half, 0:HC], k.ident16[0:NP, 0:NP],
                                     neg[:, d, half * HC:(half + 1) * HC], start=False, stop=True)
                    m.then_inc(scored[s], 1)

                def mix(h):
                    s = h % 2
                    for j in range(NB):
                        m = t.matmul(P[s * HD:(s + 1) * HD, 6 + s, 0:NP], v[:, j, vcols[h]:vcols[h] + HD],
                                     wT[s][:, j, :], start=(j == 0), stop=(j == NB - 1))
                    m.then_inc(mixed[s], 1)

                open_slots(pe, mixed[0])
                pe.wait_ge(q_copied, 2)
                score(0, 0)
                score(0, 1)
                pe.wait_ge(wT_cleared, 1)
                with pe.Fori(0, NB) as d:
                    for h in range(H):
                        pe.wait_ge(exped, d * H + h + 1)
                        if h == 2:
                            pe.wait_ge(q_copied, d * 2 + 4)
                        score(d + (h + 2) // H, (h + 2) % H)
                        pe.wait_ge(divided, d * H + h + 1)
                        pe.wait_ge(wT_ready, d * H + h + 1)
                        for j in range(NB):
                            m = t.transpose(P[0:NP, 4 + j // 4, (j % 4) * NP:(j % 4 + 1) * NP],
                                            w[h % 2][:, j * NP:(j + 1) * NP], k.const[0:NP, C_ID:C_ID + NP])
                        m.then_inc(turned, 1)
                        pe.wait_ge(taken[(h + 1) % 2], d * 2 + h // 2 + 1)
                        mix((h + 3) % H)
                pe.wait_ge(wT_ready, NB * H + 1)
                pe.wait_ge(taken[1], 2 * NB + 1)
                mix(3)

            @block.scalar
            def _(act):
                a = nc.scalar

                def exps(u, s):
                    act.wait_ge(top_ready, u + 1)
                    a.activation(e[s][:, :].rearrange("p (a n) -> p a n", a=2), P[0:NP, 2 * s:2 * s + 2, 0:HC],
                                 ACT.Exp, bias=top[:, s, 1:2], scale=SC).then_inc(exped, 1)

                open_slots(act, wT_ready)
                exps(0, 0)
                with act.Fori(0, NB) as d:
                    for h in range(H):
                        exps(d * H + h + 1, (h + 1) % 2)
                        act.wait_ge(turned, d * H + h + 1)
                        act.wait_ge(mixed[h % 2], d * 2 + h // 2 + 1)
                        a.activation(wT[h % 2][:, 0:4, :], P[0:NP, 4, 0:4 * NP].rearrange("p (j n) -> p j n", j=4),
                                     ACT.Copy)
                        a.activation(wT[h % 2][:, 4, :], P[0:NP, 5, 0:NP], ACT.Copy).then_inc(wT_ready, 1)

            @block.vector
            def _(dve):
                vec = nc.vector

                def find_top(j, s, n):
                    dve.wait_ge(scored[s], j + 1)
                    vec.tensor_reduce(top[:, s, 0:1], P[0:NP, 2 * s:2 * s + 2, 0:HC], AX.XY,
                                      ALU.max).then_inc(step, 1)
                    dve.wait_ge(step, n + 1)
                    vec.tensor_scalar(top[:, s, 1:2], top[:, s, 0:1], -SC, None, ALU.mult).then_inc(top_ready, 1)

                def add(block_, h, n):
                    s = h % 2
                    dve.wait_ge(mixed[s], n)
                    at = bass.ds(block_ * NP, NP) if not isinstance(block_, int) else \
                        slice(block_ * NP, block_ * NP + NP)
                    to = oT[s * HD:(s + 1) * HD, h // 2, at]
                    vec.tensor_tensor(to, P[s * HD:(s + 1) * HD, 6 + s, 0:NP], to, ALU.add).then_inc(taken[s], 1)

                vec.memset(wT[1][:, :, :], 0.0).then_inc(wT_cleared, 1)
                open_slots(dve, *taken)
                find_top(0, 0, 0)
                steps = 3
                with dve.Fori(0, NB) as d:
                    for h in range(H):
                        s = h % 2
                        n = d * (H * steps) + (h * steps + 1)
                        dve.wait_ge(exped, d * H + h + 1)
                        vec.scalar_tensor_tensor(w[s][:, :], e[s][:, :], 1.0, times[:, d, :], ALU.mult, ALU.mult,
                                                 accum_out=den[:, s, 0:1]).then_inc(weighed, 1)
                        dve.wait_ge(weighed, d * H + h + 1)
                        vec.tensor_scalar(den[:, s, 1:2], den[:, s, 0:1], 1e-30, None, ALU.max).then_inc(step, 1)
                        dve.wait_ge(step, n + 1)
                        vec.reciprocal(den[:, s, 2:3], den[:, s, 1:2]).then_inc(step, 1)
                        dve.wait_ge(step, n + 2)
                        vec.tensor_scalar(w[s][:, :], w[s][:, :], den[:, s, 2:3], None,
                                          ALU.mult).then_inc(divided, 1)
                        find_top(d * 2 + (h + 1) // 2, 1 - s, n + 2)
                        if h == 0:
                            add(d, 3, d * 2 + 1)
                        else:
                            add(d + 1, h - 1, d * 2 + (h - 1) // 2 + 2)
                add(NB, 3, 2 * NB + 1)
    k.stack = k.all


def conv_project(k, i):
    nc, P = k.nc, k.psum
    name = f"conv{i}"
    loaded, product, copied, values = (k.sem(f"{name}_{s}") for s in ("bias_loaded", "product", "copied", "values"))
    w = k.wconv[:, i, :, :]
    with nc.Block() as block:

        @block.tensor
        def _(pe):
            t = nc.tensor
            pe.wait_ge(k.wconv_loaded, 16 * 12)
            pe.wait_ge(loaded, 16)
            for g in range(6):
                if g >= 4:
                    pe.wait_ge(copied, g - 3)
                for half in range(2):
                    for kk in range(KD):
                        m = t.matmul(P[:, 2 * (g % 4) + half, 0:HC], w[:, kk, g * 128:(g + 1) * 128],
                                     k.xT[:, kk, half * HC:(half + 1) * HC], start=(kk == 0), stop=(kk == KD - 1))
                m.then_inc(product, 1)
            for b in range(NB):
                pe.wait_ge(copied, 4 if b < 4 else 5)
                bank = (4 + b) % 8
                for kk in range(KD):
                    t.matmul(P[0:NP, bank, 0:D], k.xT[:, kk, b * NP:(b + 1) * NP], w[:, kk, 3 * D:4 * D],
                             start=(kk == 0), stop=False)
                t.matmul(P[0:NP, bank, 0:D], k.ones[0:1, 0:NP], k.brow[0:1, 0:D], start=False,
                         stop=True).then_inc(values, 1)

        @block.sync
        def _(sp):
            sp.dma_start(k.brow[0:1, 0:D], k.ins["L0_gnn_bv"][i:i + 1]).then_inc(loaded, 16)

        @block.scalar
        def _(act):
            for g in range(6):
                act.wait_ge(product, g + 1)
                to = (k.qT, k.kT, k.oT)[g // KD][:, g % KD, 0:NC]
                nc.scalar.activation(to.rearrange("p (a n) -> p a n", a=2), P[:, 2 * (g % 4):2 * (g % 4) + 2, 0:HC],
                                     ACT.Identity, bias=col(k, "conv_bias", 6 * i + g)).then_inc(copied, 1)

        @block.vector
        def _(dve):
            for b in range(NB):
                dve.wait_ge(values, b + 1)
                nc.vector.tensor_copy(k.v[:, b, :], P[0:NP, (4 + b) % 8, 0:D])


def batch_norm(k, i):
    nc, P = k.nc, k.psum
    name = f"bn{i}"
    with ExitStack() as st:
        k.stack = st
        stats = k.sb(f"{name}_stats", [128, KD, 2, 6])
        mv = k.sb(f"{name}_mv", [128, KD, 2])
        f = k.sb(f"{name}_f", [128, 4, KD])
        spread, root, step, ready = (k.sem(f"{name}_{s}") for s in (
            "var_ready", "root_ready", "step", "affine_ready"))
        with nc.Block() as block:

            @block.vector
            def _(dve):
                c, v = Chain(dve, step), nc.vector
                for m in range(KD):
                    v.bn_stats(stats[:, m, 0, :], k.oT[:, m, 0:HC])
                    c(v.bn_stats(stats[:, m, 1, :], k.oT[:, m, HC:NODES]))
                    c(v.bn_aggr(mv[:, m, :], stats[:, m, :, :]))
                v.tensor_scalar(f[:, 0, :], mv[:, :, 1], LN_EPS, None, ALU.add).then_inc(spread, 1)
                dve.wait_ge(root, 1)
                c(v.reciprocal(f[:, 2, :], f[:, 1, :]))
                c(v.tensor_tensor(f[:, 2, :], f[:, 2, :], col(k, "bn_gamma", KD * i, KD), ALU.mult))
                c(v.tensor_tensor(f[:, 3, :], f[:, 2, :], mv[:, :, 0], ALU.mult))
                v.tensor_tensor(f[:, 3, :], col(k, "bn_beta", KD * i, KD), f[:, 3, :], ALU.subtract).then_inc(ready, 1)

            @block.scalar
            def _(act):
                a = nc.scalar
                act.wait_ge(spread, 1)
                a.activation(f[:, 1, :], f[:, 0, :], ACT.Sqrt).then_inc(root, 1)
                act.wait_ge(ready, 1)
                for m in range(KD):
                    a.activation(k.xT[:, m, 0:NODES], k.oT[:, m, 0:NODES], ACT.Relu, bias=f[:, 3, m:m + 1],
                                 scale=f[:, 2, m:m + 1])
    k.stack = k.all


def conv_layers(k):
    normalize(k, "ln_conv", k.x, k.xn, k.xT)
    mixed = k.sem("conv_basis_mixed")
    st = ExitStack()
    term = st.enter_context(k.nc.sbuf_tensor("conv_basis_term", [128, RELS // 2, D], F32))

    def step(a, half, b, add):
        w = k.rgcn_w0[:, a, half * RELS // 2:(half + 1) * RELS // 2, :]
        if add:
            return k.nc.gpsimd.tensor_tensor(w, w, term[:, :, :], ALU.add)
        base = k.basis[:, b, a, :].unsqueeze(1).to_broadcast([128, RELS // 2, D])
        factor = k.coeff[:, 0, :].rearrange("p (r b) -> p r b", b=RELS)[:, half * RELS // 2:(half + 1) * RELS // 2, b]
        return k.nc.gpsimd.tensor_tensor(w if b == 0 else term[:, :, :], base,
                                         factor.unsqueeze(2).to_broadcast([128, RELS // 2, D]), ALU.mult)

    steps = [(a, half, b, add) for a in range(KD) for half in range(2) for b in range(RELS)
             for add in range(2) if b or not add]
    share = -(-len(steps) // (2 * NB))

    def mix(pool, d):
        if d == 0:
            pool.wait_ge(k.basis_loaded, BASIS_LOADS)
        for n in range((i - 1) * NB * share + d * share, min((i - 1) * NB * share + (d + 1) * share, len(steps))):
            step(*steps[n]).then_inc(mixed, 1)
            pool.wait_ge(mixed, n + 1)

    for i in range(3):
        conv_project(k, i)
        attention(k, f"conv{i}", k.qT, k.kT, k.v, [0, 64, 128, 192], k.oT_padded, k.negC, k.C, mix if i else None)
        if i < 2:
            batch_norm(k, i)
    st.close()
    turned = k.sem("conv_out_turned")
    with k.nc.Block() as block:

        @block.tensor
        def _(pe):
            for b in range(NB):
                for m in range(KD):
                    ins = k.nc.tensor.transpose(k.psum[0:NP, b, m * 128:(m + 1) * 128],
                                                k.oT[:, m, b * NP:(b + 1) * NP], k.const[:, C_ID:C_ID + 128])
                ins.then_inc(turned, 1)

        @block.vector
        def _(dve):
            for b in range(NB):
                dve.wait_ge(turned, b + 1)
                k.nc.vector.tensor_tensor(k.x[:, b, :], k.x[:, b, :], k.psum[0:NP, b, 0:D], ALU.add)


def add_to_x(k, name, what):
    done = k.sem(f"{name}_added")
    with k.nc.Block() as block:

        @block.vector
        def _(dve):
            k.nc.vector.tensor_tensor(k.x[:, :, :], k.x[:, :, :], what[:, :, :], ALU.add).then_inc(done, 1)


def softmax8(k, c, v, p, small, exp_to, exp_done, exp_wait):
    n = p.shape[1]
    wide = lambda s: s.unsqueeze(2).to_broadcast([NP, n, EXPERTS])
    c(v.tensor_reduce(small[:, 0, :], p, AX.X, ALU.max))
    v.tensor_tensor(p, p, wide(small[:, 0, :]), ALU.subtract).then_inc(exp_to, 1)
    c.eng.wait_ge(exp_done, exp_wait)
    c(v.tensor_reduce(small[:, 0, :], p, AX.X, ALU.add))
    c(v.reciprocal(small[:, 1, :], small[:, 0, :]))
    c(v.tensor_tensor(p, p, wide(small[:, 1, :]), ALU.mult))


def rank8(k, c, v, p, rank, pair, tie):
    n = p.shape[1]
    tri = k.const[0:NP, C_RANK:C_ROW].rearrange("p (e f) -> p e f", e=EXPERTS)
    for i in range(n):
        mine = p[:, i, :].unsqueeze(2).to_broadcast([NP, EXPERTS, EXPERTS])
        other = p[:, i, :].unsqueeze(1).to_broadcast([NP, EXPERTS, EXPERTS])
        c(v.tensor_tensor(tie[:, i], other, mine, ALU.is_equal))
        c(v.tensor_tensor(tie[:, i], tie[:, i], tri, ALU.mult))
        c(v.tensor_tensor(pair[:, i], other, mine, ALU.is_gt))
        c(v.tensor_tensor(pair[:, i], pair[:, i], tie[:, i], ALU.add))
    c(v.tensor_reduce(rank, pair[:, :, :, :], AX.X, ALU.add))


def route(k, name, xT, tiles, router, bias, top, floor):
    nc, P = k.nc, k.psum
    with ExitStack() as st:
        k.stack = st
        small = k.sb(f"{name}_small", [NP, 2, NB])
        rank = k.sb(f"{name}_rank", [NP, NB, EXPERTS])
        pair = k.sb(f"{name}_pair", [NP, NB, EXPERTS, EXPERTS])
        tie = k.sb(f"{name}_tie", [NP, NB, EXPERTS, EXPERTS])
        brow = k.sb(f"{name}_bias", [1, EXPERTS])
        loaded, logits, step, to_exp, exped = (k.sem(f"{name}_{s}") for s in (
            "bias_loaded", "logits", "step", "to_exp", "exped"))
        g = k.gate
        with nc.Block() as block:

            @block.sync
            def _(sp):
                if bias is not None:
                    sp.dma_start(brow[:, :], k.ins[bias].rearrange("(a n) -> a n", a=1)).then_inc(loaded, 16)

            @block.tensor
            def _(pe):
                t = nc.tensor
                if bias is not None:
                    pe.wait_ge(loaded, 16)
                for b in range(NB):
                    for kk in range(tiles):
                        m = t.matmul(P[0:NP, 0, b * EXPERTS:(b + 1) * EXPERTS], xT[:, kk, b * NP:(b + 1) * NP],
                                     col(k, router, kk * EXPERTS, EXPERTS), start=(kk == 0),
                                     stop=(kk == tiles - 1 and bias is None))
                    if bias is not None:
                        m = t.matmul(P[0:NP, 0, b * EXPERTS:(b + 1) * EXPERTS], k.ones[0:1, 0:NP], brow[:, :],
                                     start=False, stop=True)
                m.then_inc(logits, 1)

            @block.scalar
            def _(act):
                act.wait_ge(to_exp, 1)
                nc.scalar.activation(g[:, :, :], g[:, :, :], ACT.Exp).then_inc(exped, 1)

            @block.vector
            def _(dve):
                c, v = Chain(dve, step), nc.vector
                dve.wait_ge(logits, 1)
                c(v.tensor_copy(g[:, :, :], P[0:NP, 0, 0:NB * EXPERTS].rearrange("p (b e) -> p b e", b=NB)))
                softmax8(k, c, v, g[:, :, :], small, to_exp, exped, 1)
                rank8(k, c, v, g, rank[:, :, :], pair, tie)
                c(v.tensor_scalar(rank[:, :, :], rank[:, :, :], float(top), None, ALU.is_lt))
                c(v.tensor_tensor(g[:, :, :], g[:, :, :], rank[:, :, :], ALU.mult))
                if floor is not None:
                    c(v.tensor_reduce(small[:, 0, :], g[:, :, :], AX.X, ALU.add))
                    c(v.tensor_scalar(small[:, 0, :], small[:, 0, :], floor, None, ALU.add))
                    c(v.reciprocal(small[:, 1, :], small[:, 0, :]))
                    c(v.tensor_tensor(g[:, :, :], g[:, :, :],
                                      small[:, 1, :].unsqueeze(2).to_broadcast([NP, NB, EXPERTS]), ALU.mult))
    k.stack = k.all


def down(k, pe, hT, w, brow, tiles, rows, i, s, given, taken):
    P, t = k.psum, k.nc.tensor
    for b in range(NB):
        q = (NB * s + b) % 2
        pe.wait_ge(taken[q], i * NB + ((NB * s + b) // 2 + 1))
        for kk in range(tiles):
            m = t.matmul(P[0:NP, 6 + q, 0:D], hT[0:rows, kk, b * NP:(b + 1) * NP], w[0:rows, kk, :],
                         start=(kk == 0), stop=(brow is None and kk == tiles - 1))
        if brow is not None:
            m = t.matmul(P[0:NP, 6 + q, 0:D], k.ones[0:1, 0:NP], brow, start=False, stop=True)
        m.then_inc(given[q], 1)


def gather_outputs(k, dve, acc, i, s, given, taken):
    for b in range(NB):
        q = (NB * s + b) % 2
        dve.wait_ge(given[q], i * NB + (NB * s + b) // 2 + 1)
        k.nc.vector.scalar_tensor_tensor(acc[:, b, :], k.psum[0:NP, 6 + q, 0:D],
                                         k.gate[:, b, bass.ds(i * 2 + s, 1)], acc[:, b, :], ALU.mult,
                                         ALU.add).then_inc(taken[q], 1)


def experts_gelu(k, name, w1_of, w2_of, b2_of, tiles, pairs, b1, affine, acc, before=None):
    nc, P = k.nc, k.psum
    hidden = tiles * 128
    with ExitStack() as st:
        k.stack = st
        w1 = [k.sb(f"{name}_w1_{s}", [128, KD, hidden]) for s in range(2)]
        w2 = [k.sb(f"{name}_w2_{s}", [128, tiles, D]) for s in range(2)]
        b2 = [k.sb(f"{name}_b2_{s}", [1, D]) for s in range(2)]
        xe = [k.sb(f"{name}_x_{s}", [128, KD, NC]) if affine else k.xT for s in range(2)]
        hT = k.sb(f"{name}_hT", [128, tiles, NC])
        two = lambda n: [k.sem(f"{name}_{n}{s}") for s in range(2)]
        w1_loaded, w2_loaded, w1_used, w2_used, x_ready, up_given, up_taken, given, taken = (two(n) for n in (
            "w1_loaded", "w2_loaded", "w1_used", "w2_used", "x_ready", "up_given", "up_taken", "down_given",
            "down_taken"))
        cleared = k.sem(f"{name}_cleared")
        half = tiles // 2
        with nc.Block() as block:

            @block.sync
            def _(sp):
                if before is not None:
                    before(sp)
                with sp.Fori(0, pairs) as i:
                    for s in range(2):
                        e = i * 2 + s
                        sp.wait_ge(w1_used[s], i + 1)
                        sp.dma_start(w1[s][:, :, :], w1_of(sp, e)).then_inc(w1_loaded[s], 16)
                        sp.wait_ge(w2_used[s], i + 1)
                        sp.dma_start(w2[s][:, :, :], w2_of(sp, e)).then_inc(w2_loaded[s], 16)
                        sp.dma_start(b2[s][:, :], b2_of(sp, e)).then_inc(w2_loaded[s], 16)

            @block.tensor
            def _(pe):
                t = nc.tensor
                open_slots(pe, *w1_used, *w2_used)
                with pe.Fori(0, pairs) as i:
                    for s in range(2):
                        pe.wait_ge(w1_loaded[s], i * 16 + 16)
                        if affine:
                            pe.wait_ge(x_ready[s], i + 1)
                        for m in range(tiles):
                            q = m % 2
                            pe.wait_ge(up_taken[q], (i * 2 + s) * half + (m // 2 + 1))
                            for a in range(2):
                                for kk in range(KD):
                                    ins = t.matmul(P[:, 2 * q + a, 0:HC], w1[s][:, kk, m * 128:(m + 1) * 128],
                                                   xe[s][:, kk, a * HC:(a + 1) * HC], start=(kk == 0),
                                                   stop=(kk == KD - 1))
                            ins.then_inc(up_given[q], 1)
                        t.matmul(P[:, 5, 0:1], k.zeros[0:1, 0:128], k.zeros[0:1, 0:1], start=True,
                                 stop=True).then_inc(w1_used[s], 1)
                        for q in range(2):
                            pe.wait_ge(up_taken[q], (i * 2 + s + 1) * half + 1)
                        pe.wait_ge(w2_loaded[s], i * 32 + 32)
                        down(k, pe, hT, w2[s], b2[s][:, :], tiles, 128, i, s, given, taken)
                        t.matmul(P[:, 5, 0:1], k.zeros[0:1, 0:128], k.zeros[0:1, 0:1], start=True,
                                 stop=True).then_inc(w2_used[s], 1)

            @block.scalar
            def _(act):
                open_slots(act, *up_taken)
                with act.Fori(0, pairs) as i:
                    for s in range(2):
                        for m in range(tiles):
                            act.wait_ge(up_given[m % 2], (i * 2 + s) * half + m // 2 + 1)
                            nc.scalar.activation(hT[:, m, :].rearrange("p (a n) -> p a n", a=2),
                                                 P[:, 2 * (m % 2):2 * (m % 2) + 2, 0:HC], ACT.Gelu,
                                                 bias=b1(i * 2 + s, m)).then_inc(up_taken[m % 2], 1)

            @block.vector
            def _(dve):
                v = nc.vector

                def make_x(e, s):
                    for kk in range(KD):
                        ins = v.tensor_scalar(xe[s][:, kk, :], k.xT[:, kk, :],
                                              col(k, affine[0], e + kk * (EXPERTS + 1)),
                                              col(k, affine[1], e + kk * (EXPERTS + 1)), ALU.mult, ALU.add)
                    ins.then_inc(x_ready[s], 1)

                open_slots(dve, *taken)
                v.memset(acc[:, :, :], 0.0).then_inc(cleared, 1)
                dve.wait_ge(cleared, 1)
                if affine:
                    make_x(0, 0)
                with dve.Fori(0, pairs) as i:
                    for s in range(2):
                        if affine:
                            dve.wait_ge(w1_used[1 - s], i + (s + 1))
                            make_x(i * 2 + s + 1, 1 - s)
                        gather_outputs(k, dve, acc, i, s, given, taken)
    k.stack = k.all


def moe0(k):
    normalize(k, "ln_moe0", k.x, k.xn, k.xT)
    route(k, "moe0_route", k.xT, KD, "moe0_router", "L0_ffn_br", 2, 0.0)
    normalize(k, "ln_moe0_inner", k.xn, k.xn, k.xT)
    experts_gelu(k, "moe0",
                 lambda sp, e: k.ins["L0_ffn_W1"][bass.ds(e, 1)].rearrange("o (a p) n -> p (o a) n", p=128),
                 lambda sp, e: k.ins["L0_ffn_W2"][bass.ds(e, 1)].rearrange("o (a p) n -> p (o a) n", p=128),
                 lambda sp, e: k.ins["L0_ffn_b2"][bass.ds(e, 1), :],
                 8, EXPERTS // 2, lambda e, m: col(k, "moe0_b1", e * 8 + m), ("moe0_ln_g", "moe0_ln_b"), k.o)
    add_to_x(k, "moe0", k.o)


def sage(k):
    nc, P = k.nc, k.psum
    normalize(k, "ln_sage", k.x, k.xn, k.xT)
    with ExitStack() as st:
        k.stack = st
        w = k.sb("sage_w", [128, 2, KD, D])
        brow = k.sb("sage_b", [1, D])
        aggT = k.sb("sage_aggT", [128, KD, NC])
        rdeg = k.sb("sage_rdeg", [NP, 2, NB])
        z = k.sb("sage_z", [NP, NB, D])
        loaded, agg, agg_ready, own, neigh, step = (k.sem(f"sage_{s}") for s in (
            "loaded", "agg", "agg_copied", "own_products", "neighbour_products", "step"))
        with nc.Block() as block:

            @block.sync
            def _(sp):
                for n, m in enumerate(("W_self", "W_neigh")):
                    sp.dma_start(w[:, n], k.ins[f"L1_gnn_{m}"].rearrange("(a p) n -> p a n", p=128)
                                 ).then_inc(loaded, 16)
                sp.dma_start(brow[:, :], k.ins["L1_gnn_b"].rearrange("(a n) -> a n", a=1)).then_inc(loaded, 16)

            @block.tensor
            def _(pe):
                t = nc.tensor
                for m in range(KD):
                    for a in range(2):
                        for j in range(NB):
                            ins = t.matmul(P[:, 2 * m + a, 0:HC], k.xn[:, j, m * 128:(m + 1) * 128],
                                           k.CT[:, j, a * HC:(a + 1) * HC], start=(j == 0), stop=(j == NB - 1))
                    ins.then_inc(agg, 1)
                pe.wait_ge(loaded, 16 * 3)
                for b in range(NB):
                    q = b % 2
                    if b >= 2:
                        pe.wait_ge(step, b - 1)
                    for kk in range(KD):
                        t.matmul(P[0:NP, 4 + q, 0:D], k.xT[:, kk, b * NP:(b + 1) * NP], w[:, 0, kk, :],
                                 start=(kk == 0), stop=False)
                    t.matmul(P[0:NP, 4 + q, 0:D], k.ones[0:1, 0:NP], brow[:, :], start=False,
                             stop=True).then_inc(own, 1)
                    pe.wait_ge(agg_ready, KD)
                    for kk in range(KD):
                        ins = t.matmul(P[0:NP, 6 + q, 0:D], aggT[:, kk, b * NP:(b + 1) * NP], w[:, 1, kk, :],
                                       start=(kk == 0), stop=(kk == KD - 1))
                    ins.then_inc(neigh, 1)

            @block.scalar
            def _(act):
                for m in range(KD):
                    act.wait_ge(agg, m + 1)
                    nc.scalar.activation(aggT[:, m, :].rearrange("p (a n) -> p a n", a=2),
                                         P[:, 2 * m:2 * m + 2, 0:HC], ACT.Copy).then_inc(agg_ready, 1)

            @block.vector
            def _(dve):
                v = nc.vector
                c = Chain(dve, k.sem("sage_chain"))
                c(v.tensor_scalar(rdeg[:, 0, :], k.deg[:, :], 1.0, None, ALU.max))
                c(v.reciprocal(rdeg[:, 1, :], rdeg[:, 0, :]))
                for b in range(NB):
                    dve.wait_ge(neigh, b + 1)
                    dve.wait_ge(own, b + 1)
                    c(v.tensor_scalar(z[:, b, :], P[0:NP, 6 + b % 2, 0:D], rdeg[:, 1, b:b + 1], None, ALU.mult))
                    v.tensor_tensor(z[:, b, :], z[:, b, :], P[0:NP, 4 + b % 2, 0:D], ALU.add).then_inc(step, 1)
                    dve.wait_ge(step, b + 1)
                    v.scalar_tensor_tensor(k.x[:, b, :], z[:, b, :], 0.0, k.x[:, b, :], ALU.max, ALU.add)
    k.stack = k.all


def route_graph(k):
    nc, P = k.nc, k.psum
    CAPACITY = -(-NODES * 5 // (4 * EXPERTS))
    with ExitStack() as st:
        k.stack = st
        mean = k.sb("moe1_mean", [128, KD])
        means = k.sb("moe1_means", [128, KD, NP])
        p = k.sb("moe1_p", [NP, 1, EXPERTS])
        f = k.sb("moe1_f", [NP, 1, EXPERTS])
        small = k.sb("moe1_small", [NP, 2, 1])
        rank = k.sb("moe1_rank", [NP, 1, EXPERTS])
        pair = k.sb("moe1_pair", [NP, 1, EXPERTS, EXPERTS])
        tie = k.sb("moe1_tie", [NP, 1, EXPERTS, EXPERTS])
        pick = k.sb("moe1_pick", [NP, EXPERTS])
        junk = k.sb("moe1_junk", [NP, EXPERTS])
        val = k.sb("moe1_val", [NP, 6])
        brow = k.sb("moe1_brow", [1, EXPERTS])
        loaded, mean_ready, logits, step, to_exp, exped, picked, bias_loaded = (k.sem(f"moe1_{s}") for s in (
            "loaded", "mean_ready", "logits", "step", "to_exp", "exped", "picked", "picked_bias_loaded"))
        with nc.Block() as block:

            @block.sync
            def _(sp):
                sp.dma_start(brow[:, :], k.ins["L1_ffn_br"].rearrange("(a n) -> a n", a=1)).then_inc(loaded, 16)
                sp.wait_ge(picked, 1)
                for s in range(2):
                    e = sp.value_load(k.picked[0:1, s:s + 1], min_val=0, max_val=EXPERTS - 1)
                    sp.dma_start(k.picked_b1[:, s * 4:(s + 1) * 4],
                                 k.ins["moe1_b1"][bass.ds(e, 1)].rearrange("o p m -> p (o m)")
                                 ).then_inc(bias_loaded, 16)
                sp.wait_ge(bias_loaded, 32)

            @block.tensor
            def _(pe):
                t = nc.tensor
                pe.wait_ge(mean_ready, 1)
                pe.wait_ge(loaded, 16)
                for kk in range(KD):
                    t.matmul(P[0:NP, 0, 0:EXPERTS], means[:, kk, :], col(k, "moe1_router", kk * EXPERTS, EXPERTS),
                             start=(kk == 0), stop=False)
                t.matmul(P[0:NP, 0, 0:EXPERTS], k.ones[0:1, 0:NP], brow[:, :], start=False,
                         stop=True).then_inc(logits, 1)

            @block.scalar
            def _(act):
                a = nc.scalar
                for n in range(2):
                    act.wait_ge(to_exp, n + 1)
                    a.activation(p[:, 0, :], p[:, 0, :], ACT.Exp).then_inc(exped, 1)
                act.wait_ge(to_exp, 3)
                a.activation(val[:, 3:4], val[:, 2:3], ACT.Exp).then_inc(exped, 1)

            @block.vector
            def _(dve):
                c, v = Chain(dve, step), nc.vector
                c(v.tensor_reduce(mean[:, :], k.xT[:, :, 0:NODES], AX.X, ALU.add))
                c(v.tensor_scalar(mean[:, :], mean[:, :], 1.0 / NODES, None, ALU.mult))
                for kk in range(KD):
                    ins = v.tensor_scalar(means[:, kk, :], k.ones[:, 0:NP], mean[:, kk:kk + 1], None, ALU.mult)
                    c(ins)
                v.memset(junk[:, :], 0.0).then_inc(mean_ready, 1)
                dve.wait_ge(mean_ready, 1)
                dve.wait_ge(logits, 1)
                c(v.tensor_copy(p[:, 0, :], P[0:NP, 0, 0:EXPERTS]))
                softmax8(k, c, v, p[:, :, :], small, to_exp, exped, 1)
                c(v.tensor_scalar(f[:, 0, :], p[:, 0, :], float(NODES), 1e-30, ALU.mult, ALU.max))
                c(v.reciprocal(f[:, 0, :], f[:, 0, :]))
                c(v.tensor_scalar(f[:, 0, :], f[:, 0, :], float(CAPACITY), 1.0, ALU.mult, ALU.min))
                c(v.tensor_tensor(p[:, 0, :], p[:, 0, :], f[:, 0, :], ALU.mult))
                softmax8(k, c, v, p[:, :, :], small, to_exp, exped, 2)
                rank8(k, c, v, p, rank[:, :, :], pair, tie)
                for s in range(2):
                    c(v.tensor_scalar(pick[:, :], rank[:, 0, :], float(s), None, ALU.is_equal))
                    for n, what in enumerate((p[:, 0, :], k.const[0:NP, C_IOTA:C_IOTA + EXPERTS])):
                        c(v.tensor_tensor(junk[:, :], pick[:, :], what, ALU.mult))
                        c(v.tensor_reduce(val[:, s + 4 * n:s + 4 * n + 1], junk[:, :], AX.X, ALU.add))
                v.tensor_copy(k.picked[0:1, :], val[0:1, 4:6]).then_inc(picked, 1)
                v.tensor_tensor(val[:, 2:3], val[:, 1:2], val[:, 0:1], ALU.subtract).then_inc(to_exp, 1)
                dve.wait_ge(exped, 3)
                c(v.tensor_scalar(val[:, 2:3], val[:, 3:4], 1.0, None, ALU.add))
                c(v.reciprocal(val[:, 0:1], val[:, 2:3]))
                c(v.tensor_tensor(val[:, 1:2], val[:, 3:4], val[:, 0:1], ALU.mult))
                c(v.tensor_copy(k.gate[:, :, 0:2], val[:, 0:2].unsqueeze(1).to_broadcast([NP, NB, 2])))
    k.stack = k.all


def moe1(k):
    nc = k.nc
    normalize(k, "ln_moe1", k.x, k.xn, k.xT)
    route_graph(k)
    hidden = 4

    def expert(sp, e):
        return sp.value_load(k.picked[0:1, bass.ds(e, 1)], min_val=0, max_val=EXPERTS - 1)

    experts_gelu(k, "moe1",
                 lambda sp, e: k.ins["L1_ffn_W1"][bass.ds(expert(sp, e), 1)].rearrange("o (a p) n -> p (o a) n", p=128),
                 lambda sp, e: k.ins["L1_ffn_W2"][bass.ds(expert(sp, e), 1)].rearrange("o (a p) n -> p (o a) n", p=128),
                 lambda sp, e: k.ins["L1_ffn_b2"][bass.ds(expert(sp, e), 1), :],
                 hidden, 1, lambda e, m: k.picked_b1[:, bass.ds(e * hidden + m, 1)], None, k.o)

    def add_tokens(dve, c):
        c(nc.vector.tensor_tensor(k.o[:, :, :], k.o[:, :, :], k.xn[:, :, :], ALU.add))

    normalize(k, "ln_moe1_out", k.o, k.o, k.xT, pre=add_tokens)
    with ExitStack() as st:
        k.stack = st
        par = k.sb("moe1_par", [NP, 2, D])
        loaded, step = k.sem("moe1_par_loaded"), k.sem("moe1_out_step")
        with nc.Block() as block:

            @block.sync
            def _(sp):
                sp.dma_start(par[:, 0, :], k.ins["moe1_gamma"]).then_inc(loaded, 16)
                sp.dma_start(par[:, 1, :], k.ins["moe1_beta"]).then_inc(loaded, 16)

            @block.vector
            def _(dve):
                c, v = Chain(dve, step), nc.vector
                wide = lambda n: par[:, n, :].unsqueeze(1).to_broadcast([NP, NB, D])
                dve.wait_ge(loaded, 32)
                c(v.tensor_tensor(k.o[:, :, :], k.o[:, :, :], wide(0), ALU.mult))
                c(v.tensor_tensor(k.o[:, :, :], k.o[:, :, :], wide(1), ALU.add))
                c(v.tensor_tensor(k.x[:, :, :], k.x[:, :, :], k.o[:, :, :], ALU.add))
    k.stack = k.all


def gather_tiles(k, pool, index, idx, idx_ready, idx_seen, free, rows, table, gathered):
    with pool.Fori(0, ET // 8) as i:
        for g in range(2):
            nc = k.nc
            nc.gpsimd.tensor_copy(idx[g][:, :], index[:, bass.ds(i * 8 + g * 4, 4)]).then_inc(idx_ready, 1)
            pool.wait_ge(idx_ready, i * 2 + g + 1)
            for s in range(4):
                pool.wait_ge(free[s], i * 2 + g + 1)
                pool.sem_inc(idx_seen, 1)
                nc.gpsimd.indirect_dma_start(
                    out=rows[s][:, :], out_offset=None, in_=table,
                    in_offset=bass.IndirectOffsetOnAxis(ap=idx[g][:, s:s + 1], axis=0)).then_inc(gathered[s], 16)


def rgcn_layer(k, l, w1):
    nc, P = k.nc, k.psum
    name = f"rgcn{l}"
    with ExitStack() as st:
        k.stack = st
        w = (k.rgcn_w0, w1)[l]
        ah = [k.sb(f"{name}_all_h{s}", [NP, RELS * D]) for s in range(2)]
        brow = k.sb(f"{name}_bias", [1, 2 * D])
        idx = [k.sb(f"{name}_idx{s}", [LANES, 4], U32) for s in range(2)]
        rows = [k.sb(f"{name}_rows{s}", [LANES, D]) for s in range(4)]
        hot = [k.sb(f"{name}_hot{s}", [LANES, NP]) for s in range(4)]
        loaded, mixed, products, copied, whole = (k.sem(f"{name}_{s}") for s in (
            "loaded", "basis_mixed", "products", "copied", "summed"))
        idx_ready, idx_seen = k.sem(f"{name}_idx_ready"), k.sem(f"{name}_idx_seen")
        stored = [k.sem(f"{name}_stored{s}") for s in range(2)]
        four = lambda n: [k.sem(f"{name}_{n}{s}") for s in range(4)]
        gathered, hot_ready, used = (four(n) for n in ("gathered", "hot_ready", "used"))
        table = k.tables[:, 0:RELS * D]
        with nc.Block() as block:

            @block.sync
            def _(sp):
                sp.dma_start(brow[0:1, 0:D], k.ins["L2_gnn_bias"][l:l + 1]).then_inc(loaded, 16)
                sp.dma_start(brow[0:1, D:2 * D], k.ins["L2_gnn_bias"][l:l + 1]).then_inc(loaded, 16)
                if l == 0:
                    load_basis(k, sp, 1)
                for b in range(NB):
                    sp.wait_ge(copied, 4 * (b + 1))
                    sp.dma_start(table[b * NP:(b + 1) * NP, :], ah[b % 2][:, :]).then_inc(stored[b % 2], 16)

            @block.gpsimd
            def _(pool):
                pool.wait_ge(stored[0], 16 * 3)
                pool.wait_ge(stored[1], 16 * 2)
                gather_tiles(k, pool, k.e_row, idx, idx_ready, idx_seen, used, rows, k.table_rows, gathered)

            @block.vector
            def _(dve):
                v = nc.vector
                for b in range(NB):
                    if b >= 2:
                        dve.wait_ge(stored[b % 2], 16 * (b // 2))
                    for q in range(4):
                        dve.wait_ge(products, 4 * b + q + 1)
                        v.tensor_copy(ah[b % 2][:, q * 2 * D:(q + 1) * 2 * D], P[0:NP, q, :]).then_inc(copied, 1)

                def onehots(i):
                    for s in range(4):
                        at = bass.ds(i * 4 + s, 1)
                        dve.wait_ge(used[s], i + 1)
                        v.tensor_scalar(hot[s][:, :], k.const[:, C_IOTA:C_IOTA + NP], k.e_ldst[:, at],
                                        k.e_w[:, at], ALU.is_equal, ALU.mult).then_inc(hot_ready[s], 1)

                beside = 4 * RELS if l == 0 else 0
                if l == 0:
                    dve.wait_ge(k.basis_loaded, BASIS_LOADS + 16 * RELS)
                    with dve.Fori(0, RELS) as r:
                        for q in range(4):
                            onehots(r * 4 + q)
                            for b in range(2 * q, 2 * q + 2):
                                mix_basis(k, v, w1, 1, r, b).then_inc(mixed, 1)
                                dve.wait_ge(mixed, r * RELS + b + 1)
                with dve.Fori(beside, ET // 4) as i:
                    onehots(i)
                dve.wait_ge(whole, 1)
                for b in range(NB):
                    sums = P[0:NP, 4 + b // 2, (b % 2) * D:(b % 2 + 1) * D]
                    if l == 0:
                        v.tensor_scalar(k.o[:, b, :], sums, 0.0, None, ALU.max)
                    else:
                        v.tensor_tensor(k.x[:, b, :], k.x[:, b, :], sums, ALU.add)

            @block.tensor
            def _(pe):
                t = nc.tensor
                open_slots(pe, *used)
                for b in range(NB):
                    for q in range(4):
                        if b:
                            pe.wait_ge(copied, 4 * (b - 1) + q + 1)
                        for kk in range(KD):
                            m = t.matmul(P[0:NP, q, :], k.xT[:, kk, b * NP:(b + 1) * NP],
                                         w[:, kk, 2 * q:2 * q + 2, :], start=(kk == 0), stop=(kk == KD - 1))
                        m.then_inc(products, 1)
                pe.wait_ge(loaded, 32)
                for q in range(3):
                    t.matmul(P[0:NP, 4 + q, :], k.ones[0:1, 0:NP], brow[0:1, :], start=True, stop=False)
                with pe.Fori(0, ET // 4) as i:
                    of = tile_blocks(k, pe, i)
                    for s in range(4):
                        b = of[s]
                        pe.wait_ge(hot_ready[s], i + 1)
                        pe.wait_ge(gathered[s], i * 16 + 16)
                        t.matmul(k.psum_flat[0:NP, bass.ds(b * D + 4 * 512, D)], hot[s][:, :], rows[s][:, :],
                                 start=False, stop=False, skip_group_check=True).then_inc(used[s], 1)
                for q in range(3):
                    m = t.matmul(P[0:NP, 4 + q, :], k.zeros[0:1, 0:NP], k.zeros[0:1, 0:512], start=False, stop=True)
                m.then_inc(whole, 1)
    k.stack = k.all


def turn_o(k, name, src, weight=None):
    nc, P = k.nc, k.psum
    turned = k.sem(f"{name}_turned")
    with nc.Block() as block:

        @block.tensor
        def _(pe):
            turn(k, pe, src, 0).then_inc(turned, 1)

        @block.scalar
        def _(act):
            act.wait_ge(turned, 1)
            for m in range(KD):
                nc.scalar.activation(k.xT[:, m, 0:4 * NP], P[:, 2 * m, 0:4 * NP], ACT.Copy)
                nc.scalar.activation(k.xT[:, m, 4 * NP:NODES], P[:, 2 * m + 1, 0:NP], ACT.Copy)


def rgcn(k):
    normalize(k, "ln_rgcn", k.x, k.xn, k.xT)
    with ExitStack() as st:
        k.stack = st
        w1 = k.sb("rgcn_w1", [128, KD, RELS, D])
        rgcn_layer(k, 0, w1)
        turn_o(k, "rgcn_mid", k.o)
        rgcn_layer(k, 1, w1)
    k.stack = k.all


def moe2_attention(k):
    nc, P = k.nc, k.psum
    normalize(k, "ln_moe2", k.x, k.xn, k.xT)
    normalize(k, "rms1", k.xn, k.o, k.xT, rms=True, weight=col(k, "ln1_w", 0, KD))
    with ExitStack() as outer:
        k.stack = outer
        causal = k.sb("causal", [NP, NB, NC])
        neg = k.sb("causal_neg", [NP, NB + 1, NC], BF16)
        with ExitStack() as st:
            k.stack = st
            w = k.sb("rope_w", [128, 4, KD, D])
            wv = k.sb("rope_wv", [128, KD, D // 2])
            rope = k.sb("rope_tables", [128, 2, NC])
            part = k.sb("rope_part", [128, 2, NC])
            loaded, raw, raw_taken, step, vs = (k.sem(f"rope_{s}") for s in (
                "loaded", "products", "products_taken", "step", "v_products"))
            with nc.Block() as block:

                @block.sync
                def _(sp):
                    sp.dma_start(rope[:, :, :], k.ins["rope"]).then_inc(loaded, 16)
                    for n, m in enumerate(("rope_wq", "rope_wq_swapped", "rope_wk", "rope_wk_swapped")):
                        sp.dma_start(w[:, n], k.ins[m].rearrange("(a p) n -> p a n", p=128)).then_inc(loaded, 16)
                    sp.dma_start(wv[:, :, :], k.ins["moe2_wv"].rearrange("(a p) n -> p a n", p=128)
                                 ).then_inc(loaded, 16)

                @block.tensor
                def _(pe):
                    t = nc.tensor
                    pe.wait_ge(loaded, 16 * 6)
                    for g in range(4):
                        at = 4 * (g % 2)
                        if g >= 2:
                            pe.wait_ge(raw_taken, g - 1)
                        for n in range(2):
                            for a in range(2):
                                for kk in range(KD):
                                    m = t.matmul(P[:, at + 2 * n + a, 0:HC],
                                                 w[:, 2 * (g // 2) + n, kk, (g % 2) * 128:(g % 2 + 1) * 128],
                                                 k.xT[:, kk, a * HC:(a + 1) * HC], start=(kk == 0),
                                                 stop=(kk == KD - 1))
                        m.then_inc(raw, 1)
                    pe.wait_ge(raw_taken, 4)
                    for b in range(NB):
                        for kk in range(KD):
                            m = t.matmul(P[0:NP, b, 0:D // 2], k.xT[:, kk, b * NP:(b + 1) * NP], wv[:, kk, :],
                                         start=(kk == 0), stop=(kk == KD - 1))
                    m.then_inc(vs, 1)

                @block.vector
                def _(dve):
                    c, v = Chain(dve, step), nc.vector
                    iota = k.const[0:NP, C_IOTA:C_IOTA + NC]
                    c(v.memset(k.oT[:, :, :], 0.0))
                    c(v.memset(neg[:, NB, :], 0.0))
                    for b in range(NB):
                        c(v.tensor_scalar(causal[:, b, :], iota, k.const[0:NP, C_ROW + b:C_ROW + b + 1], None,
                                          ALU.is_le))
                        c(v.tensor_scalar(neg[:, b, :], iota, k.const[0:NP, C_ROW + b:C_ROW + b + 1], NEG,
                                          ALU.is_gt, ALU.mult))
                    dve.wait_ge(loaded, 16 * 6)
                    for g in range(4):
                        dve.wait_ge(raw, g + 1)
                        at = 4 * (g % 2)
                        for n in range(2):
                            c(v.tensor_tensor(part[:, n, :].rearrange("p (a n) -> p a n", a=2),
                                              P[:, at + 2 * n:at + 2 * n + 2, 0:HC],
                                              rope[:, n, :].rearrange("p (a n) -> p a n", a=2), ALU.mult))
                        to = (k.qT if g < 2 else k.kT)[:, g % 2, 0:NC]
                        c(v.tensor_tensor(to, part[:, 0, :], part[:, 1, :], ALU.add))
                        v.tensor_scalar(to, to, 1.0, None, ALU.mult).then_inc(raw_taken, 1)
                        dve.wait_ge(raw_taken, g + 1)
                    dve.wait_ge(vs, 1)
                    v.tensor_copy(k.v[:, :, 0:D // 2], P[0:NP, 0:NB, 0:D // 2])
        attention(k, "causal", k.qT, k.kT, k.v, [0, 0, 64, 64], k.oT_padded, neg, causal)
    with ExitStack() as st:
        k.stack = st
        wo = k.sb("wo", [128, KD, D])
        loaded, out = k.sem("wo_loaded"), k.sem("wo_products")
        with nc.Block() as block:

            @block.sync
            def _(sp):
                sp.dma_start(wo[:, :, :], k.ins["moe2_wo"].rearrange("(a p) n -> p a n", p=128)).then_inc(loaded, 16)

            @block.tensor
            def _(pe):
                pe.wait_ge(loaded, 16)
                for b in range(NB):
                    for kk in range(KD):
                        m = nc.tensor.matmul(P[0:NP, b, 0:D], k.oT[:, kk, b * NP:(b + 1) * NP], wo[:, kk, :],
                                             start=(kk == 0), stop=(kk == KD - 1))
                    m.then_inc(out, 1)

            @block.vector
            def _(dve):
                for b in range(NB):
                    dve.wait_ge(out, b + 1)
                    nc.vector.tensor_tensor(k.z[:, b, :], k.xn[:, b, :], P[0:NP, b, 0:D], ALU.add)
    k.stack = k.all


HID = int(8 / 3 * D)
HT = 6
HR = -(-HID // HT)


def experts_swiglu(k, acc):
    nc, P = k.nc, k.psum
    with ExitStack() as st:
        k.stack = st
        w13 = [k.sb(f"moe2_w13_{s}", [128, 2, KD, HT * HR]) for s in range(2)]
        w2 = [k.sb(f"moe2_w2_{s}", [HR, HT, D]) for s in range(2)]
        act1 = [k.sb(f"moe2_silu{s}", [HR, NC]) for s in range(2)]
        hT = k.sb("moe2_hT", [HR, HT, NC])
        two = lambda n: [k.sem(f"moe2_{n}{s}") for s in range(2)]
        w13_loaded, w13_used, w2_loaded, w2_used, up_given, silu_ready, given, taken = (two(n) for n in (
            "w13_loaded", "w13_used", "w2_loaded", "w2_used", "up_given", "silu_ready", "down_given", "down_taken"))
        gate_given, gate_taken, cleared = (k.sem(f"moe2_{n}") for n in ("gate_given", "gate_taken", "cleared"))
        half = HT // 2
        with nc.Block() as block:

            @block.sync
            def _(sp):
                with sp.Fori(0, EXPERTS // 2) as i:
                    for s in range(2):
                        e = i * 2 + s
                        sp.wait_ge(w13_used[s], i + 1)
                        for n, m in enumerate(("moe2_w1", "moe2_w3")):
                            sp.dma_start(w13[s][:, n], k.ins[m][bass.ds(e, 1)].rearrange(
                                "o (a p) n -> p (o a) n", p=128)).then_inc(w13_loaded[s], 16)
                        sp.wait_ge(w2_used[s], i + 1)
                        sp.dma_start(w2[s][:, :, :], k.ins["moe2_w2"][bass.ds(e, 1)].rearrange(
                            "o (a p) n -> p (o a) n", p=HR)).then_inc(w2_loaded[s], 16)

            @block.tensor
            def _(pe):
                t = nc.tensor

                def up(s, n, m, bank):
                    for a in range(2):
                        for kk in range(KD):
                            ins = t.matmul(P[0:HR, bank + a, 0:HC], w13[s][:, n, kk, m * HR:(m + 1) * HR],
                                           k.xT[:, kk, a * HC:(a + 1) * HC], start=(kk == 0), stop=(kk == KD - 1))
                    return ins

                open_slots(pe, *w13_used, *w2_used)
                with pe.Fori(0, EXPERTS // 2) as i:
                    for s in range(2):
                        pe.wait_ge(w13_loaded[s], i * 32 + 32)
                        for m in range(HT):
                            pe.wait_ge(silu_ready[m % 2], (i * 2 + s) * half + (m // 2 + 1))
                            up(s, 0, m, 2 * (m % 2)).then_inc(up_given[m % 2], 1)
                            pe.wait_ge(gate_taken, (i * 2 + s) * HT + (m + 1))
                            up(s, 1, m, 4).then_inc(gate_given, 1)
                        pe.wait_ge(gate_taken, (i * 2 + s + 1) * HT + 1)
                        t.matmul(P[:, 4, 0:1], k.zeros[0:1, 0:128], k.zeros[0:1, 0:1], start=True,
                                 stop=True).then_inc(w13_used[s], 1)
                        pe.wait_ge(w2_loaded[s], i * 16 + 16)
                        down(k, pe, hT, w2[s], None, HT, HR, i, s, given, taken)
                        t.matmul(P[:, 4, 0:1], k.zeros[0:1, 0:128], k.zeros[0:1, 0:1], start=True,
                                 stop=True).then_inc(w2_used[s], 1)

            @block.scalar
            def _(act):
                open_slots(act, *silu_ready)
                with act.Fori(0, EXPERTS // 2) as i:
                    for s in range(2):
                        for m in range(HT):
                            act.wait_ge(up_given[m % 2], (i * 2 + s) * half + m // 2 + 1)
                            act.wait_ge(gate_taken, (i * 2 + s) * HT + max(m, 1))
                            nc.scalar.activation(act1[m % 2][:, :].rearrange("p (a n) -> p a n", a=2),
                                                 P[0:HR, 2 * (m % 2):2 * (m % 2) + 2, 0:HC],
                                                 ACT.Silu).then_inc(silu_ready[m % 2], 1)

            @block.vector
            def _(dve):
                v = nc.vector
                open_slots(dve, gate_taken, *taken)
                v.memset(acc[:, :, :], 0.0).then_inc(cleared, 1)
                dve.wait_ge(cleared, 1)
                with dve.Fori(0, EXPERTS // 2) as i:
                    for s in range(2):
                        for m in range(HT):
                            dve.wait_ge(silu_ready[m % 2], (i * 2 + s) * half + (m // 2 + 2))
                            dve.wait_ge(gate_given, (i * 2 + s) * HT + m + 1)
                            v.tensor_tensor(hT[:, m, :].rearrange("p (a n) -> p a n", a=2), P[0:HR, 4:6, 0:HC],
                                            act1[m % 2][:, :].rearrange("p (a n) -> p a n", a=2),
                                            ALU.mult).then_inc(gate_taken, 1)
                        gather_outputs(k, dve, acc, i, s, given, taken)
    k.stack = k.all


def moe2(k):
    moe2_attention(k)
    normalize(k, "rms2", k.z, k.xn, k.xT, rms=True, weight=col(k, "ln2_w", 0, KD))
    route(k, "moe2_route", k.xT, KD, "moe2_router", None, 2, 1e-9)
    experts_swiglu(k, k.o)
    add_to_x(k, "moe2_z", k.z)
    add_to_x(k, "moe2", k.o)


def edge_conv(k):
    nc, P = k.nc, k.psum
    normalize(k, "ln_edge", k.x, k.xn, k.xT)
    W = 2 * D
    with ExitStack() as st:
        k.stack = st
        own = k.sb("edge_own", [NP, 2, NB, W], F32R)
        ident = k.sb("edge_ident", [128, 128], F32R)
        sums = k.sb("edge_sums", [NP, NB, W])
        with ExitStack() as st2:
            k.stack = st2
            w1 = k.sb("edge_w1", [128, 4, W])
            brow = k.sb("edge_b1", [1, W])
            other = k.sb("edge_other", [NP, NB, W])
            whole_own = k.sb("edge_whole_own", [NP, W])
            loaded, products, copied, stored, taken, step = (k.sem(f"edge_node_{s}") for s in (
                "loaded", "products", "copied", "stored", "taken", "step"))
            with nc.Block() as block:

                @block.sync
                def _(sp):
                    sp.dma_start(w1[:, :, :], k.ins["L3_gnn_W1"].rearrange("(a p) n -> p a n", p=128)
                                 ).then_inc(loaded, 16)
                    sp.dma_start(brow[:, :], k.ins["L3_gnn_b1"].rearrange("(a n) -> a n", a=1)).then_inc(loaded, 16)
                    for b in range(NB):
                        sp.wait_ge(copied, b + 1)
                        sp.dma_start(k.node_tables[b * NP:(b + 1) * NP, :], other[:, b, :]).then_inc(stored, 16)
                    sp.wait_ge(stored, 16 * NB)

                @block.tensor
                def _(pe):
                    t = nc.tensor
                    pe.wait_ge(loaded, 32)
                    for b in range(NB):
                        q = 2 * (b % 2)
                        if b >= 2:
                            pe.wait_ge(taken, b - 1)
                        for kk in range(KD):
                            t.matmul(P[0:NP, q, :], k.xT[:, kk, b * NP:(b + 1) * NP], w1[:, KD + kk, :],
                                     start=(kk == 0), stop=(kk == KD - 1))
                        for kk in range(KD):
                            t.matmul(P[0:NP, q + 1, :], k.xT[:, kk, b * NP:(b + 1) * NP], w1[:, kk, :],
                                     start=(kk == 0), stop=False)
                        t.matmul(P[0:NP, q + 1, :], k.ones[0:1, 0:NP], brow[:, :], start=False,
                                 stop=True).then_inc(products, 1)

                @block.vector
                def _(dve):
                    c, v = Chain(dve, step), nc.vector
                    v.tensor_copy(ident[:, :], k.const[:, C_ID:C_ID + 128])
                    for b in range(NB):
                        q = 2 * (b % 2)
                        dve.wait_ge(products, b + 1)
                        v.tensor_copy(other[:, b, :], P[0:NP, q, :]).then_inc(copied, 1)
                        dve.wait_ge(copied, b + 1)
                        v.tensor_tensor(whole_own[:, :], P[0:NP, q + 1, :], other[:, b, :],
                                        ALU.subtract).then_inc(taken, 1)
                        dve.wait_ge(taken, b + 1)
                        c(v.tensor_copy(own[:, 0, b, :], whole_own[:, :]))
                        c(v.tensor_tensor(own[:, 1, b, :], whole_own[:, :], own[:, 0, b, :].bitcast(F32),
                                          ALU.subtract))
        with ExitStack() as st2:
            k.stack = st2
            four = lambda n: [k.sem(f"edge_{n}{s}") for s in range(4)]
            gathered, hotT_given, hotT_ready, mine, rows_free, high_ready, low_ready = (four(n) for n in (
                "rows_gathered", "onehotT_given", "onehotT_ready", "own_given", "rows_free", "high_ready",
                "low_ready"))
            hot_ready, used = ([k.sem(f"edge_{n}{s}") for s in range(8)] for n in ("onehot_ready", "used"))
            idx_ready, idx_seen, whole, cleared = (k.sem(f"edge_{n}") for n in (
                "idx_ready", "idx_seen", "whole", "cleared"))
            idx = [k.sb(f"edge_idx{s}", [LANES, 4], U32) for s in range(2)]
            rows = [k.sb(f"edge_rows{s}", [LANES, W]) for s in range(4)]
            pre = [k.sb(f"edge_pre{s}", [LANES, W]) for s in range(4)]
            high = [k.sb(f"edge_high{s}", [LANES, W], F32R) for s in range(4)]
            low = [k.sb(f"edge_low{s}", [LANES, W], F32R) for s in range(4)]
            hot = [k.sb(f"edge_hot_{s}", [LANES, NP + 1], F32R) for s in range(8)]
            hotT = [k.sb(f"edge_hotT{s}", [NP, LANES], F32R) for s in range(4)]
            eights = lambda i, n: (n % 8, i + n // 8)
            fours = lambda i, n: (n % 4, i * 2 + n // 4)
            with nc.Block() as block:

                @block.gpsimd
                def _(pool):
                    gather_tiles(k, pool, k.e_srci, idx, idx_ready, idx_seen, rows_free, rows, k.node_rows, gathered)

                @block.tensor
                def _(pe):
                    t = nc.tensor

                    def onehotT(i, n):
                        s, m = eights(i, n)
                        q, _ = fours(i, n)
                        pe.wait_ge(hot_ready[s], m + 1)
                        if n or not isinstance(i, int):
                            p, m = fours(i, n - 1)
                            pe.wait_ge(hotT_ready[p], m + 1)
                        t.matmul(P[0:NP, 5, q * 128:(q + 1) * 128], hot[s][:, 0:NP], ident[:, :], start=True,
                                 stop=True).then_inc(hotT_given[q], 1)

                    def own_rows(b, i, n):
                        q, m = fours(i, n)
                        pe.wait_ge(hotT_ready[q], m + 1)
                        t.matmul(P[:, 6 + n % 2, :], hotT[q][:, :], own[:, 0, bass.ds(b, 1), :],
                                 start=True, stop=False)
                        t.matmul(P[:, 6 + n % 2, :], hotT[q][:, :], own[:, 1, bass.ds(b, 1), :],
                                 start=False, stop=True).then_inc(mine[q], 1)

                    open_slots(pe, *mine, *used)
                    for b in range(NB):
                        t.matmul(P[0:NP, b, :], k.zeros[0:1, 0:NP], k.zeros[0:1, 0:512], start=True, stop=False)
                    first = tile_blocks(k, pe, 0)
                    for n in range(3):
                        onehotT(0, n)
                    for n in range(2):
                        own_rows(first[n], 0, n)
                    with pe.Fori(0, ET // 8) as i:
                        of = tile_blocks(k, pe, i * 2)[:4] + tile_blocks(k, pe, i * 2 + 1)
                        for n in range(8):
                            onehotT(i, n + 3)
                            q, m = fours(i, n)
                            pe.wait_ge(rows_free[q], m + 2)
                            own_rows(of[n + 2], i, n + 2)
                            pe.wait_ge(low_ready[q], m + (2 if q == 3 else 1))
                            for part in (high, low):
                                last = t.matmul(k.psum_flat[0:NP, bass.ds(of[n] * 512, 512)], hot[n][:, 0:NP],
                                                part[q][:, :], start=False, stop=False, skip_group_check=True)
                            last.then_inc(used[n], 1)
                    for b in range(NB):
                        m = t.matmul(P[0:NP, b, :], k.zeros[0:1, 0:NP], k.zeros[0:1, 0:512], start=False, stop=True)
                    m.then_inc(whole, 1)

                @block.scalar
                def _(act):
                    a = nc.scalar

                    def copy_onehotT(i, n):
                        q, m = fours(i, n)
                        act.wait_ge(hotT_given[q], m + 1)
                        act.wait_ge(mine[q], m + 1)
                        a.activation(hotT[q][:, :], P[0:NP, 5, q * 128:(q + 1) * 128],
                                     ACT.Copy).then_inc(hotT_ready[q], 1)

                    open_slots(act, *high_ready)
                    for n in range(3):
                        copy_onehotT(0, n)
                    with act.Fori(0, ET // 8) as i:
                        for n in range(8):
                            q, m = fours(i, n)
                            act.wait_ge(rows_free[q], m + 2)
                            act.wait_ge(used[(n + 4) % 8], i + 1 + n // 4)
                            a.activation(high[q][:, :], pre[q][:, :], ACT.Relu).then_inc(high_ready[q], 1)
                            copy_onehotT(i, n + 3)

                @block.vector
                def _(dve):
                    v = nc.vector

                    def onehot(i, n):
                        s, m = eights(i, n)
                        dve.wait_ge(used[s], m + 1)
                        at = slice(n, n + 1) if isinstance(i, int) else bass.ds(i * 8 + n, 1)
                        v.tensor_scalar(hot[s][:, :], k.const[:, C_IOTA:C_IOTA + NP + 1], k.e_ldst[:, at], None,
                                        ALU.is_equal).then_inc(hot_ready[s], 1)

                    def split(q, count):
                        dve.wait_ge(high_ready[q], count)
                        v.scalar_tensor_tensor(low[q][:, :], pre[q][:, :], 0.0, high[q][:, :].bitcast(F32), ALU.max,
                                               ALU.subtract).then_inc(low_ready[q], 1)

                    open_slots(dve, *rows_free)
                    v.memset(pre[3][:, :], 0.0).then_inc(cleared, 1)
                    v.tensor_copy(high[3][:, :], k.zeros[:, 0:W]).then_inc(cleared, 1)
                    dve.wait_ge(cleared, 2)
                    for n in range(3):
                        onehot(0, n)
                    with dve.Fori(0, ET // 8) as i:
                        for n in range(8):
                            onehot(i, n + 3)
                            q, m = fours(i, n)
                            dve.wait_ge(mine[q], m + 2)
                            dve.wait_ge(gathered[q], m * 16 + 16)
                            dve.wait_ge(high_ready[q], m + 1)
                            v.tensor_tensor(pre[q][:, :], P[:, 6 + n % 2, :], rows[q][:, :],
                                            ALU.add).then_inc(rows_free[q], 1)
                            split((n - 1) % 4, i * 2 + (n - 1) // 4 + 2)
                    split(3, ET // 4 + 1)
                    dve.wait_ge(whole, 1)
                    v.tensor_copy(sums[:, :, :], P[0:NP, 0:NB, :])
        with ExitStack() as st2:
            k.stack = st2
            w2 = k.sb("edge_w2", [128, 4, D])
            b2 = k.sb("edge_b2", [NP, D])
            sumsT = k.sb("edge_sumsT", [128, 4, NC])
            rdeg = k.sb("edge_rdeg", [NP, 2, NB])
            y = k.sb("edge_y", [NP, NB, D])
            loaded, turned, copied, out, step = (k.sem(f"edge_out_{s}") for s in (
                "loaded", "turned", "copied", "products", "step"))
            with nc.Block() as block:

                @block.sync
                def _(sp):
                    sp.dma_start(w2[:, :, :], k.ins["L3_gnn_W2"].rearrange("(a p) n -> p a n", p=128)
                                 ).then_inc(loaded, 16)
                    sp.dma_start(b2[:, :], k.ins["edge_b2"]).then_inc(loaded, 16)

                @block.tensor
                def _(pe):
                    t = nc.tensor
                    for m in range(4):
                        for b in range(NB):
                            ins = t.transpose(P[:, 2 * m + b // 4, (b % 4) * NP:(b % 4 + 1) * NP],
                                              sums[:, b, m * 128:(m + 1) * 128], k.const[0:NP, C_ID:C_ID + NP])
                        ins.then_inc(turned, 1)
                    pe.wait_ge(loaded, 32)
                    pe.wait_ge(copied, 4)
                    for b in range(NB):
                        for kk in range(4):
                            ins = t.matmul(P[0:NP, b, 0:D], sumsT[:, kk, b * NP:(b + 1) * NP], w2[:, kk, :],
                                           start=(kk == 0), stop=(kk == 3))
                        ins.then_inc(out, 1)

                @block.scalar
                def _(act):
                    for m in range(4):
                        act.wait_ge(turned, m + 1)
                        nc.scalar.activation(sumsT[:, m, 0:4 * NP], P[:, 2 * m, 0:4 * NP], ACT.Copy)
                        nc.scalar.activation(sumsT[:, m, 4 * NP:NODES], P[:, 2 * m + 1, 0:NP],
                                             ACT.Copy).then_inc(copied, 1)

                @block.vector
                def _(dve):
                    c, v = Chain(dve, step), nc.vector
                    c(v.tensor_scalar(rdeg[:, 0, :], k.deg[:, :], 1e-8, None, ALU.add))
                    c(v.reciprocal(rdeg[:, 1, :], rdeg[:, 0, :]))
                    dve.wait_ge(loaded, 32)
                    for b in range(NB):
                        dve.wait_ge(out, b + 1)
                        c(v.scalar_tensor_tensor(y[:, b, :], b2[:, :], k.deg[:, b:b + 1], P[0:NP, b, 0:D], ALU.mult,
                                                 ALU.add))
                        c(v.scalar_tensor_tensor(k.x[:, b, :], y[:, b, :], rdeg[:, 1, b:b + 1], k.x[:, b, :],
                                                 ALU.mult, ALU.add))
    k.stack = k.all


def moe3(k):
    nc, P = k.nc, k.psum
    tiles = 8
    normalize(k, "ln_moe3", k.x, k.xn, k.xT)
    with ExitStack() as outer:
        k.stack = outer
        hT = k.sb("moe3_hT", [128, tiles, NC])
        with ExitStack() as st:
            k.stack = st
            w1 = k.sb("moe3_w1", [128, KD, tiles * 128])
            loaded = k.sem("moe3_w1_loaded")
            given, taken = ([k.sem(f"moe3_up_{n}{s}") for s in range(2)] for n in ("given", "taken"))
            with nc.Block() as block:

                @block.sync
                def _(sp):
                    sp.dma_start(w1[:, :, :], k.ins["L3_ffn_W1"].rearrange("(a p) n -> p a n", p=128)
                                 ).then_inc(loaded, 16)

                @block.tensor
                def _(pe):
                    pe.wait_ge(loaded, 16)
                    for m in range(tiles):
                        q = m % 2
                        if m >= 2:
                            pe.wait_ge(taken[q], m // 2)
                        for a in range(2):
                            for kk in range(KD):
                                ins = nc.tensor.matmul(P[:, 2 * q + a, 0:HC], w1[:, kk, m * 128:(m + 1) * 128],
                                                       k.xT[:, kk, a * HC:(a + 1) * HC], start=(kk == 0),
                                                       stop=(kk == KD - 1))
                        ins.then_inc(given[q], 1)

                @block.scalar
                def _(act):
                    for m in range(tiles):
                        act.wait_ge(given[m % 2], m // 2 + 1)
                        nc.scalar.activation(hT[:, m, :].rearrange("p (a n) -> p a n", a=2),
                                             P[:, 2 * (m % 2):2 * (m % 2) + 2, 0:HC], ACT.Gelu,
                                             bias=col(k, "moe3_b1", m)).then_inc(taken[m % 2], 1)
        route(k, "moe3_route", hT, tiles, "moe3_router", "L3_ffn_bg", 1, None)
        with ExitStack() as st:
            k.stack = st
            wd = [k.sb(f"moe3_wd{s}", [128, tiles, D]) for s in range(2)]
            bd = [k.sb(f"moe3_bd{s}", [1, D]) for s in range(2)]
            w_loaded, w_used, given, taken = ([k.sem(f"moe3_{n}{s}") for s in range(2)] for n in (
                "wd_loaded", "wd_used", "down_given", "down_taken"))
            cleared = k.sem("moe3_cleared")
            with nc.Block() as block:

                @block.sync
                def _(sp):
                    with sp.Fori(0, EXPERTS // 2) as i:
                        for s in range(2):
                            e = i * 2 + s
                            sp.wait_ge(w_used[s], i + 1)
                            sp.dma_start(wd[s][:, :, :], k.ins["L3_ffn_Wd"][bass.ds(e, 1)].rearrange(
                                "o (a p) n -> p (o a) n", p=128)).then_inc(w_loaded[s], 16)
                            sp.dma_start(bd[s][:, :], k.ins["L3_ffn_bd"][bass.ds(e, 1), :]).then_inc(w_loaded[s], 16)

                @block.tensor
                def _(pe):
                    open_slots(pe, *w_used)
                    with pe.Fori(0, EXPERTS // 2) as i:
                        for s in range(2):
                            pe.wait_ge(w_loaded[s], i * 32 + 32)
                            down(k, pe, hT, wd[s], bd[s][:, :], tiles, 128, i, s, given, taken)
                            nc.tensor.matmul(P[:, 4, 0:1], k.zeros[0:1, 0:128], k.zeros[0:1, 0:1], start=True,
                                             stop=True).then_inc(w_used[s], 1)

                @block.vector
                def _(dve):
                    open_slots(dve, *taken)
                    nc.vector.memset(k.o[:, :, :], 0.0).then_inc(cleared, 1)
                    dve.wait_ge(cleared, 1)
                    with dve.Fori(0, EXPERTS // 2) as i:
                        for s in range(2):
                            gather_outputs(k, dve, k.o, i, s, given, taken)
    k.stack = k.all
    add_to_x(k, "moe3", k.o)


def store(k):
    done = k.sem("stored")
    with k.nc.Block() as block:

        @block.sync
        def _(sp):
            sp.dma_start(k.out.rearrange("(b p) d -> p b d", b=NB), k.x[:, :, :]).then_inc(done, 16)
            sp.wait_ge(done, 16)
STAGES = [edges, conv_layers, moe0, sage, moe1, rgcn, moe2, edge_conv, moe3, store]


def build(nc, ins, out, stages=None):
    k = Kernel(nc, ins, out)
    with k.all:
        k.const = k.sb("const", [128, C_END])
        k.ones = k.sb("ones", [128, 512])
        k.zeros = k.sb("zeros", [128, 512])
        k.x = k.sb("x_res", [NP, NB, D])
        k.xn = k.sb("xn", [NP, NB, D])
        k.xT = k.sb("xT", [128, KD, NC])
        k.C = k.sb("C", [NP, NB, NC])
        k.CT = k.sb("CT", [NP, NB, NC])
        k.deg = k.sb("deg", [NP, NB])
        k.e_ldst = k.sb("e_ldst", [LANES, ET + AHEAD])
        k.e_src = k.sb("e_src", [LANES, ET])
        k.e_w = k.sb("e_w", [LANES, ET])
        k.e_row = k.sb("e_row", [LANES, ET], U32)
        k.e_srci = k.sb("e_srci", [LANES, ET], U32)
        k.e_blk = k.sb("e_blk", [1, ET // 4], I32)
        k.negC = k.sb("negC", [NP, NB + 1, NC], BF16)
        k.ident16 = k.sb("ident16", [128, 128], BF16)
        k.wconv = k.sb("wconv", [128, 3, KD, 4 * D])
        k.rgcn_w0 = k.wconv[:, 0:2].rearrange("p i a n -> p (i a n)").rearrange("p (a r d) -> p a r d", a=KD, r=RELS)
        k.wconv_loaded = k.all.enter_context(nc.semaphore("wconv_loaded"))
        k.basis = k.sb("rgcn_basis", [128, RELS, KD, D])
        k.coeff = k.sb("rgcn_coeff", [128, 2, RELS * RELS])
        k.basis_loaded = k.all.enter_context(nc.semaphore("rgcn_basis_loaded"))
        k.col = k.sb("columns", [128, sum(COLS.values())])
        k.brow = k.sb("brow", [1, 2 * D])
        k.qT = k.sb("qT", [128, KD, NODES + NP])
        k.kT = k.sb("kT", [128, KD, NC])
        k.v = k.sb("v", [NP, NB, D])
        k.o = k.sb("o", [NP, NB, D])
        k.oT_padded = k.sb("oT", [128, KD, NP + NC])
        k.oT = k.oT_padded[:, :, NP:NP + NC]
        k.gate = k.sb("gate", [NP, NB, EXPERTS])
        k.z = k.sb("z", [NP, NB, D])
        k.picked = k.sb("picked", [1, 2], I32)
        k.picked_b1 = k.sb("picked_b1", [128, 8])
        k.tables = nc.dram_tensor("edge_tables", (NODES, RELS * D), F32).ap()
        k.table_rows = k.tables.rearrange("n (r d) -> (n r) d", d=D)
        k.node_tables = nc.dram_tensor("node_tables", (NODES, 2 * D), F32).ap()
        k.node_rows = k.node_tables
        k.psum = k.all.enter_context(nc.psum_tensor("psum", [128, 8, 512], F32))
        k.psum_flat = k.psum[:, :, :].rearrange("p b n -> p (b n)")
        for s in (stages or STAGES):
            s(k)
            k.end_layer()
    return k


def layout(i):
    a = {"const": constants()}
    a["x"] = i["x"].reshape(NB, NP, D).transpose(1, 0, 2)
    for n in ("src", "dst", "edge_type_8", "edge_weight1"):
        a[n] = i[n].reshape(EP, EC)

    def tiles(v):
        v = v.reshape(*v.shape[:-1], -1, 128)
        return np.moveaxis(v, -1, 0).reshape(128, -1)

    def padded(v):
        v = np.concatenate([v, np.zeros_like(v[:1])]).reshape(EXPERTS + 1, KD, 128)
        return v.transpose(2, 1, 0).reshape(128, -1)

    def router(w):
        return w.reshape(-1, 128, EXPERTS).transpose(1, 0, 2).reshape(128, -1)

    c = {"conv_bias": tiles(np.stack([i["L0_gnn_bq"], i["L0_gnn_bk"], i["L0_gnn_bs"]], 1)),
         "bn_gamma": tiles(i["L0_gnn_bn_gamma"]), "bn_beta": tiles(i["L0_gnn_bn_beta"]),
         "moe0_ln_g": padded(i["L0_ffn_ln_g"]), "moe0_ln_b": padded(i["L0_ffn_ln_b"]),
         "moe0_b1": tiles(i["L0_ffn_b1"]), "moe3_b1": tiles(i["L3_ffn_b1"]),
         "ln1_w": tiles(i["L2_ffn_ln1_w"]), "ln2_w": tiles(i["L2_ffn_ln2_w"]),
         "moe0_router": router(i["L0_ffn_Wr"]), "moe1_router": router(i["L1_ffn_Wr"]),
         "moe2_router": router(i["L2_ffn_router_w"].T), "moe3_router": router(i["L3_ffn_Wg"])}
    a["cols"] = np.concatenate([c[n] for n in COLS], 1)
    a["coeff_rows"] = np.broadcast_to(i["L2_gnn_coeff"].reshape(1, -1), (128, i["L2_gnn_coeff"].size))
    a["moe1_b1"] = i["L1_ffn_b1"].reshape(EXPERTS, -1, 128).transpose(0, 2, 1)
    for n in ("gamma", "beta"):
        a[f"moe1_{n}"] = np.broadcast_to(i[f"L1_ffn_{n}"].reshape(1, D), (NP, D))
    a["edge_b2"] = np.broadcast_to(i["L3_gnn_b2"].reshape(1, D), (NP, D))
    swap = np.arange(D).reshape(-1, 2, 32)[:, ::-1].reshape(-1)
    wq = i["L2_ffn_wq"]
    wk = i["L2_ffn_wk"].reshape(2, 1, 64, D).repeat(2, 1).reshape(D, D)
    a["rope_wq"], a["rope_wq_swapped"] = wq.T, wq[swap].T
    a["rope_wk"], a["rope_wk_swapped"] = wk.T, wk[swap].T
    a["moe2_wv"], a["moe2_wo"] = i["L2_ffn_wv"].T, i["L2_ffn_wo"].T
    a["rope"] = rope_tables()
    wide = lambda w: np.concatenate([w, np.zeros((EXPERTS, HT * HR - HID, D), np.float32)], 1)
    for n, m in (("moe2_w1", "L2_ffn_w1"), ("moe2_w3", "L2_ffn_w3")):
        a[n] = wide(i[m]).transpose(0, 2, 1)
    a["moe2_w2"] = wide(i["L2_ffn_w2"].transpose(0, 2, 1))
    for n in i:
        if n not in a:
            a[n] = i[n]
    return {n: np.ascontiguousarray(v) for n, v in a.items()}


def rope_tables():
    hd = 64
    inv = 1.0 / 10000.0 ** (np.arange(0, hd, 2, dtype=np.float32) / hd)
    f = np.outer(np.arange(NC, dtype=np.float32), inv)
    e = np.concatenate([f, f], -1).T
    sign = np.where(np.arange(hd) < hd // 2, -1.0, 1.0)[:, None]
    both = np.stack([np.cos(e), np.sin(e) * sign], 1)
    return np.concatenate([both, both]).astype(np.float32)


def kernel(**inputs):
    import concourse.bacc as bacc
    from concourse.bass_utils import run_bass_kernel_spmd

    arrays = layout({n: np.asarray(v) for n, v in inputs.items()})
    nc = bacc.Bacc("TRN2", target_bir_lowering=False, num_devices=1)
    ins = {n: nc.dram_tensor(f"in_{n}", a.shape, mybir.dt.from_np(a.dtype), kind="ExternalInput").ap()
           for n, a in arrays.items()}
    out = nc.dram_tensor("out", (NODES, D), F32, kind="ExternalOutput").ap()
    build(nc, ins, out)
    r = run_bass_kernel_spmd(nc, [{f"in_{n}": a for n, a in arrays.items()}], core_ids=[0])
    return r.results[0]["out"]
```

```python
import numpy as np
import concourse.bass as bass
from concourse import mybir
from contextlib import ExitStack

F32 = mybir.dt.float32
BF16 = mybir.dt.bfloat16
F32R = mybir.dt.float32r
F16 = mybir.dt.float16
I32 = mybir.dt.int32
U32 = mybir.dt.uint32
ALU = mybir.AluOpType
ACT = mybir.ActivationFunctionType
AX = mybir.AxisListType

NODES = 625
NB = 5
NP = NODES // NB
NC = NODES + 1
HC = NC // 2
WC = -(-NC // 4) * 4
D = 256
KD = D // 128
EDGES = 20625
EP = 125
EC = EDGES // EP
LANES = 128
ET = -(-((EDGES + NB * (LANES - 1)) // LANES) // 4) * 4
AHEAD = 4
EXPERTS = 8
RELS = 8
BASIS_LOADS = 16 * (1 + RELS)
NEG = -1e30
LN_EPS = 1e-5

C_ID = 0
C_TRI = C_ID + 128
C_IOTA = C_TRI + 128
C_RANK = C_IOTA + NC
C_ROW = C_RANK + EXPERTS * EXPERTS
C_END = C_ROW + NB


def constants():
    c = np.zeros((128, C_END), np.float32)
    c[:, C_ID:C_ID + 128] = np.eye(128)
    c[:, C_TRI:C_TRI + 128] = np.triu(np.ones((128, 128)), 1)
    c[:, C_IOTA:C_IOTA + NC] = np.arange(NC)
    c[:, C_ROW:C_END] = np.arange(128)[:, None] + NP * np.arange(NB)
    c[:, C_RANK:C_ROW] = np.tril(np.ones((EXPERTS, EXPERTS)), -1).reshape(-1)
    return c


COLS = {"conv_bias": 3 * 3 * KD, "bn_gamma": 2 * KD, "bn_beta": 2 * KD, "moe0_ln_g": KD * (EXPERTS + 1),
        "moe0_ln_b": KD * (EXPERTS + 1), "moe0_b1": EXPERTS * 8, "moe3_b1": 8, "ln1_w": KD, "ln2_w": KD,
        "moe0_router": KD * EXPERTS, "moe1_router": KD * EXPERTS, "moe2_router": KD * EXPERTS,
        "moe3_router": 8 * EXPERTS}


def col(k, name, first=0, count=1):
    at = sum(w for n, w in COLS.items() if list(COLS).index(n) < list(COLS).index(name))
    if isinstance(first, int):
        return k.col[:, at + first:at + first + count]
    return k.col[:, bass.ds(first + at, count)]


class Kernel:

    def __init__(self, nc, ins, out):
        self.nc, self.ins, self.out = nc, ins, out
        self.all = ExitStack()
        self.layer_sems = []
        self.stack = self.all

    def sb(self, name, shape, dt=F32):
        return self.stack.enter_context(self.nc.sbuf_tensor(name, shape, dt))

    def sem(self, name):
        self.layer_sems.append(self.nc.alloc_semaphore(name))
        return self.layer_sems[-1]

    def end_layer(self):
        self.nc.clear_and_free_semaphores(self.layer_sems)
        self.nc.all_engine_barrier()
        self.layer_sems = []


class Chain:

    def __init__(self, eng, sem):
        self.eng, self.sem, self.n = eng, sem, 0

    def __call__(self, ins):
        ins.then_inc(self.sem, 1)
        self.n = self.n + 1
        self.eng.wait_ge(self.sem, self.n)


def open_slots(eng, *sems):
    for s in sems:
        eng.sem_inc(s, 1)


class AheadWord:

    def __init__(self, k, pe, name, first):
        self.k, self.pe, self.reg = k, pe, pe.alloc_register(name)
        self.load(first)

    def load(self, i):
        self.pe.reg_load(self.reg, self.k.e_blk[0:1, bass.ds(i, 1)])

    def take(self):
        return self.pe.snap(self.reg, min_val=0, max_val=8 ** 10 - 1)


def tile_blocks(k, pe, i, word=None):
    if word is None:
        word = pe.value_load(k.e_blk[0:1, bass.ds(i, 1)], min_val=0, max_val=8 ** 10 - 1)
    of = []
    for _ in range(10):
        of.append(k.nc.s_assert_within(word % 8, min_val=0, max_val=NB - 1, skip_runtime_bounds_check_because=(
            "every digit counts which of the blocks 1 to NB - 1 start at its tile or before it")))
        word = word // 8
    return of


def load_basis(k, eng, basis, l):
    for b in range(RELS):
        eng.dma_start(basis[:, b], k.ins["L2_gnn_basis"][l, b].rearrange("(a p) n -> p a n", p=128)
                      ).then_inc(k.basis_loaded, 16)


def mix_basis(k, v, basis, w, l, r, b):
    at = bass.ds(r * RELS + b, 1)
    to = w[:, :, bass.ds(r, 1), :] if not isinstance(r, int) else w[:, :, r:r + 1, :]
    base = basis[:, b:b + 1].rearrange("p o a n -> p a o n")
    if b == 0:
        return v.tensor_scalar(to, base, k.coeff[:, l, at], None, ALU.mult)
    return v.scalar_tensor_tensor(to, base, k.coeff[:, l, at], to, ALU.mult, ALU.add)


def edges(k):
    nc, P = k.nc, k.psum
    with ExitStack() as st:
        k.stack = st
        ints = k.sb("edge_ints", [EP, 3, EC], I32)
        flt = k.sb("edge_floats", [EP, 3, EC])
        ge = k.sb("edge_ge", [EP, NB + 1, EC])
        member = k.sb("edge_member", [EP, NB, EC])
        count = k.sb("edge_count", [EP, NB, EC])
        ones = k.sb("edge_ones", [EP, EC])
        tot = k.sb("edge_tot", [128, 4, NB + 1])
        toti = k.sb("edge_toti", [128, NB], I32)
        ldst = k.sb("edge_ldst", [EP, EC])
        blk = k.sb("edge_blk", [EP, EC])
        pos = k.sb("edge_pos", [EP, EC])
        posi = k.sb("edge_posi", [EP, 2, EC], I32)
        lane = k.sb("edge_lane", [EP, 2, EC])
        field = k.sb("edge_field", [EP, 2, EC])
        hot = [k.sb(f"edge_hot{s}", [EP, 5, LANES]) for s in range(3)]
        put = [k.sb(f"edge_put{s}", [EP, 2, ET]) for s in range(5)]
        keyi = k.sb("edge_keyi", [LANES, 4, ET], I32)
        tb = k.sb("edge_tb", [1, ET + 3 * AHEAD])
        tbw = k.sb("edge_tb_words", [1, 2, ET // 4])
        tbi = k.sb("edge_tb_halves", [1, 2, ET // 4], I32)
        dhot = [k.sb(f"edge_dhot{s}", [LANES, 4, NP], BF16) for s in range(3)]
        shot = [k.sb(f"edge_shot{s}", [LANES, NC], BF16) for s in range(4)]
        iota16 = k.sb("iota16", [128, NC], F16)
        iota = k.const[:, C_IOTA:C_IOTA + NC]

        loaded, const_loaded, rest_loaded = (k.sem(f"edges_{n}") for n in ("loaded", "const_loaded", "rest_loaded"))
        step = k.sem("edges_step")
        rows = k.sem("edge_row_totals")
        prefix = k.sem("edge_prefix")
        put_ready = [k.sem(f"edge_put_ready{s}") for s in range(5)]
        put_used = [k.sem(f"edge_put_used{s}") for s in range(5)]
        lanes_ready = [k.sem(f"edge_lanes_ready{s}") for s in range(3)]
        lanes_far = [k.sem(f"edge_lanes_far{s}") for s in range(3)]
        dhot_far = [k.sem(f"edge_dhot_far{s}") for s in range(3)]
        squared = k.sem("edge_squared")
        laned = k.sem("edge_laned")
        sorted_ = k.sem("edges_sorted")
        unpacked = k.sem("edges_unpacked")
        blocks_known = k.sem("edge_blocks_known")
        dhot_ready = [k.sem(f"edge_dhot_ready{s}") for s in range(3)]
        shot_ready, shot_used = ([k.sem(f"edge_{n}{s}") for s in range(4)] for n in ("shot_ready", "shot_used"))
        counted = k.sem("edges_counted")
        c_ready = k.sem("c_ready")
        turned = k.sem("c_turned")
        ct_half = k.sem("ct_half_copied")
        with nc.Block() as block:

            @block.sync
            def _(sp):
                sp.dma_start(ints[:, 0, :], k.ins["dst"]).then_inc(loaded, 16)
                sp.dma_start(ints[:, 1, :], k.ins["src"]).then_inc(loaded, 16)
                sp.dma_start(ints[:, 2, :], k.ins["edge_type_8"]).then_inc(loaded, 16)
                sp.dma_start(field[:, 1, :], k.ins["edge_weight1"]).then_inc(loaded, 16)
                sp.dma_start(k.const[:, :], k.ins["const"]).then_inc(const_loaded, 16)
                sp.dma_start(k.x[:, :, :], k.ins["x"]).then_inc(rest_loaded, 16)
                sp.dma_start(k.col[:, :], k.ins["cols"]).then_inc(rest_loaded, 16)
                for i in range(3):
                    for n, m in enumerate(("Wq", "Wk", "Ws", "Wv")):
                        sp.dma_start(k.wconv[:, i, :, n * D:(n + 1) * D],
                                     k.ins[f"L0_gnn_{m}"][i].rearrange("(a p) n -> p a n", p=128)
                                     ).then_inc(k.wconv_loaded, 16)
                sp.dma_start(k.coeff[:, :, :], k.ins["coeff_rows"].rearrange("p (l n) -> p l n", l=2)
                             ).then_inc(k.basis_loaded, 16)

            @block.vector
            def _(dve):
                c = Chain(dve, step)
                v = nc.vector
                v.memset(ones[:, :], 1.0)
                v.memset(tot[:, :, :], 0.0)
                v.memset(k.ones[:, :], 1.0)
                v.memset(k.zeros[:, :], 0.0)
                v.memset(k.gates[:, :], 0.0)
                v.memset(k.zeros16[:, :], 0.0)
                v.memset(k.C[:, :, NODES:NC], 0.0)
                v.memset(k.CT[:, :, NODES:NC], 0.0)
                v.memset(k.xT[:, :, NODES:NC], 0.0)
                v.memset(k.oT_padded[:, :, :], 0.0)
                c(v.memset(k.qT[:, :, NC:NODES + NP], 0.0))
                dve.wait_ge(loaded, 16 * 4)
                c(v.tensor_copy(flt[:, :, :], ints[:, :, :]))
                for b in range(NB + 1):
                    last = v.tensor_scalar(ge[:, b, :], flt[:, 0, :], float(b * NP), None, ALU.is_ge)
                c(last)
                c(v.tensor_tensor(member[:, :, :], ge[:, 0:NB, :], ge[:, 1:NB + 1, :], ALU.subtract))
                for b in range(NB):
                    last = v.tensor_tensor_scan(count[:, b, :], ones[:, :], member[:, b, :], 0.0, ALU.mult, ALU.add)
                c(last)
                v.tensor_copy(tot[0:EP, 0, 0:NB], count[:, :, EC - 1]).then_inc(rows, 1)
                dve.wait_ge(const_loaded, 16)
                v.tensor_copy(iota16[:, :], iota)
                c(v.tensor_tensor(blk[:, :], ge[:, 1, :], ge[:, 2, :], ALU.add))
                c(v.tensor_tensor(blk[:, :], blk[:, :], ge[:, 3, :], ALU.add))
                c(v.tensor_tensor(blk[:, :], blk[:, :], ge[:, 4, :], ALU.add))
                c(v.scalar_tensor_tensor(ldst[:, :], blk[:, :], float(-NP), flt[:, 0, :], ALU.mult, ALU.add))
                c(v.scalar_tensor_tensor(field[:, 0, :], flt[:, 1, :], 8.0, flt[:, 2, :], ALU.mult, ALU.add))
                c(v.scalar_tensor_tensor(field[:, 0, :], field[:, 0, :], 128.0, ldst[:, :], ALU.mult, ALU.add))
                c(v.tensor_scalar(field[:, 0, :], field[:, 0, :], 1.0, None, ALU.add))
                dve.wait_ge(prefix, 1)
                c(v.tensor_scalar(tot[:, 1, 0:NB], P[:, 1, 0:NB], float(LANES - 1), None, ALU.add))
                c(v.tensor_copy(toti[:, :], tot[:, 1, 0:NB]))
                c(v.tensor_scalar(toti[:, :], toti[:, :], 7, None, ALU.logical_shift_right))
                c(v.tensor_copy(tot[:, 1, 0:NB], toti[:, :]))
                c(v.tensor_tensor_scan(tot[:, 2, 1:NB + 1], k.ones[:, 0:NB], tot[:, 1, 0:NB], 0.0, ALU.mult, ALU.add))
                c(v.scalar_tensor_tensor(tot[0:EP, 3, 0:NB], tot[0:EP, 2, 0:NB], float(LANES), P[0:EP, 0, 0:NB],
                                         ALU.mult, ALU.add))
                c(v.tensor_scalar(tot[0:EP, 3, 0:NB], tot[0:EP, 3, 0:NB], -1.0, None, ALU.add))
                for b in range(NB):
                    last = v.scalar_tensor_tensor(count[:, b, :], count[:, b, :], tot[0:EP, 3, b:b + 1],
                                                  member[:, b, :], ALU.add, ALU.mult)
                c(last)
                c(v.tensor_tensor(pos[:, :], count[:, 0, :], count[:, 1, :], ALU.add))
                for b in range(2, NB):
                    c(v.tensor_tensor(pos[:, :], pos[:, :], count[:, b, :], ALU.add))
                c(v.tensor_copy(posi[:, 0, :], pos[:, :]))
                c(v.tensor_scalar(posi[:, 1, :], posi[:, 0, :], 7, None, ALU.logical_shift_right))
                c(v.tensor_scalar(posi[:, 0, :], posi[:, 0, :], LANES - 1, None, ALU.bitwise_and))
                v.tensor_copy(lane[:, :, :], posi[:, :, :]).then_inc(laned, 1)
                dve.wait_ge(laned, 1)
                c(v.tensor_scalar(tb[:, :], iota[0:1, 0:ET + 3 * AHEAD], tot[0:1, 2, 1:2], None, ALU.is_ge))
                for b in range(2, NB):
                    c(v.scalar_tensor_tensor(tb[:, :], iota[0:1, 0:ET + 3 * AHEAD], tot[0:1, 2, b:b + 1], tb[:, :],
                                             ALU.is_ge, ALU.add))
                fours = lambda j: tb[:, j:j + ET].rearrange("o (i q) -> o i q", q=4)[:, :, 0]
                for half in range(2):
                    c(v.tensor_copy(tbw[:, half, :], fours(5 * half)))
                for j in range(1, 5):
                    for half in range(2):
                        c(v.scalar_tensor_tensor(tbw[:, half, :], fours(5 * half + j), float(8 ** j),
                                                 tbw[:, half, :], ALU.mult, ALU.add))
                c(v.tensor_copy(tbi[:, :, :], tbw[:, :, :]))
                c(v.tensor_scalar(tbi[:, 1, :], tbi[:, 1, :], 15, None, ALU.logical_shift_left))
                c(v.memset(k.e_blk[:, ET // 4:], 0))
                v.tensor_tensor(k.e_blk[:, 0:ET // 4], tbi[:, 0, :], tbi[:, 1, :],
                                ALU.bitwise_or).then_inc(blocks_known, 1)
                with dve.Fori(0, EC // 15) as i:
                    for n in range(15):
                        col, s = i * 15 + n, n % 5
                        dve.wait_ge(put_used[s], i * 3 + n // 5 + (1 if s < 4 else 4))
                        v.tensor_scalar(put[s][:, 0, :], iota[0:EP, 0:ET], lane[:, 1, bass.ds(col, 1)],
                                        field[:, 0, bass.ds(col, 1)], ALU.is_equal, ALU.mult)
                        v.tensor_scalar(put[s][:, 1, :], iota[0:EP, 0:ET], lane[:, 1, bass.ds(col, 1)],
                                        field[:, 1, bass.ds(col, 1)], ALU.is_equal,
                                        ALU.mult).then_inc(put_ready[s], 1)
                dve.wait_ge(sorted_, 1)
                c(v.tensor_copy(keyi[:, 0, :], P[:, 0, 0:ET]))
                c(v.tensor_copy(k.e_w[:, :], P[:, 0, ET:2 * ET]))
                c(v.tensor_scalar(keyi[:, 1, :], keyi[:, 0, :], LANES - 1, None, ALU.bitwise_and))
                c(v.tensor_scalar(keyi[:, 2, :], keyi[:, 0, :], 7, None, ALU.logical_shift_right))
                c(v.tensor_scalar(keyi[:, 3, :], keyi[:, 0, :], 10, None, ALU.logical_shift_right))
                c(v.memset(k.e_ldst[:, ET:ET + AHEAD], 0.0))
                c(v.tensor_copy(k.e_ldst[:, 0:ET], keyi[:, 1, :]))
                v.tensor_copy(k.e_src[:, :], keyi[:, 3, :])
                v.tensor_scalar(k.e_ldst[:, :], k.e_ldst[:, :], -1.0, None, ALU.add).then_inc(unpacked, 1)
                v.tensor_copy(k.e_row[:, :], keyi[:, 2, :])
                v.tensor_copy(k.e_srci[:, :], keyi[:, 3, :])
                dve.wait_ge(unpacked, 1)
                with dve.Fori(0, ET // 12) as i:
                    for n in range(12):
                        s = n % 4
                        dve.wait_ge(shot_used[s], i * 3 + n // 4 + (1 if s < 3 else 4))
                        v.tensor_scalar(shot[s][:, :], iota16[:, :], k.e_src[:, bass.ds(i * 12 + n, 1)], None,
                                        ALU.is_equal).then_inc(shot_ready[s], 1)
                dve.wait_ge(counted, 1)
                v.tensor_copy(k.C[:, :, 0:4 * NP], P[0:NP, 0:NB, 0:4 * NP])
                v.tensor_copy(k.C[:, 0:4, 4 * NP:NODES],
                              P[0:NP, 5, :].rearrange("p (b n) -> p b n", b=4)[:, :, 0:NP])
                v.tensor_copy(k.C[:, 4, 4 * NP:NODES], P[0:NP, 6, 0:NP]).then_inc(c_ready, 1)
                dve.wait_ge(c_ready, 1)
                dve.wait_ge(rest_loaded, 32)
                c(v.tensor_reduce(k.deg[:, :], k.C[:, :, 0:NODES], AX.X, ALU.add))
                c(v.memset(k.negC[:, NB, :], 0.0))
                c(v.tensor_scalar(k.negC[:, 0:NB, :], k.C[:, :, :], 0.0, NEG, ALU.is_equal, ALU.mult))
                c(v.tensor_copy(k.ident16[:, :], k.const[:, C_ID:C_ID + 128]))
                for j in range(NB):
                    dve.wait_ge(turned, j + 1)
                    q = j % 4
                    v.tensor_copy(k.CT[:, j, 0:4 * NP], P[0:NP, 2 * q, 0:4 * NP])
                    v.tensor_copy(k.CT[:, j, 4 * NP:NODES], P[0:NP, 2 * q + 1, 0:NP]).then_inc(ct_half, 1)

            @block.gpsimd
            def _(pool):
                pool.wait_ge(laned, 1)
                with pool.Fori(0, EC // 15) as i:
                    for g in range(3):
                        pool.wait_ge(put_used[4], i * 3 + g + 2)
                        nc.gpsimd.tensor_tensor(
                            hot[g][:, :, :], iota[0:EP, 0:LANES].unsqueeze(1).to_broadcast([EP, 5, LANES]),
                            lane[:, 0, bass.ds(i * 15 + g * 5, 5)].unsqueeze(2).to_broadcast([EP, 5, LANES]),
                            ALU.subtract).then_inc(lanes_far[g], 1)
                pool.wait_ge(unpacked, 1)
                with pool.Fori(0, ET // 12) as i:
                    for g in range(3):
                        pool.wait_ge(shot_used[3], i * 3 + g + 2)
                        nc.gpsimd.tensor_tensor(
                            dhot[g][:, :, :], iota[:, 0:NP].unsqueeze(1).to_broadcast([LANES, 4, NP]),
                            k.e_ldst[:, bass.ds(i * 12 + g * 4, 4)].unsqueeze(2).to_broadcast([LANES, 4, NP]),
                            ALU.subtract).then_inc(dhot_far[g], 1)

            @block.scalar
            def _(act):

                def one_hot(x, ready, n):
                    nc.scalar.activation(x, x, ACT.Square).then_inc(squared, 1)
                    act.wait_ge(squared, n)
                    nc.scalar.activation(x, x, ACT.Relu, bias=1.0, scale=-1.0).then_inc(ready, 1)

                with act.Fori(0, EC // 15) as i:
                    for g in range(3):
                        act.wait_ge(lanes_far[g], i + 1)
                        one_hot(hot[g][:, :, :], lanes_ready[g], i * 3 + g + 1)
                with act.Fori(0, ET // 12) as i:
                    for g in range(3):
                        act.wait_ge(dhot_far[g], i + 1)
                        one_hot(dhot[g][:, :, :], dhot_ready[g], i * 3 + (EC // 5 + g + 1))

            @block.tensor
            def _(pe):
                t = nc.tensor
                open_slots(pe, *put_used, *shot_used)
                pe.wait_ge(const_loaded, 16)
                pe.sem_inc(put_used[4], 3)
                pe.sem_inc(shot_used[3], 3)
                pe.wait_ge(rows, 1)
                t.matmul(P[0:EP, 0, 0:NB], k.const[0:EP, C_TRI:C_TRI + EP], tot[0:EP, 0, 0:NB], start=True, stop=True)
                t.matmul(P[:, 1, 0:NB], k.ones[0:EP, 0:128], tot[0:EP, 0, 0:NB], start=True,
                         stop=True).then_inc(prefix, 1)
                pe.wait_ge(put_ready[0], 1)
                t.matmul(P[:, 0, 0:2 * ET], k.zeros[0:1, 0:128], k.zeros[0:1, 0:2 * ET], start=True, stop=False)
                with pe.Fori(0, EC // 15) as i:
                    for n in range(15):
                        s, g = n % 5, n // 5
                        if n % 5 == 0:
                            pe.wait_ge(lanes_ready[g], i + 1)
                        pe.wait_ge(put_ready[s], i * 3 + n // 5 + 1)
                        t.matmul(P[:, 0, 0:2 * ET], hot[g][:, n % 5, :], put[s][:, :, :], start=False, stop=False,
                                 skip_group_check=True).then_inc(put_used[s], 1)
                t.matmul(P[:, 0, 0:2 * ET], k.zeros[0:1, 0:128], k.zeros[0:1, 0:2 * ET], start=False,
                         stop=True).then_inc(sorted_, 1)
                pe.wait_ge(unpacked, 1)
                for b in range(7):
                    t.matmul(P[0:NP, b, :], k.zeros16[:, 0:NP], k.zeros16[:, :], start=True, stop=False)
                pe.wait_ge(blocks_known, 1)
                words = [AheadWord(k, pe, f"edge_count_blocks{n}", 2 * n) for n in range(2)]
                with pe.Fori(0, ET // 12) as i:
                    of = (tile_blocks(k, pe, None, words[0].take())[:8] +
                          tile_blocks(k, pe, None, words[1].take())[:4])
                    for n in range(12):
                        if n in (4, 8):
                            words[n // 8].load(i * 3 + (3 + 2 * (n // 8)))
                        g, s = n // 4, n % 4
                        b = of[n]
                        if s == 0:
                            pe.wait_ge(dhot_ready[g], i + 1)
                        pe.wait_ge(shot_ready[s], i * 3 + g + 1)
                        t.matmul(k.psum_flat[0:NP, bass.ds(b * 512, 4 * NP)], dhot[g][:, s, :], shot[s][:, 0:4 * NP],
                                 start=False, stop=False, skip_group_check=True)
                        t.matmul(k.psum_flat[0:NP, bass.ds(b * 128 + 5 * 512, NP)], dhot[g][:, s, :],
                                 shot[s][:, 4 * NP:NODES], start=False, stop=False,
                                 skip_group_check=True).then_inc(shot_used[s], 1)
                for b in range(7):
                    m = t.matmul(P[0:NP, b, :], k.zeros16[:, 0:NP], k.zeros16[:, :], start=False, stop=True)
                m.then_inc(counted, 1)
                pe.wait_ge(c_ready, 1)
                for j in range(NB):
                    q = j % 4
                    if j >= 4:
                        pe.wait_ge(ct_half, j - 3)
                    for b in range(NB):
                        m = t.transpose(P[0:NP, 2 * q + b // 4, (b % 4) * NP:(b % 4 + 1) * NP],
                                        k.C[:, b, j * NP:(j + 1) * NP], k.const[0:NP, C_ID:C_ID + NP])
                    m.then_inc(turned, 1)
    k.stack = k.all




def turn(k, pe, src, bank, ready=None):
    for b in range(NB):
        if ready is not None:
            pe.wait_ge(ready, b + 1)
        for m in range(KD):
            last = k.nc.tensor.transpose(k.psum[:, bank + 2 * m + b // 4, (b % 4) * NP:(b % 4 + 1) * NP],
                                         src[:, b, m * 128:(m + 1) * 128], k.const[0:NP, C_ID:C_ID + NP])
    return last


def normalize(k, name, x, xn, xT, rms=False, weight=None, pre=None, loads=None):
    nc, P = k.nc, k.psum
    with ExitStack() as st:
        k.stack = st
        stats = k.sb(f"{name}_stats", [NP, NB, 6])
        mv = k.sb(f"{name}_mv", [NP, NB, 2])
        rs = k.sb(f"{name}_rs", [NP, 2, NB])
        sq = k.sb(f"{name}_sq", [NP, D])
        step, spread, root, normed, turned = (k.sem(f"{name}_{s}") for s in (
            "step", "var_ready", "root_ready", "normed", "turned"))
        eps = 1e-6 if rms else LN_EPS
        with nc.Block() as block:

            @block.sync
            def _(sp):
                if loads is not None:
                    loads(sp)

            @block.vector
            def _(dve):
                c, v = Chain(dve, step), nc.vector
                if pre is not None:
                    pre(dve, c)
                for b in range(NB):
                    if rms:
                        c(v.tensor_tensor_reduce(out=sq[:, :], in0=x[:, b, :], in1=x[:, b, :], scale=1.0, scalar=0.0,
                                                 op0=ALU.mult, op1=ALU.add, accum_out=mv[:, b, 1:2]))
                    else:
                        last = v.bn_stats(stats[:, b, :], x[:, b, :])
                if not rms:
                    c(last)
                    for b in range(NB):
                        last = v.bn_aggr(mv[:, b, :], stats[:, b, :])
                    c(last)
                v.tensor_scalar(rs[:, 0, :], mv[:, :, 1], 1.0 / D if rms else 1.0, eps, ALU.mult,
                                ALU.add).then_inc(spread, 1)
                dve.wait_ge(root, 1)
                c(v.reciprocal(rs[:, 0, :], rs[:, 1, :]))
                for b in range(NB):
                    if rms:
                        v.tensor_scalar(xn[:, b, :], x[:, b, :], rs[:, 0, b:b + 1], None,
                                        ALU.mult).then_inc(normed, 1)
                    else:
                        v.tensor_scalar(xn[:, b, :], x[:, b, :], mv[:, b, 0:1], rs[:, 0, b:b + 1], ALU.subtract,
                                        ALU.mult).then_inc(normed, 1)

            @block.tensor
            def _(pe):
                turn(k, pe, xn, 0, normed).then_inc(turned, 1)

            @block.scalar
            def _(act):
                a = nc.scalar
                act.wait_ge(spread, 1)
                a.activation(rs[:, 1, :], rs[:, 0, :], ACT.Sqrt).then_inc(root, 1)
                act.wait_ge(turned, 1)
                for m in range(KD):
                    scale = 1.0 if weight is None else weight[:, m:m + 1]
                    a.activation(xT[:, m, 0:4 * NP], P[:, 2 * m, 0:4 * NP], ACT.Copy, scale=scale)
                    a.activation(xT[:, m, 4 * NP:NODES], P[:, 2 * m + 1, 0:NP], ACT.Copy, scale=scale)
    k.stack = k.all


def attention(k, name, qT, kT, v, vcols, oT, neg, times, meanwhile=None):
    nc, P = k.nc, k.psum
    H, HD = 4, 64
    SC = HD ** -0.5
    with ExitStack() as st:
        k.stack = st
        qs = k.sb(f"{name}_q_block", [128, 2, KD, NP])
        top = k.sb(f"{name}_top", [NP, 2, 2])
        e = [k.sb(f"{name}_exp{s}", [NP, NC]) for s in range(2)]
        w = [k.sb(f"{name}_weights{s}", [NP, NC]) for s in range(2)]
        wT = [k.sb(f"{name}_weightsT{s}", [NP, NB, NP]) for s in range(2)]
        den = k.sb(f"{name}_den", [NP, 2, 3])
        wT_cleared = k.sem(f"{name}_wT_cleared")
        q_cleared, q_copied, top_ready, exped, weighed, divided, turned, wT_ready, step = (
            k.sem(f"{name}_{s}") for s in ("q_cleared", "q_copied", "top_ready", "exped", "weighed", "divided", "turned",
                                           "wT_ready", "attn_step"))
        scored, mixed, taken = ([k.sem(f"{name}_{n}{s}") for s in range(2)] for n in ("scored", "mixed", "taken"))
        with nc.Block() as block:

            @block.gpsimd
            def _(pool):
                nc.gpsimd.memset(qs[:, :, :, :], 0.0).then_inc(q_cleared, 1)
                pool.wait_ge(q_cleared, 1)
                for a in range(2):
                    nc.gpsimd.tensor_copy(qs[a * HD:(a + 1) * HD, a], qT[a * HD:(a + 1) * HD, :, 0:NP]
                                          ).then_inc(q_copied, 1)
                for d in range(NB):
                    pool.wait_ge(scored[1], d * 2 + 2)
                    for a in range(2):
                        nc.gpsimd.tensor_copy(qs[a * HD:(a + 1) * HD, a],
                                              qT[a * HD:(a + 1) * HD, :, (d + 1) * NP:(d + 2) * NP]
                                              ).then_inc(q_copied, 1)
                    if meanwhile is not None:
                        pool.wait_ge(q_copied, 2 * d + 4)
                        meanwhile(pool, d)

            @block.tensor
            def _(pe):
                t = nc.tensor

                def score(d, h):
                    s = h % 2
                    for half in range(2):
                        t.matmul(P[0:NP, 2 * s + half, 0:HC], qs[:, s, h // 2, :],
                                 kT[:, h // 2, half * HC:(half + 1) * HC], start=True, stop=False)
                        m = t.matmul(P[0:NP, 2 * s + half, 0:HC], k.ident16[0:NP, 0:NP],
                                     neg[:, d, half * HC:(half + 1) * HC], start=False, stop=True)
                    m.then_inc(scored[s], 1)

                def mix(h):
                    s = h % 2
                    for j in range(NB):
                        m = t.matmul(P[s * HD:(s + 1) * HD, 6 + s, 0:NP], v[:, j, vcols[h]:vcols[h] + HD],
                                     wT[s][:, j, :], start=(j == 0), stop=(j == NB - 1))
                    m.then_inc(mixed[s], 1)

                pe.wait_ge(q_copied, 2)
                score(0, 0)
                score(0, 1)
                pe.wait_ge(wT_cleared, 1)
                mix(2)
                with pe.Fori(0, NB) as d:
                    for h in range(H):
                        pe.wait_ge(exped, d * H + h + 1)
                        if h == 2:
                            pe.wait_ge(q_copied, d * 2 + 4)
                        score(d + (h + 2) // H, (h + 2) % H)
                        pe.wait_ge(wT_ready, d * H + h + 1)
                        pe.wait_ge(taken[(h + 1) % 2], d * 2 + (h + 1) // 2 + 1)
                        mix((h + 3) % H)
                        pe.wait_ge(divided, d * H + h + 1)
                        for j in range(NB):
                            m = t.transpose(P[0:NP, 4 + j // 4, (j % 4) * NP:(j % 4 + 1) * NP],
                                            w[h % 2][:, j * NP:(j + 1) * NP], k.const[0:NP, C_ID:C_ID + NP])
                        m.then_inc(turned, 1)
                pe.wait_ge(wT_ready, NB * H + 1)
                pe.wait_ge(taken[1], 2 * NB + 1)
                mix(3)

            @block.scalar
            def _(act):
                a = nc.scalar

                def exps(u, s):
                    act.wait_ge(top_ready, u + 1)
                    a.activation(e[s][:, :].rearrange("p (a n) -> p a n", a=2), P[0:NP, 2 * s:2 * s + 2, 0:HC],
                                 ACT.Exp, bias=top[:, s, 1:2], scale=SC).then_inc(exped, 1)

                open_slots(act, wT_ready)
                exps(0, 0)
                with act.Fori(0, NB) as d:
                    for h in range(H):
                        exps(d * H + h + 1, (h + 1) % 2)
                        act.wait_ge(turned, d * H + h + 1)
                        act.wait_ge(mixed[h % 2], d * 2 + h // 2 + 1)
                        a.activation(wT[h % 2][:, 0:4, :], P[0:NP, 4, 0:4 * NP].rearrange("p (j n) -> p j n", j=4),
                                     ACT.Copy)
                        a.activation(wT[h % 2][:, 4, :], P[0:NP, 5, 0:NP], ACT.Copy).then_inc(wT_ready, 1)

            @block.vector
            def _(dve):
                vec = nc.vector

                def find_top(j, s, n):
                    dve.wait_ge(scored[s], j + 1)
                    vec.tensor_reduce(top[:, s, 0:1], P[0:NP, 2 * s:2 * s + 2, 0:HC], AX.XY,
                                      ALU.max).then_inc(step, 1)
                    dve.wait_ge(step, n + 1)
                    vec.tensor_scalar(top[:, s, 1:2], top[:, s, 0:1], -SC, None, ALU.mult).then_inc(top_ready, 1)

                def add(block_, h, n):
                    s = h % 2
                    dve.wait_ge(mixed[s], n)
                    at = bass.ds(block_ * NP, NP) if not isinstance(block_, int) else \
                        slice(block_ * NP, block_ * NP + NP)
                    to = oT[s * HD:(s + 1) * HD, h // 2, at]
                    vec.tensor_tensor(to, P[s * HD:(s + 1) * HD, 6 + s, 0:NP], to, ALU.add).then_inc(taken[s], 1)

                vec.memset(wT[0][:, :, :], 0.0)
                vec.memset(wT[1][:, :, :], 0.0).then_inc(wT_cleared, 1)
                open_slots(dve, *taken)
                find_top(0, 0, 0)
                steps = 3
                with dve.Fori(0, NB) as d:
                    for h in range(H):
                        s = h % 2
                        n = d * (H * steps) + (h * steps + 1)
                        find_top(d * 2 + (h + 1) // 2, 1 - s, n)
                        dve.wait_ge(exped, d * H + h + 1)
                        vec.scalar_tensor_tensor(w[s][:, :], e[s][:, :], 1.0, times[:, d, :], ALU.mult, ALU.mult,
                                                 accum_out=den[:, s, 0:1]).then_inc(weighed, 1)
                        dve.wait_ge(weighed, d * H + h + 1)
                        vec.tensor_scalar(den[:, s, 1:2], den[:, s, 0:1], 1e-30, None, ALU.max).then_inc(step, 1)
                        dve.wait_ge(step, n + 2)
                        vec.reciprocal(den[:, s, 2:3], den[:, s, 1:2]).then_inc(step, 1)
                        dve.wait_ge(step, n + 3)
                        vec.tensor_scalar(w[s][:, :], w[s][:, :], den[:, s, 2:3], None,
                                          ALU.mult).then_inc(divided, 1)
                        add(d + h // 2, (h + 2) % H, d * 2 + h // 2 + 1)
                for h in (2, 3):
                    add(NB, h, 2 * NB + 1)
    k.stack = k.all


def conv_project(k, i, basis=None):
    nc, P = k.nc, k.psum
    name = f"conv{i}"
    loaded, product, copied, values = (k.sem(f"{name}_{s}") for s in ("bias_loaded", "product", "copied", "values"))
    w = k.wconv[:, i, :, :]
    with nc.Block() as block:

        @block.tensor
        def _(pe):
            t = nc.tensor
            pe.wait_ge(k.wconv_loaded, 16 * 12)
            for g in range(6):
                if g >= 4:
                    pe.wait_ge(copied, g - 3)
                for half in range(2):
                    for kk in range(KD):
                        m = t.matmul(P[:, 2 * (g % 4) + half, 0:HC], w[:, kk, g * 128:(g + 1) * 128],
                                     k.xT[:, kk, half * HC:(half + 1) * HC], start=(kk == 0), stop=(kk == KD - 1))
                m.then_inc(product, 1)
            pe.wait_ge(loaded, 16)
            for b in range(NB):
                pe.wait_ge(copied, 4 if b < 4 else 5)
                bank = (4 + b) % 8
                for kk in range(KD):
                    t.matmul(P[0:NP, bank, 0:D], k.xT[:, kk, b * NP:(b + 1) * NP], w[:, kk, 3 * D:4 * D],
                             start=(kk == 0), stop=False)
                t.matmul(P[0:NP, bank, 0:D], k.ones[0:1, 0:NP], k.brow[0:1, 0:D], start=False,
                         stop=True).then_inc(values, 1)

        @block.sync
        def _(sp):
            sp.dma_start(k.brow[0:1, 0:D], k.ins["L0_gnn_bv"][i:i + 1]).then_inc(loaded, 16)
            if basis is not None:
                load_basis(k, sp, basis, 0)

        @block.scalar
        def _(act):
            for g in range(6):
                act.wait_ge(product, g + 1)
                to = (k.qT, k.kT, k.oT)[g // KD][:, g % KD, 0:NC]
                nc.scalar.activation(to.rearrange("p (a n) -> p a n", a=2), P[:, 2 * (g % 4):2 * (g % 4) + 2, 0:HC],
                                     ACT.Identity, bias=col(k, "conv_bias", 6 * i + g)).then_inc(copied, 1)

        @block.vector
        def _(dve):
            for b in range(NB):
                dve.wait_ge(values, b + 1)
                nc.vector.tensor_copy(k.v[:, b, :], P[0:NP, (4 + b) % 8, 0:D])


def batch_norm(k, i):
    nc, P = k.nc, k.psum
    name = f"bn{i}"
    with ExitStack() as st:
        k.stack = st
        stats = k.sb(f"{name}_stats", [128, KD, 2, 6])
        mv = k.sb(f"{name}_mv", [128, KD, 2])
        f = k.sb(f"{name}_f", [128, 4, KD])
        spread, root, step, ready = (k.sem(f"{name}_{s}") for s in (
            "var_ready", "root_ready", "step", "affine_ready"))
        with nc.Block() as block:

            @block.vector
            def _(dve):
                c, v = Chain(dve, step), nc.vector
                for m in range(KD):
                    v.bn_stats(stats[:, m, 0, :], k.oT[:, m, 0:HC])
                    c(v.bn_stats(stats[:, m, 1, :], k.oT[:, m, HC:NODES]))
                    c(v.bn_aggr(mv[:, m, :], stats[:, m, :, :]))
                v.tensor_scalar(f[:, 0, :], mv[:, :, 1], LN_EPS, None, ALU.add).then_inc(spread, 1)
                dve.wait_ge(root, 1)
                c(v.reciprocal(f[:, 2, :], f[:, 1, :]))
                c(v.tensor_tensor(f[:, 2, :], f[:, 2, :], col(k, "bn_gamma", KD * i, KD), ALU.mult))
                c(v.tensor_tensor(f[:, 3, :], f[:, 2, :], mv[:, :, 0], ALU.mult))
                v.tensor_tensor(f[:, 3, :], col(k, "bn_beta", KD * i, KD), f[:, 3, :], ALU.subtract).then_inc(ready, 1)

            @block.scalar
            def _(act):
                a = nc.scalar
                act.wait_ge(spread, 1)
                a.activation(f[:, 1, :], f[:, 0, :], ACT.Sqrt).then_inc(root, 1)
                act.wait_ge(ready, 1)
                for m in range(KD):
                    a.activation(k.xT[:, m, 0:NODES], k.oT[:, m, 0:NODES], ACT.Relu, bias=f[:, 3, m:m + 1],
                                 scale=f[:, 2, m:m + 1])
    k.stack = k.all


def conv_layers(k):
    normalize(k, "ln_conv", k.x, k.xn, k.xT)
    mixed = k.sem("conv_basis_mixed")
    st = ExitStack()
    term = st.enter_context(k.nc.sbuf_tensor("conv_basis_term", [128, RELS // 2, D], F32))
    basis = st.enter_context(k.nc.sbuf_tensor("conv_basis", [128, RELS, KD, D], F32))

    def step(a, half, b, add):
        w = k.rgcn_w[:, a, half * RELS // 2:(half + 1) * RELS // 2, :]
        if add:
            return k.nc.gpsimd.tensor_tensor(w, w, term[:, :, :], ALU.add)
        base = basis[:, b, a, :].unsqueeze(1).to_broadcast([128, RELS // 2, D])
        factor = k.coeff[:, 0, :].rearrange("p (r b) -> p r b", b=RELS)[:, half * RELS // 2:(half + 1) * RELS // 2, b]
        return k.nc.gpsimd.tensor_tensor(w if b == 0 else term[:, :, :], base,
                                         factor.unsqueeze(2).to_broadcast([128, RELS // 2, D]), ALU.mult)

    steps = [(a, half, b, add) for a in range(KD) for half in range(2) for b in range(RELS)
             for add in range(2) if b or not add]
    share = -(-len(steps) // (3 * NB))

    def mix(pool, d):
        if d == 0:
            pool.wait_ge(k.basis_loaded, BASIS_LOADS)
        first = (i * NB + d) * share
        for n in range(first, min(first + share, len(steps))):
            assert i or steps[n][0] == 0
            step(*steps[n]).then_inc(mixed, 1)
            pool.wait_ge(mixed, n + 1)

    for i in range(3):
        conv_project(k, i, basis if i == 0 else None)
        attention(k, f"conv{i}", k.qT, k.kT, k.v, [0, 64, 128, 192], k.oT_padded, k.negC, k.C, mix)
        if i < 2:
            batch_norm(k, i)
    st.close()
    turned = k.sem("conv_out_turned")
    with k.nc.Block() as block:

        @block.tensor
        def _(pe):
            for b in range(NB):
                for m in range(KD):
                    ins = k.nc.tensor.transpose(k.psum[0:NP, b, m * 128:(m + 1) * 128],
                                                k.oT[:, m, b * NP:(b + 1) * NP], k.const[:, C_ID:C_ID + 128])
                ins.then_inc(turned, 1)

        @block.vector
        def _(dve):
            for b in range(NB):
                dve.wait_ge(turned, b + 1)
                k.nc.vector.tensor_tensor(k.x[:, b, :], k.x[:, b, :], k.psum[0:NP, b, 0:D], ALU.add)


def softmax8(k, c, v, p, small, exp_to, exp_done, exp_wait):
    n = p.shape[1]
    wide = lambda s: s.unsqueeze(2).to_broadcast([NP, n, EXPERTS])
    c(v.tensor_reduce(small[:, 0, :], p, AX.X, ALU.max))
    v.tensor_tensor(p, p, wide(small[:, 0, :]), ALU.subtract).then_inc(exp_to, 1)
    c.eng.wait_ge(exp_done, exp_wait)
    c(v.tensor_reduce(small[:, 0, :], p, AX.X, ALU.add))
    c(v.reciprocal(small[:, 1, :], small[:, 0, :]))
    c(v.tensor_tensor(p, p, wide(small[:, 1, :]), ALU.mult))


def rank8(k, c, v, p, rank, pair, tie):
    n = p.shape[1]
    tri = k.const[0:NP, C_RANK:C_ROW].rearrange("p (e f) -> p e f", e=EXPERTS)
    shape = [NP, n, EXPERTS, EXPERTS]
    mine, other = p[:, :, :].unsqueeze(3).to_broadcast(shape), p[:, :, :].unsqueeze(2).to_broadcast(shape)
    v.tensor_tensor(pair, other, mine, ALU.is_gt)
    c(v.tensor_tensor(tie, other, mine, ALU.is_equal))
    c(v.tensor_tensor(tie, tie, tri.unsqueeze(1).to_broadcast(shape), ALU.mult))
    c(v.tensor_tensor(pair, pair, tie, ALU.add))
    c(v.tensor_reduce(rank, pair[:, :, :, :], AX.X, ALU.add))


def route(k, name, xT, tiles, router, bias, top, floor):
    nc, P = k.nc, k.psum
    with ExitStack() as st:
        k.stack = st
        small = k.sb(f"{name}_small", [NP, 2, NB])
        rank = k.sb(f"{name}_rank", [NP, NB, EXPERTS])
        pair = k.sb(f"{name}_pair", [NP, NB, EXPERTS, EXPERTS])
        tie = k.sb(f"{name}_tie", [NP, NB, EXPERTS, EXPERTS])
        brow = k.sb(f"{name}_bias", [1, EXPERTS])
        loaded, logits, step, to_exp, exped = (k.sem(f"{name}_{s}") for s in (
            "bias_loaded", "logits", "step", "to_exp", "exped"))
        g = k.gate
        with nc.Block() as block:

            @block.sync
            def _(sp):
                if bias is not None:
                    sp.dma_start(brow[:, :], k.ins[bias].rearrange("(a n) -> a n", a=1)).then_inc(loaded, 16)

            @block.tensor
            def _(pe):
                t = nc.tensor
                for b in range(NB):
                    for kk in range(tiles):
                        m = t.matmul(P[0:NP, 0, b * EXPERTS:(b + 1) * EXPERTS], xT[:, kk, b * NP:(b + 1) * NP],
                                     col(k, router, kk * EXPERTS, EXPERTS), start=(kk == 0),
                                     stop=(kk == tiles - 1 and bias is None))
                    if bias is not None:
                        pe.wait_ge(loaded, 16)
                        m = t.matmul(P[0:NP, 0, b * EXPERTS:(b + 1) * EXPERTS], k.ones[0:1, 0:NP], brow[:, :],
                                     start=False, stop=True)
                m.then_inc(logits, 1)

            @block.scalar
            def _(act):
                act.wait_ge(to_exp, 1)
                nc.scalar.activation(g[:, :, :], g[:, :, :], ACT.Exp).then_inc(exped, 1)

            @block.vector
            def _(dve):
                c, v = Chain(dve, step), nc.vector
                dve.wait_ge(logits, 1)
                c(v.tensor_copy(g[:, :, :], P[0:NP, 0, 0:NB * EXPERTS].rearrange("p (b e) -> p b e", b=NB)))
                softmax8(k, c, v, g[:, :, :], small, to_exp, exped, 1)
                rank8(k, c, v, g, rank[:, :, :], pair[:, :, :, :], tie[:, :, :, :])
                c(v.tensor_scalar(rank[:, :, :], rank[:, :, :], float(top), None, ALU.is_lt))
                c(v.tensor_tensor(g[:, :, :], g[:, :, :], rank[:, :, :], ALU.mult))
                if floor is not None:
                    c(v.tensor_reduce(small[:, 0, :], g[:, :, :], AX.X, ALU.add))
                    c(v.tensor_scalar(small[:, 0, :], small[:, 0, :], floor, None, ALU.add))
                    c(v.reciprocal(small[:, 1, :], small[:, 0, :]))
                    c(v.tensor_tensor(g[:, :, :], g[:, :, :],
                                      small[:, 1, :].unsqueeze(2).to_broadcast([NP, NB, EXPERTS]), ALU.mult))
    k.stack = k.all


def cut(v, x, high, low, done):
    done(v.tensor_copy(high, x))
    return v.tensor_tensor(low, x, high.bitcast(F32), ALU.subtract)


def products3(t, to, w, x, start, stop):
    for n, (a, b) in enumerate(((0, 0), (1, 0), (0, 1))):
        last = t.matmul(to, w[a], x[b], start=start and n == 0, stop=stop and n == 2, skip_group_check=True)
    return last


class Raw:

    def __init__(self, k, name, tiles, rows, w1_of, w2_of, b2_of=None, gated=False):
        self.NW, self.PT = 2 if gated else 1, tiles // 2
        self.width = self.PT * rows
        self.w1_of, self.w2_of, self.b2_of = w1_of, w2_of, b2_of
        self.w1 = [k.sb(f"{name}_raw1_{s}", [128, self.NW, KD, self.width]) for s in range(2)]
        self.w2 = [k.sb(f"{name}_raw2_{s}", [rows, self.PT, D]) for s in range(2)]
        self.b2 = k.sb(f"{name}_b2raw", [1, 2 * D]) if b2_of is not None else None
        self.loaded = [k.sem(f"{name}_raw_loaded{s}") for s in range(2)]
        self.counts = [16 * (self.NW + 1 + (2 if b2_of is not None else 0)), 16 * (self.NW + 1)]

    def load(self, sp, e, p):
        for n in range(self.NW):
            sp.dma_start(self.w1[p][:, n], self.w1_of(sp, e, n)[:, :, p * self.width:(p + 1) * self.width]
                         ).then_inc(self.loaded[p], 16)
        sp.dma_start(self.w2[p][:, :, :], self.w2_of(sp, e)[:, p * self.PT:(p + 1) * self.PT, :]
                     ).then_inc(self.loaded[p], 16)
        if self.b2 is not None and p == 0:
            for n in range(2):
                sp.dma_start(self.b2[:, n * D:(n + 1) * D], self.b2_of(sp, e)).then_inc(self.loaded[p], 16)

    def load_first(self, sp):
        for p in range(2):
            self.load(sp, 0, p)


def experts(k, name, pairs, tiles, rows, ring, raw, acc, b1=None, affine=None, gated=False, plus=None,
            first_loaded=True):
    nc, P = k.nc, k.psum
    NW = 2 if gated else 1
    U = 1 if gated else 2
    PT = tiles // 2
    LEAD = min(ring - 2, PT)
    biased = raw.b2 is not None
    with ExitStack() as st:
        k.stack = st
        w1 = [k.sb(f"{name}_w1_{s}", [128, 2, NW, KD, rows], F32R) for s in range(ring)]
        w2 = [k.sb(f"{name}_w2_{s}", [rows, 2, D], F32R) for s in range(ring)]
        xs = 2 if affine else 1
        xe = [k.sb(f"{name}_x_{s}", [128, 2, KD, WC], F32R) for s in range(xs)]
        x = k.sb(f"{name}_x", [128, KD, NC]) if affine else k.xT
        g = [k.sb(f"{name}_g{s}", [rows, WC]) for s in range(2)]
        h = [k.sb(f"{name}_product{s}", [rows, WC]) for s in range(2)] if gated else None
        hT = [k.sb(f"{name}_hT{s}", [rows, 2, WC], F32R) for s in range(2)]
        one = k.sb(f"{name}_one", [1, NP], F32R)
        if biased:
            b2 = k.sb(f"{name}_b2", [1, 2, 2 * D], F32R)
        two = lambda n: [k.sem(f"{name}_{n}{s}") for s in range(2)]
        raw_used, h_ready, x_ready = (two(n) for n in ("raw_used", "h_ready", "x_ready"))
        up_given, up_taken = ([k.sem(f"{name}_{n}{s}") for s in range(U)] for n in ("up_given", "up_taken"))
        w_high, w_ready, step_done = ([k.sem(f"{name}_{n}{s}") for s in range(ring)] for n in (
            "w_high", "w_ready", "step_done"))
        weight_part, high_part, activated, up3_given, up3_taken, output_taken, cleared, b2_used = (k.sem(f"{name}_{n}") for n in (
            "weight_part", "high_part", "activated", "up3_given", "up3_taken", "output_taken", "cleared",
            "b2_used"))

        def nth(i, s, m, slots):
            return (i * 2 + s) * (tiles // slots) + m // slots

        def acc_of(b):
            return P[0:NP, 4 + b // 2, (b % 2) * D:(b % 2 + 1) * D]

        with nc.Block() as block:

            @block.sync
            def _(sp):
                if not first_loaded:
                    raw.load_first(sp)
                with sp.Fori(0, pairs) as i:
                    for s in range(2):
                        e = i * 2 + s
                        for p in range(2):
                            sp.wait_ge(raw_used[p], e + 1)
                            if biased and p == 0:
                                sp.wait_ge(b2_used, e + 1)
                            raw.load(sp, (e + 1) % (2 * pairs), p)
                for p in range(2):
                    sp.wait_ge(raw.loaded[p], (2 * pairs + 1) * raw.counts[p])

            @block.gpsimd
            def _(pool):
                v = nc.gpsimd
                with pool.Fori(0, pairs) as i:
                    for s in range(2):
                        e, n = i * 2 + s, 0

                        def done(ins):
                            nonlocal n
                            n += 1
                            ins.then_inc(weight_part, 1)
                            pool.wait_ge(weight_part, e * tiles + n)

                        for m in range(tiles):
                            p, c = m // PT, m % ring
                            pool.wait_ge(w_high[c], nth(i, s, m, ring) + 1)
                            at = m % PT
                            done(v.tensor_tensor(w1[c][:, 1], raw.w1[p][:, :, :, at * rows:(at + 1) * rows],
                                                 w1[c][:, 0].bitcast(F32), ALU.subtract))
                            v.tensor_tensor(w2[c][:, 1, :], raw.w2[p][:, at, :], w2[c][:, 0, :].bitcast(F32),
                                            ALU.subtract).then_inc(w_ready[c], 1)
                            pool.wait_ge(w_ready[c], nth(i, s, m, ring) + 1)
                            if at == PT - 1:
                                pool.sem_inc(raw_used[p], 1)

            @block.tensor
            def _(pe):
                t = nc.tensor

                def down(m, ready):
                    pe.wait_ge(h_ready[m % 2], ready)
                    hidden, w = hT[m % 2], w2[m % ring]
                    for b in range(NB):
                        last = products3(t, acc_of(b), [hidden[:, n, b * NP:(b + 1) * NP] for n in range(2)],
                                         [w[:, n, :] for n in range(2)], False, False)
                    if m == tiles - 1:
                        for b in range(3):
                            last = t.matmul(P[0:NP, 4 + b, :], k.zeros16[:, 0:NP], k.zeros16[:, :], start=False, stop=True)
                    last.then_inc(step_done[m % ring], 1)

                open_slots(pe, *step_done[:ring - 1])
                pe.wait_ge(cleared, 1)
                for b in range(3):
                    t.matmul(P[0:NP, 4 + b, :], k.zeros16[:, 0:NP], k.zeros16[:, :], start=True, stop=False)
                if not affine:
                    pe.wait_ge(x_ready[0], 1)
                with pe.Fori(0, pairs) as i:
                    for s in range(2):
                        if affine:
                            pe.wait_ge(x_ready[s], i + 1)
                        xp = xe[s] if affine else xe[0]
                        for m in range(tiles):
                            q, c = m % U, m % ring
                            pe.wait_ge(w_ready[c], nth(i, s, m, ring) + 1)
                            for n in range(NW):
                                pe.wait_ge(up3_taken if n else up_taken[q], nth(i, s, m, U) + 1)
                                for a in range(2):
                                    for kk in range(KD):
                                        last = products3(
                                            t, P[0:rows, 2 * (n + q) + a, 0:WC // 2],
                                            [w1[c][:, r, n, kk, :] for r in range(2)],
                                            [xp[:, r, kk, a * WC // 2:(a + 1) * WC // 2] for r in range(2)],
                                            kk == 0, kk == KD - 1)
                                last.then_inc(up3_given if n else up_given[q], 1)
                            if m == 2:
                                pe.wait_ge(output_taken, i * 2 + s + 1)
                                for b in range(3):
                                    if not biased:
                                        t.matmul(P[0:NP, 4 + b, :], k.zeros16[:, 0:NP], k.zeros16[:, :], start=True, stop=False)
                                    else:
                                        for r in range(2):
                                            t.matmul(P[0:NP, 4 + b, :], one[:, :], b2[:, r, :], start=(r == 0),
                                                     stop=False)
                            for n in {1: (), 2: (0, 1)}.get(m, (m - 1,)):
                                down(n % tiles, nth(i, s, n + 2, 2) + 1)
                down(tiles - 1, pairs * tiles + 1)

            @block.scalar
            def _(act):
                open_slots(act, *up_taken)
                with act.Fori(0, pairs) as i:
                    for s in range(2):
                        for m in range(tiles):
                            q = m % U
                            act.wait_ge(up_given[q], nth(i, s, m, U) + 1)
                            act.wait_ge(h_ready[m % 2], nth(i, s, m, 2) + 1)
                            nc.scalar.activation(g[m % 2][:, :].rearrange("p (a n) -> p a n", a=2),
                                                 P[0:rows, 2 * q:2 * q + 2, 0:WC // 2], ACT.Silu if gated else ACT.Gelu,
                                                 bias=0.0 if gated else b1(i * 2 + s, m)).then_inc(up_taken[q], 1)

            @block.vector
            def _(dve):
                v = nc.vector
                cuts = KD if affine else 0

                def done(ins, count):
                    ins.then_inc(high_part, 1)
                    dve.wait_ge(high_part, count)

                def make_x(e, slot, kk, count):
                    done(v.tensor_scalar(x[:, kk, :], k.xT[:, kk, :], col(k, affine[0], e + kk * (EXPERTS + 1)),
                                         col(k, affine[1], e + kk * (EXPERTS + 1)), ALU.mult, ALU.add), count - 1)
                    return cut(v, x[:, kk, :], xe[slot][:, 0, kk, 0:NC], xe[slot][:, 1, kk, 0:NC],
                               lambda ins: done(ins, count))

                def high_weights(e, m):
                    p, c, at = m // PT, m % ring, m % PT
                    dve.wait_ge(raw.loaded[p], e * raw.counts[p] + raw.counts[p])
                    v.tensor_copy(w1[c][:, 0], raw.w1[p][:, :, :, at * rows:(at + 1) * rows])
                    v.tensor_copy(w2[c][:, 0, :], raw.w2[p][:, at, :]).then_inc(w_high[c], 1)

                def cut_bias(count):
                    cut(v, raw.b2[:, :], b2[:, 0, :], b2[:, 1, :], lambda ins: done(ins, count)).then_inc(b2_used, 1)

                def read_output(e, column):
                    dve.wait_ge(step_done[ring - 1], e * (tiles // ring) + 1)
                    for b in range(NB):
                        last = v.scalar_tensor_tensor(acc[:, b, :], acc_of(b), column(b), acc[:, b, :], ALU.mult,
                                                      ALU.add)
                    last.then_inc(output_taken, 1)

                open_slots(dve, h_ready[0])
                if gated:
                    open_slots(dve, up3_taken)
                if acc is k.x:
                    if plus is not None:
                        v.tensor_tensor(acc[:, :, :], acc[:, :, :], plus[:, :, :], ALU.add)
                else:
                    v.memset(acc[:, :, :], 0.0)
                for r in range(2):
                    v.tensor_copy(w2[ring - 1][:, r, :], k.zeros[0:rows, 0:D])
                    v.tensor_copy(hT[1][:, r, 0:WC // 2], k.zeros[0:rows, 0:WC // 2])
                    v.tensor_copy(hT[1][:, r, WC // 2:WC], k.zeros[0:rows, 0:WC // 2])
                    for xp in xe:
                        v.tensor_copy(xp[:, r, :, NC:WC], k.zeros[:, 0:KD * (WC - NC)].rearrange(
                            "p (a n) -> p a n", a=KD))
                v.tensor_copy(one[:, :], k.ones[0:1, 0:NP]).then_inc(cleared, 1)
                dve.wait_ge(cleared, 1)
                dve.sem_inc(h_ready[1], 1)
                for m in range(LEAD):
                    high_weights(0, m)
                ahead = (2 * KD if affine else KD) + biased
                for kk in range(KD):
                    if affine:
                        last = make_x(0, 0, kk, 2 * kk + 2)
                    else:
                        last = cut(v, x[:, kk, :], xe[0][:, 0, kk, 0:NC], xe[0][:, 1, kk, 0:NC],
                                   lambda ins: done(ins, kk + 1))
                last.then_inc(x_ready[0], 1)
                if biased:
                    cut_bias(ahead)
                with dve.Fori(0, pairs) as i:
                    for s in range(2):
                        n = 0
                        per = tiles + 2 * cuts + (1 if biased else 0)
                        for m in range(tiles):
                            q = m % 2
                            dve.wait_ge(up_taken[m % U], nth(i, s, m, U) + 2)
                            dve.wait_ge(step_done[(m - 2) % ring], nth(i, s, m - 2, ring) + 2)
                            tile = g[q][:, :]
                            if gated:
                                dve.wait_ge(up3_given, nth(i, s, m, 1) + 1)
                                v.tensor_tensor(h[q][:, :].rearrange("p (a n) -> p a n", a=2), P[0:rows, 2:4, 0:WC // 2],
                                                tile.rearrange("p (a n) -> p a n", a=2), ALU.mult
                                                ).then_inc(up3_taken, 1)
                                dve.wait_ge(up3_taken, nth(i, s, m, 1) + 2)
                                tile = h[q][:, :]
                            n += 1
                            count = (i * 2 + s) * per + (ahead + n)
                            cut(v, tile, hT[q][:, 0, :], hT[q][:, 1, :],
                                lambda ins: done(ins, count)).then_inc(h_ready[q], 1)
                            far = m + LEAD
                            high_weights(i * 2 + (s + far // tiles), far % tiles)
                            if biased and far == tiles:
                                n += 1
                                cut_bias((i * 2 + s) * per + (ahead + n))
                            if m == 0:
                                read_output(i * 2 + s, lambda b: k.gate_before[:, b, bass.ds(i * 2 + s, 1)])
                            if affine and m in (3, 5):
                                n += 2
                                ins = make_x(i * 2 + s + 1, 1 - s, (m - 3) // 2, (i * 2 + s) * per + (ahead + n))
                                if m == 5:
                                    ins.then_inc(x_ready[1 - s], 1)
                read_output(2 * pairs, lambda b: k.gate[:, b, 2 * pairs - 1:2 * pairs])
    k.stack = k.all


def moe0(k):
    with ExitStack() as st:
        k.stack = st
        raw = Raw(k, "moe0", 8, 128,
                  lambda sp, e, n: k.ins["L0_ffn_W1"][bass.ds(e, 1)].rearrange("o (a p) n -> p (o a) n", p=128),
                  lambda sp, e: k.ins["L0_ffn_W2"][bass.ds(e, 1)].rearrange("o (a p) n -> p (o a) n", p=128),
                  lambda sp, e: k.ins["L0_ffn_b2"][bass.ds(e, 1), :])
        normalize(k, "ln_moe0", k.x, k.xn, k.xT, loads=raw.load_first)
        route(k, "moe0_route", k.xT, KD, "moe0_router", "L0_ffn_br", 2, 0.0)
        normalize(k, "ln_moe0_inner", k.xn, k.xn, k.xT)
        experts(k, "moe0", EXPERTS // 2, 8, 128, 4, raw, k.x, lambda e, m: col(k, "moe0_b1", e * 8 + m),
                ("moe0_ln_g", "moe0_ln_b"))


def sage(k):
    nc, P = k.nc, k.psum
    with ExitStack() as st:
        k.stack = st
        w = k.sb("sage_w", [128, 2, KD, D])
        brow = k.sb("sage_b", [1, D])
        loaded = k.sem("sage_loaded")

        def loads(sp):
            for n, m in enumerate(("W_self", "W_neigh")):
                sp.dma_start(w[:, n], k.ins[f"L1_gnn_{m}"].rearrange("(a p) n -> p a n", p=128)).then_inc(loaded, 16)
            sp.dma_start(brow[:, :], k.ins["L1_gnn_b"].rearrange("(a n) -> a n", a=1)).then_inc(loaded, 16)

        normalize(k, "ln_sage", k.x, k.xn, k.xT, loads=loads)
        k.stack = st
        aggT = k.sb("sage_aggT", [128, KD, NC])
        rdeg = k.sb("sage_rdeg", [NP, 2, NB])
        z = k.sb("sage_z", [NP, NB, D])
        agg, agg_ready, own, neigh, step = (k.sem(f"sage_{s}") for s in (
            "agg", "agg_copied", "own_products", "neighbour_products", "step"))
        with nc.Block() as block:

            @block.tensor
            def _(pe):
                t = nc.tensor
                for m in range(KD):
                    for a in range(2):
                        for j in range(NB):
                            ins = t.matmul(P[:, 2 * m + a, 0:HC], k.xn[:, j, m * 128:(m + 1) * 128],
                                           k.CT[:, j, a * HC:(a + 1) * HC], start=(j == 0), stop=(j == NB - 1))
                    ins.then_inc(agg, 1)
                pe.wait_ge(loaded, 16 * 3)
                for b in range(NB):
                    q = b % 2
                    if b >= 2:
                        pe.wait_ge(step, b - 1)
                    for kk in range(KD):
                        t.matmul(P[0:NP, 4 + q, 0:D], k.xT[:, kk, b * NP:(b + 1) * NP], w[:, 0, kk, :],
                                 start=(kk == 0), stop=False)
                    t.matmul(P[0:NP, 4 + q, 0:D], k.ones[0:1, 0:NP], brow[:, :], start=False,
                             stop=True).then_inc(own, 1)
                    pe.wait_ge(agg_ready, KD)
                    for kk in range(KD):
                        ins = t.matmul(P[0:NP, 6 + q, 0:D], aggT[:, kk, b * NP:(b + 1) * NP], w[:, 1, kk, :],
                                       start=(kk == 0), stop=(kk == KD - 1))
                    ins.then_inc(neigh, 1)

            @block.scalar
            def _(act):
                for m in range(KD):
                    act.wait_ge(agg, m + 1)
                    nc.scalar.activation(aggT[:, m, :].rearrange("p (a n) -> p a n", a=2),
                                         P[:, 2 * m:2 * m + 2, 0:HC], ACT.Copy).then_inc(agg_ready, 1)

            @block.vector
            def _(dve):
                v = nc.vector
                c = Chain(dve, k.sem("sage_chain"))
                c(v.tensor_scalar(rdeg[:, 0, :], k.deg[:, :], 1.0, None, ALU.max))
                c(v.reciprocal(rdeg[:, 1, :], rdeg[:, 0, :]))
                for b in range(NB):
                    dve.wait_ge(neigh, b + 1)
                    dve.wait_ge(own, b + 1)
                    c(v.tensor_scalar(z[:, b, :], P[0:NP, 6 + b % 2, 0:D], rdeg[:, 1, b:b + 1], None, ALU.mult))
                    v.tensor_tensor(z[:, b, :], z[:, b, :], P[0:NP, 4 + b % 2, 0:D], ALU.add).then_inc(step, 1)
                    dve.wait_ge(step, b + 1)
                    v.scalar_tensor_tensor(k.x[:, b, :], z[:, b, :], 0.0, k.x[:, b, :], ALU.max, ALU.add)
    k.stack = k.all


def route_graph(k):
    nc, P = k.nc, k.psum
    CAPACITY = -(-NODES * 5 // (4 * EXPERTS))
    with ExitStack() as st:
        k.stack = st
        mean = k.sb("moe1_mean", [128, KD])
        means = k.sb("moe1_means", [128, KD, NP])
        p = k.sb("moe1_p", [NP, 1, EXPERTS])
        f = k.sb("moe1_f", [NP, 1, EXPERTS])
        small = k.sb("moe1_small", [NP, 2, 1])
        rank = k.sb("moe1_rank", [NP, 1, EXPERTS])
        pair = k.sb("moe1_pair", [NP, 1, EXPERTS, EXPERTS])
        tie = k.sb("moe1_tie", [NP, 1, EXPERTS, EXPERTS])
        pick = k.sb("moe1_pick", [NP, EXPERTS])
        junk = k.sb("moe1_junk", [NP, EXPERTS])
        val = k.sb("moe1_val", [NP, 6])
        brow = k.sb("moe1_brow", [1, EXPERTS])
        loaded, mean_ready, logits, step, to_exp, exped, picked, bias_loaded = (k.sem(f"moe1_{s}") for s in (
            "loaded", "mean_ready", "logits", "step", "to_exp", "exped", "picked", "picked_bias_loaded"))
        with nc.Block() as block:

            @block.sync
            def _(sp):
                sp.dma_start(brow[:, :], k.ins["L1_ffn_br"].rearrange("(a n) -> a n", a=1)).then_inc(loaded, 16)
                sp.wait_ge(picked, 1)
                for s in range(2):
                    e = sp.value_load(k.picked[0:1, s:s + 1], min_val=0, max_val=EXPERTS - 1)
                    sp.dma_start(k.picked_b1[:, s * 4:(s + 1) * 4],
                                 k.ins["moe1_b1"][bass.ds(e, 1)].rearrange("o p m -> p (o m)")
                                 ).then_inc(bias_loaded, 16)
                sp.wait_ge(bias_loaded, 32)

            @block.tensor
            def _(pe):
                t = nc.tensor
                pe.wait_ge(mean_ready, 1)
                pe.wait_ge(loaded, 16)
                for kk in range(KD):
                    t.matmul(P[0:NP, 0, 0:EXPERTS], means[:, kk, :], col(k, "moe1_router", kk * EXPERTS, EXPERTS),
                             start=(kk == 0), stop=False)
                t.matmul(P[0:NP, 0, 0:EXPERTS], k.ones[0:1, 0:NP], brow[:, :], start=False,
                         stop=True).then_inc(logits, 1)

            @block.scalar
            def _(act):
                a = nc.scalar
                for n in range(2):
                    act.wait_ge(to_exp, n + 1)
                    a.activation(p[:, 0, :], p[:, 0, :], ACT.Exp).then_inc(exped, 1)
                act.wait_ge(to_exp, 3)
                a.activation(val[:, 3:4], val[:, 2:3], ACT.Exp).then_inc(exped, 1)

            @block.vector
            def _(dve):
                c, v = Chain(dve, step), nc.vector
                c(v.tensor_reduce(mean[:, :], k.xT[:, :, 0:NODES], AX.X, ALU.add))
                c(v.tensor_scalar(mean[:, :], mean[:, :], 1.0 / NODES, None, ALU.mult))
                for kk in range(KD):
                    ins = v.tensor_scalar(means[:, kk, :], k.ones[:, 0:NP], mean[:, kk:kk + 1], None, ALU.mult)
                    c(ins)
                v.memset(junk[:, :], 0.0).then_inc(mean_ready, 1)
                dve.wait_ge(mean_ready, 1)
                dve.wait_ge(logits, 1)
                c(v.tensor_copy(p[:, 0, :], P[0:NP, 0, 0:EXPERTS]))
                softmax8(k, c, v, p[:, :, :], small, to_exp, exped, 1)
                c(v.tensor_scalar(f[:, 0, :], p[:, 0, :], float(NODES), 1e-30, ALU.mult, ALU.max))
                c(v.reciprocal(f[:, 0, :], f[:, 0, :]))
                c(v.tensor_scalar(f[:, 0, :], f[:, 0, :], float(CAPACITY), 1.0, ALU.mult, ALU.min))
                c(v.tensor_tensor(p[:, 0, :], p[:, 0, :], f[:, 0, :], ALU.mult))
                softmax8(k, c, v, p[:, :, :], small, to_exp, exped, 2)
                rank8(k, c, v, p, rank[:, :, :], pair[:, :, :, :], tie[:, :, :, :])
                for s in range(2):
                    c(v.tensor_scalar(pick[:, :], rank[:, 0, :], float(s), None, ALU.is_equal))
                    for n, what in enumerate((p[:, 0, :], k.const[0:NP, C_IOTA:C_IOTA + EXPERTS])):
                        c(v.tensor_tensor(junk[:, :], pick[:, :], what, ALU.mult))
                        c(v.tensor_reduce(val[:, s + 4 * n:s + 4 * n + 1], junk[:, :], AX.X, ALU.add))
                v.tensor_copy(k.picked[0:1, :], val[0:1, 4:6]).then_inc(picked, 1)
                v.tensor_tensor(val[:, 2:3], val[:, 1:2], val[:, 0:1], ALU.subtract).then_inc(to_exp, 1)
                dve.wait_ge(exped, 3)
                c(v.tensor_scalar(val[:, 2:3], val[:, 3:4], 1.0, None, ALU.add))
                c(v.reciprocal(val[:, 0:1], val[:, 2:3]))
                c(v.tensor_tensor(val[:, 1:2], val[:, 3:4], val[:, 0:1], ALU.mult))
                c(v.tensor_copy(k.gate[:, :, 0:2], val[:, 0:2].unsqueeze(1).to_broadcast([NP, NB, 2])))
    k.stack = k.all


def moe1(k):
    nc = k.nc
    normalize(k, "ln_moe1", k.x, k.xn, k.xT)
    route_graph(k)
    hidden = 4

    def expert(sp, e):
        return sp.value_load(k.picked[0:1, bass.ds(e, 1)], min_val=0, max_val=EXPERTS - 1)

    with ExitStack() as st:
        k.stack = st
        raw = Raw(k, "moe1", hidden, 128,
                  lambda sp, e, n: k.ins["L1_ffn_W1"][bass.ds(expert(sp, e), 1)].rearrange(
                      "o (a p) n -> p (o a) n", p=128),
                  lambda sp, e: k.ins["L1_ffn_W2"][bass.ds(expert(sp, e), 1)].rearrange(
                      "o (a p) n -> p (o a) n", p=128),
                  lambda sp, e: k.ins["L1_ffn_b2"][bass.ds(expert(sp, e), 1), :])
        experts(k, "moe1", 1, hidden, 128, 4, raw, k.o, lambda e, m: k.picked_b1[:, bass.ds(e * hidden + m, 1)],
                first_loaded=False)

    def add_tokens(dve, c):
        c(nc.vector.tensor_tensor(k.o[:, :, :], k.o[:, :, :], k.xn[:, :, :], ALU.add))

    normalize(k, "ln_moe1_out", k.o, k.o, k.xT, pre=add_tokens)
    with ExitStack() as st:
        k.stack = st
        par = k.sb("moe1_par", [NP, 2, D])
        loaded, step = k.sem("moe1_par_loaded"), k.sem("moe1_out_step")
        with nc.Block() as block:

            @block.sync
            def _(sp):
                sp.dma_start(par[:, 0, :], k.ins["moe1_gamma"]).then_inc(loaded, 16)
                sp.dma_start(par[:, 1, :], k.ins["moe1_beta"]).then_inc(loaded, 16)

            @block.vector
            def _(dve):
                c, v = Chain(dve, step), nc.vector
                wide = lambda n: par[:, n, :].unsqueeze(1).to_broadcast([NP, NB, D])
                dve.wait_ge(loaded, 32)
                c(v.tensor_tensor(k.o[:, :, :], k.o[:, :, :], wide(0), ALU.mult))
                c(v.tensor_tensor(k.o[:, :, :], k.o[:, :, :], wide(1), ALU.add))
                c(v.tensor_tensor(k.x[:, :, :], k.x[:, :, :], k.o[:, :, :], ALU.add))
    k.stack = k.all


def gather_tiles(k, pool, index, idx, idx_ready, idx_seen, free, rows, table, gathered):
    with pool.Fori(0, ET // 8) as i:
        for g in range(2):
            nc = k.nc
            nc.gpsimd.tensor_copy(idx[g][:, :], index[:, bass.ds(i * 8 + g * 4, 4)]).then_inc(idx_ready, 1)
            pool.wait_ge(idx_ready, i * 2 + g + 1)
            for s in range(4):
                pool.wait_ge(free[s], i * 2 + g + 1)
                pool.sem_inc(idx_seen, 1)
                nc.gpsimd.indirect_dma_start(
                    out=rows[s][:, :], out_offset=None, in_=table,
                    in_offset=bass.IndirectOffsetOnAxis(ap=idx[g][:, s:s + 1], axis=0)).then_inc(gathered[s], 16)


def rgcn_layer(k, l):
    nc, P = k.nc, k.psum
    name = f"rgcn{l}"
    with ExitStack() as st:
        k.stack = st
        w = k.rgcn_w
        wp = k.sb(f"{name}_w_parts", [128, 2, KD, RELS, D], F32R)
        xp = k.sb(f"{name}_x_parts", [128, 2, KD, NC], F32R)
        basis = k.sb(f"{name}_basis", [128, RELS, KD, D]) if l == 0 else None
        ah = [k.sb(f"{name}_all_h{s}", [NP, RELS * D]) for s in range(2)]
        brow = k.sb(f"{name}_bias", [1, 2 * D])
        idx = [k.sb(f"{name}_idx{s}", [LANES, 4], U32) for s in range(2)]
        rows = [k.sb(f"{name}_rows{s}", [LANES, D]) for s in range(4)]
        hot = [k.sb(f"{name}_hot{s}", [LANES, NP]) for s in range(4)]
        loaded, mixed, high_part, parts_ready, products, copied, whole = (k.sem(f"{name}_{s}") for s in (
            "loaded", "basis_mixed", "high_part", "parts_ready", "products", "copied", "summed"))
        idx_ready, idx_seen = k.sem(f"{name}_idx_ready"), k.sem(f"{name}_idx_seen")
        stored = [k.sem(f"{name}_stored{s}") for s in range(2)]
        four = lambda n: [k.sem(f"{name}_{n}{s}") for s in range(4)]
        gathered, hot_ready, used = (four(n) for n in ("gathered", "hot_ready", "used"))
        table = k.tables[:, 0:RELS * D]
        with nc.Block() as block:

            @block.sync
            def _(sp):
                sp.dma_start(brow[0:1, 0:D], k.ins["L2_gnn_bias"][l:l + 1]).then_inc(loaded, 16)
                sp.dma_start(brow[0:1, D:2 * D], k.ins["L2_gnn_bias"][l:l + 1]).then_inc(loaded, 16)
                if l == 0:
                    load_basis(k, sp, basis, 1)
                for b in range(NB):
                    for q in range(4):
                        part = slice(q * 2 * D, (q + 1) * 2 * D)
                        sp.wait_ge(copied, 4 * b + q + 1)
                        sp.dma_start(table[b * NP:(b + 1) * NP, part], ah[b % 2][:, part]).then_inc(stored[b % 2], 16)

            @block.gpsimd
            def _(pool):
                pool.wait_ge(stored[0], 16 * 4 * 3)
                pool.wait_ge(stored[1], 16 * 4 * 2)
                gather_tiles(k, pool, k.e_row, idx, idx_ready, idx_seen, used, rows, k.table_rows, gathered)

            @block.vector
            def _(dve):
                v, c = nc.vector, Chain(dve, high_part)
                cut(v, k.xT[:, :, :], xp[:, 0], xp[:, 1], c)
                for q in range(4):
                    pair = slice(2 * q, 2 * q + 2)
                    cut(v, w[:, :, pair, :], wp[:, 0, :, pair, :], wp[:, 1, :, pair, :], c).then_inc(parts_ready, 1)
                for b in range(NB):
                    if b >= 2:
                        dve.wait_ge(stored[b % 2], 16 * 4 * (b // 2))
                    for q in range(4):
                        dve.wait_ge(products, 4 * b + q + 1)
                        v.tensor_copy(ah[b % 2][:, q * 2 * D:(q + 1) * 2 * D], P[0:NP, q, :]).then_inc(copied, 1)

                def onehots(i):
                    for s in range(4):
                        at = bass.ds(i * 4 + s, 1)
                        dve.wait_ge(used[s], i + 1)
                        v.tensor_scalar(hot[s][:, :], k.const[:, C_IOTA:C_IOTA + NP], k.e_ldst[:, at],
                                        k.e_w[:, at], ALU.is_equal, ALU.mult).then_inc(hot_ready[s], 1)

                beside = 4 * RELS if l == 0 else 0
                if l == 0:
                    dve.wait_ge(k.basis_loaded, BASIS_LOADS + 16 * RELS)
                    with dve.Fori(0, RELS) as r:
                        for q in range(4):
                            onehots(r * 4 + q)
                            for b in range(2 * q, 2 * q + 2):
                                mix_basis(k, v, basis, w, 1, r, b).then_inc(mixed, 1)
                                dve.wait_ge(mixed, r * RELS + b + 1)
                with dve.Fori(beside, ET // 4) as i:
                    onehots(i)
                dve.wait_ge(whole, 1)
                for b in range(NB):
                    sums = P[0:NP, 4 + b // 2, (b % 2) * D:(b % 2 + 1) * D]
                    if l == 0:
                        v.tensor_scalar(k.o[:, b, :], sums, 0.0, None, ALU.max)
                    else:
                        v.tensor_tensor(k.x[:, b, :], k.x[:, b, :], sums, ALU.add)

            @block.tensor
            def _(pe):
                t = nc.tensor
                open_slots(pe, *used)
                for b in range(NB):
                    for q in range(4):
                        if b:
                            pe.wait_ge(copied, 4 * (b - 1) + q + 1)
                        else:
                            pe.wait_ge(parts_ready, q + 1)
                        for kk in range(KD):
                            m = products3(t, P[0:NP, q, :], [xp[:, r, kk, b * NP:(b + 1) * NP] for r in range(2)],
                                          [wp[:, r, kk, 2 * q:2 * q + 2, :] for r in range(2)], kk == 0, kk == KD - 1)
                        m.then_inc(products, 1)
                pe.wait_ge(loaded, 32)
                for q in range(3):
                    t.matmul(P[0:NP, 4 + q, :], k.ones[0:1, 0:NP], brow[0:1, :], start=True, stop=False)
                with pe.Fori(0, ET // 4) as i:
                    of = tile_blocks(k, pe, i)
                    for s in range(4):
                        b = of[s]
                        pe.wait_ge(hot_ready[s], i + 1)
                        pe.wait_ge(gathered[s], i * 16 + 16)
                        t.matmul(k.psum_flat[0:NP, bass.ds(b * D + 4 * 512, D)], hot[s][:, :], rows[s][:, :],
                                 start=False, stop=False, skip_group_check=True).then_inc(used[s], 1)
                for q in range(3):
                    m = t.matmul(P[0:NP, 4 + q, :], k.zeros16[:, 0:NP], k.zeros16[:, :], start=False, stop=True)
                m.then_inc(whole, 1)
    k.stack = k.all


def turn_o(k, name, src):
    nc, P = k.nc, k.psum
    turned = k.sem(f"{name}_turned")
    with nc.Block() as block:

        @block.tensor
        def _(pe):
            turn(k, pe, src, 0).then_inc(turned, 1)

        @block.scalar
        def _(act):
            act.wait_ge(turned, 1)
            for m in range(KD):
                nc.scalar.activation(k.xT[:, m, 0:4 * NP], P[:, 2 * m, 0:4 * NP], ACT.Copy)
                nc.scalar.activation(k.xT[:, m, 4 * NP:NODES], P[:, 2 * m + 1, 0:NP], ACT.Copy)


def rgcn(k):
    normalize(k, "ln_rgcn", k.x, k.xn, k.xT)
    rgcn_layer(k, 0)
    turn_o(k, "rgcn_mid", k.o)
    rgcn_layer(k, 1)


def moe2_attention(k):
    nc, P = k.nc, k.psum
    with ExitStack() as outer:
        k.stack = outer
        wo = k.sb("wo", [128, KD, D])
        wo_loaded = k.sem("wo_loaded")
        causal = k.sb("causal", [NP, NB, NC])
        neg = k.sb("causal_neg", [NP, NB + 1, NC], BF16)
        with ExitStack() as st:
            k.stack = st
            w = k.sb("rope_w", [128, 4, KD, D])
            wv = k.sb("rope_wv", [128, KD, D // 2])
            rope = k.sb("rope_tables", [128, 2, NC])
            loaded = k.sem("rope_loaded")

            def loads(sp):
                sp.dma_start(rope[:, :, :], k.ins["rope"]).then_inc(loaded, 16)
                for n, m in enumerate(("rope_wq", "rope_wq_swapped", "rope_wk", "rope_wk_swapped")):
                    sp.dma_start(w[:, n], k.ins[m].rearrange("(a p) n -> p a n", p=128)).then_inc(loaded, 16)
                sp.dma_start(wv[:, :, :], k.ins["moe2_wv"].rearrange("(a p) n -> p a n", p=128)).then_inc(loaded, 16)
                sp.dma_start(wo[:, :, :], k.ins["moe2_wo"].rearrange("(a p) n -> p a n", p=128)
                             ).then_inc(wo_loaded, 16)

            normalize(k, "ln_moe2", k.x, k.xn, k.xT, loads=loads)
            normalize(k, "rms1", k.xn, k.o, k.xT, rms=True, weight=col(k, "ln1_w", 0, KD))
            k.stack = st
            part = k.sb("rope_part", [128, 2, NC])
            raw, raw_taken, step, vs = (k.sem(f"rope_{s}") for s in (
                "products", "products_taken", "step", "v_products"))
            with nc.Block() as block:

                @block.tensor
                def _(pe):
                    t = nc.tensor
                    pe.wait_ge(loaded, 16 * 6)
                    for g in range(4):
                        at = 4 * (g % 2)
                        if g >= 2:
                            pe.wait_ge(raw_taken, g - 1)
                        for n in range(2):
                            for a in range(2):
                                for kk in range(KD):
                                    m = t.matmul(P[:, at + 2 * n + a, 0:HC],
                                                 w[:, 2 * (g // 2) + n, kk, (g % 2) * 128:(g % 2 + 1) * 128],
                                                 k.xT[:, kk, a * HC:(a + 1) * HC], start=(kk == 0),
                                                 stop=(kk == KD - 1))
                        m.then_inc(raw, 1)
                    pe.wait_ge(raw_taken, 4)
                    for b in range(NB):
                        for kk in range(KD):
                            m = t.matmul(P[0:NP, b, 0:D // 2], k.xT[:, kk, b * NP:(b + 1) * NP], wv[:, kk, :],
                                         start=(kk == 0), stop=(kk == KD - 1))
                    m.then_inc(vs, 1)

                @block.vector
                def _(dve):
                    c, v = Chain(dve, step), nc.vector
                    iota = k.const[0:NP, C_IOTA:C_IOTA + NC]
                    c(v.memset(k.oT[:, :, :], 0.0))
                    c(v.memset(neg[:, NB, :], 0.0))
                    for b in range(NB):
                        c(v.tensor_scalar(causal[:, b, :], iota, k.const[0:NP, C_ROW + b:C_ROW + b + 1], None,
                                          ALU.is_le))
                        c(v.tensor_scalar(neg[:, b, :], iota, k.const[0:NP, C_ROW + b:C_ROW + b + 1], NEG,
                                          ALU.is_gt, ALU.mult))
                    dve.wait_ge(loaded, 16 * 6)
                    for g in range(4):
                        dve.wait_ge(raw, g + 1)
                        at = 4 * (g % 2)
                        for n in range(2):
                            c(v.tensor_tensor(part[:, n, :].rearrange("p (a n) -> p a n", a=2),
                                              P[:, at + 2 * n:at + 2 * n + 2, 0:HC],
                                              rope[:, n, :].rearrange("p (a n) -> p a n", a=2), ALU.mult))
                        to = (k.qT if g < 2 else k.kT)[:, g % 2, 0:NC]
                        v.tensor_tensor(to, part[:, 0, :], part[:, 1, :], ALU.add).then_inc(raw_taken, 1)
                        dve.wait_ge(raw_taken, g + 1)
                    dve.wait_ge(vs, 1)
                    v.tensor_copy(k.v[:, :, 0:D // 2], P[0:NP, 0:NB, 0:D // 2])
        attention(k, "causal", k.qT, k.kT, k.v, [0, 0, 64, 64], k.oT_padded, neg, causal)
        k.stack = outer
        out = k.sem("wo_products")
        with nc.Block() as block:

            @block.tensor
            def _(pe):
                pe.wait_ge(wo_loaded, 16)
                for b in range(NB):
                    for kk in range(KD):
                        m = nc.tensor.matmul(P[0:NP, b, 0:D], k.oT[:, kk, b * NP:(b + 1) * NP], wo[:, kk, :],
                                             start=(kk == 0), stop=(kk == KD - 1))
                    m.then_inc(out, 1)

            @block.vector
            def _(dve):
                for b in range(NB):
                    dve.wait_ge(out, b + 1)
                    nc.vector.tensor_tensor(k.z[:, b, :], k.xn[:, b, :], P[0:NP, b, 0:D], ALU.add)
    k.stack = k.all


HID = int(8 / 3 * D)
HT = 6
HR = -(-HID // HT)


def moe2(k):
    moe2_attention(k)
    with ExitStack() as st:
        k.stack = st
        raw = Raw(k, "moe2", HT, HR,
                  lambda sp, e, n: k.ins[("moe2_w1", "moe2_w3")[n]][bass.ds(e, 1)].rearrange(
                      "o (a p) n -> p (o a) n", p=128),
                  lambda sp, e: k.ins["moe2_w2"][bass.ds(e, 1)].rearrange("o (a p) n -> p (o a) n", p=HR), gated=True)
        normalize(k, "rms2", k.z, k.xn, k.xT, rms=True, weight=col(k, "ln2_w", 0, KD), loads=raw.load_first)
        route(k, "moe2_route", k.xT, KD, "moe2_router", None, 2, 1e-9)
        experts(k, "moe2", EXPERTS // 2, HT, HR, HT, raw, k.x, gated=True, plus=k.z)


def edge_conv(k):
    nc, P = k.nc, k.psum
    W = 2 * D
    with ExitStack() as st:
        k.stack = st
        w2 = k.sb("edge_w2", [128, 4, D])
        b2 = k.sb("edge_b2", [NP, D])
        w2_loaded = k.sem("edge_w2_loaded")
        own = k.sb("edge_own", [NP, 2, NB, W], F32R)
        ident = k.sb("edge_ident", [128, 128], F32R)
        sums = k.sb("edge_sums", [NP, NB, W])
        with ExitStack() as st2:
            k.stack = st2
            w1 = k.sb("edge_w1", [128, 4, W])
            brow = k.sb("edge_b1", [1, W])
            loaded = k.sem("edge_node_loaded")

            def loads(sp):
                sp.dma_start(w1[:, :, :], k.ins["L3_gnn_W1"].rearrange("(a p) n -> p a n", p=128)
                             ).then_inc(loaded, 16)
                sp.dma_start(brow[:, :], k.ins["L3_gnn_b1"].rearrange("(a n) -> a n", a=1)).then_inc(loaded, 16)
                sp.dma_start(w2[:, :, :], k.ins["L3_gnn_W2"].rearrange("(a p) n -> p a n", p=128)
                             ).then_inc(w2_loaded, 16)
                sp.dma_start(b2[:, :], k.ins["edge_b2"]).then_inc(w2_loaded, 16)

            normalize(k, "ln_edge", k.x, k.xn, k.xT, loads=loads)
            k.stack = st2
            other = k.sb("edge_other", [NP, NB, W])
            whole_own = k.sb("edge_whole_own", [NP, W])
            products, copied, stored, taken, step = (k.sem(f"edge_node_{s}") for s in (
                "products", "copied", "stored", "taken", "step"))
            with nc.Block() as block:

                @block.sync
                def _(sp):
                    for b in range(NB):
                        sp.wait_ge(copied, b + 1)
                        sp.dma_start(k.node_tables[b * NP:(b + 1) * NP, :], other[:, b, :]).then_inc(stored, 16)
                    sp.wait_ge(stored, 16 * NB)

                @block.tensor
                def _(pe):
                    t = nc.tensor
                    pe.wait_ge(loaded, 32)
                    for b in range(NB):
                        q = 2 * (b % 2)
                        if b >= 2:
                            pe.wait_ge(taken, b - 1)
                        for kk in range(KD):
                            t.matmul(P[0:NP, q, :], k.xT[:, kk, b * NP:(b + 1) * NP], w1[:, KD + kk, :],
                                     start=(kk == 0), stop=(kk == KD - 1))
                        for kk in range(KD):
                            t.matmul(P[0:NP, q + 1, :], k.xT[:, kk, b * NP:(b + 1) * NP], w1[:, kk, :],
                                     start=(kk == 0), stop=False)
                        t.matmul(P[0:NP, q + 1, :], k.ones[0:1, 0:NP], brow[:, :], start=False,
                                 stop=True).then_inc(products, 1)

                @block.vector
                def _(dve):
                    c, v = Chain(dve, step), nc.vector
                    v.tensor_copy(ident[:, :], k.const[:, C_ID:C_ID + 128])
                    for b in range(NB):
                        q = 2 * (b % 2)
                        dve.wait_ge(products, b + 1)
                        v.tensor_copy(other[:, b, :], P[0:NP, q, :]).then_inc(copied, 1)
                        dve.wait_ge(copied, b + 1)
                        v.tensor_tensor(whole_own[:, :], P[0:NP, q + 1, :], other[:, b, :],
                                        ALU.subtract).then_inc(taken, 1)
                        dve.wait_ge(taken, b + 1)
                        c(v.tensor_copy(own[:, 0, b, :], whole_own[:, :]))
                        c(v.tensor_tensor(own[:, 1, b, :], whole_own[:, :], own[:, 0, b, :].bitcast(F32),
                                          ALU.subtract))
        with ExitStack() as st2:
            k.stack = st2
            four = lambda n: [k.sem(f"edge_{n}{s}") for s in range(4)]
            gathered, hotT_given, hotT_ready, mine, rows_free, high_ready, low_ready = (four(n) for n in (
                "rows_gathered", "onehotT_given", "onehotT_ready", "own_given", "rows_free", "high_ready",
                "low_ready"))
            hot_ready, used = ([k.sem(f"edge_{n}{s}") for s in range(8)] for n in ("onehot_ready", "used"))
            idx_ready, idx_seen, whole, cleared = (k.sem(f"edge_{n}") for n in (
                "idx_ready", "idx_seen", "whole", "cleared"))
            idx = [k.sb(f"edge_idx{s}", [LANES, 4], U32) for s in range(2)]
            rows = [k.sb(f"edge_rows{s}", [LANES, W]) for s in range(4)]
            pre = [k.sb(f"edge_pre{s}", [LANES, W]) for s in range(4)]
            high = [k.sb(f"edge_high{s}", [LANES, W], F32R) for s in range(4)]
            low = [k.sb(f"edge_low{s}", [LANES, W], F32R) for s in range(4)]
            hot = [k.sb(f"edge_hot_{s}", [LANES, NP + 1], F32R) for s in range(8)]
            hotT = [k.sb(f"edge_hotT{s}", [NP, LANES], F32R) for s in range(4)]
            eights = lambda i, n: (n % 8, i + n // 8)
            fours = lambda i, n: (n % 4, i * 2 + n // 4)
            with nc.Block() as block:

                @block.gpsimd
                def _(pool):
                    gather_tiles(k, pool, k.e_srci, idx, idx_ready, idx_seen, rows_free, rows, k.node_rows, gathered)

                @block.tensor
                def _(pe):
                    t = nc.tensor

                    def onehotT(i, n):
                        s, m = eights(i, n)
                        q, _ = fours(i, n)
                        pe.wait_ge(hot_ready[s], m + 1)
                        if n or not isinstance(i, int):
                            p, m = fours(i, n - 1)
                            pe.wait_ge(hotT_ready[p], m + 1)
                        t.matmul(P[0:NP, 5, q * 128:(q + 1) * 128], hot[s][:, 0:NP], ident[:, :], start=True,
                                 stop=True).then_inc(hotT_given[q], 1)

                    def own_rows(b, i, n):
                        q, m = fours(i, n)
                        pe.wait_ge(hotT_ready[q], m + 1)
                        t.matmul(P[:, 6 + n % 2, :], hotT[q][:, :], own[:, 0, bass.ds(b, 1), :],
                                 start=True, stop=False)
                        t.matmul(P[:, 6 + n % 2, :], hotT[q][:, :], own[:, 1, bass.ds(b, 1), :],
                                 start=False, stop=True).then_inc(mine[q], 1)

                    open_slots(pe, *mine, *used)
                    for b in range(NB):
                        t.matmul(P[0:NP, b, :], k.zeros16[:, 0:NP], k.zeros16[:, :], start=True, stop=False)
                    first = tile_blocks(k, pe, 0)
                    for n in range(3):
                        onehotT(0, n)
                    for n in range(2):
                        own_rows(first[n], 0, n)
                    ahead = AheadWord(k, pe, "edge_blocks_ahead", 0)
                    with pe.Fori(0, ET // 8) as i:
                        of = tile_blocks(k, pe, None, ahead.take())
                        for n in range(8):
                            if n == 5:
                                ahead.load(i * 2 + 2)
                            onehotT(i, n + 3)
                            q, m = fours(i, n)
                            pe.wait_ge(rows_free[q], m + 2)
                            own_rows(of[n + 2], i, n + 2)
                            pe.wait_ge(low_ready[q], m + (2 if q == 3 else 1))
                            for part in (high, low):
                                last = t.matmul(k.psum_flat[0:NP, bass.ds(of[n] * 512, 512)], hot[n][:, 0:NP],
                                                part[q][:, :], start=False, stop=False, skip_group_check=True)
                            last.then_inc(used[n], 1)
                    for b in range(NB):
                        m = t.matmul(P[0:NP, b, :], k.zeros16[:, 0:NP], k.zeros16[:, :], start=False, stop=True)
                    m.then_inc(whole, 1)

                @block.scalar
                def _(act):
                    a = nc.scalar

                    def copy_onehotT(i, n):
                        q, m = fours(i, n)
                        act.wait_ge(hotT_given[q], m + 1)
                        act.wait_ge(mine[q], m + 1)
                        a.activation(hotT[q][:, :], P[0:NP, 5, q * 128:(q + 1) * 128],
                                     ACT.Copy).then_inc(hotT_ready[q], 1)

                    open_slots(act, *high_ready)
                    for n in range(3):
                        copy_onehotT(0, n)
                    with act.Fori(0, ET // 8) as i:
                        for n in range(8):
                            q, m = fours(i, n)
                            act.wait_ge(rows_free[q], m + 2)
                            act.wait_ge(used[(n + 4) % 8], i + 1 + n // 4)
                            a.activation(high[q][:, :], pre[q][:, :], ACT.Relu).then_inc(high_ready[q], 1)
                            copy_onehotT(i, n + 3)

                @block.vector
                def _(dve):
                    v = nc.vector

                    def onehot(i, n):
                        s, m = eights(i, n)
                        dve.wait_ge(used[s], m + 1)
                        at = slice(n, n + 1) if isinstance(i, int) else bass.ds(i * 8 + n, 1)
                        v.tensor_scalar(hot[s][:, :], k.const[:, C_IOTA:C_IOTA + NP + 1], k.e_ldst[:, at], None,
                                        ALU.is_equal).then_inc(hot_ready[s], 1)

                    def split(q, count):
                        dve.wait_ge(high_ready[q], count)
                        v.scalar_tensor_tensor(low[q][:, :], pre[q][:, :], 0.0, high[q][:, :].bitcast(F32), ALU.max,
                                               ALU.subtract).then_inc(low_ready[q], 1)

                    open_slots(dve, *rows_free)
                    v.memset(pre[3][:, :], 0.0).then_inc(cleared, 1)
                    v.tensor_copy(high[3][:, :], k.zeros[:, 0:W]).then_inc(cleared, 1)
                    dve.wait_ge(cleared, 2)
                    for n in range(3):
                        onehot(0, n)
                    with dve.Fori(0, ET // 8) as i:
                        for n in range(8):
                            onehot(i, n + 3)
                            q, m = fours(i, n)
                            dve.wait_ge(mine[q], m + 2)
                            dve.wait_ge(gathered[q], m * 16 + 16)
                            dve.wait_ge(high_ready[q], m + 1)
                            v.tensor_tensor(pre[q][:, :], P[:, 6 + n % 2, :], rows[q][:, :],
                                            ALU.add).then_inc(rows_free[q], 1)
                            split((n - 1) % 4, i * 2 + (n - 1) // 4 + 2)
                    split(3, ET // 4 + 1)
                    dve.wait_ge(whole, 1)
                    v.tensor_copy(sums[:, :, :], P[0:NP, 0:NB, :])
        with ExitStack() as st2:
            k.stack = st2
            sumsT = k.sb("edge_sumsT", [128, 4, NC])
            rdeg = k.sb("edge_rdeg", [NP, 2, NB])
            y = k.sb("edge_y", [NP, NB, D])
            turned, copied, out, step = (k.sem(f"edge_out_{s}") for s in (
                "turned", "copied", "products", "step"))
            with nc.Block() as block:

                @block.tensor
                def _(pe):
                    t = nc.tensor
                    for m in range(4):
                        for b in range(NB):
                            ins = t.transpose(P[:, 2 * m + b // 4, (b % 4) * NP:(b % 4 + 1) * NP],
                                              sums[:, b, m * 128:(m + 1) * 128], k.const[0:NP, C_ID:C_ID + NP])
                        ins.then_inc(turned, 1)
                    pe.wait_ge(w2_loaded, 32)
                    pe.wait_ge(copied, 4)
                    for b in range(NB):
                        for kk in range(4):
                            ins = t.matmul(P[0:NP, b, 0:D], sumsT[:, kk, b * NP:(b + 1) * NP], w2[:, kk, :],
                                           start=(kk == 0), stop=(kk == 3))
                        ins.then_inc(out, 1)

                @block.scalar
                def _(act):
                    for m in range(4):
                        act.wait_ge(turned, m + 1)
                        nc.scalar.activation(sumsT[:, m, 0:4 * NP], P[:, 2 * m, 0:4 * NP], ACT.Copy)
                        nc.scalar.activation(sumsT[:, m, 4 * NP:NODES], P[:, 2 * m + 1, 0:NP],
                                             ACT.Copy).then_inc(copied, 1)

                @block.vector
                def _(dve):
                    c, v = Chain(dve, step), nc.vector
                    c(v.tensor_scalar(rdeg[:, 0, :], k.deg[:, :], 1e-8, None, ALU.add))
                    c(v.reciprocal(rdeg[:, 1, :], rdeg[:, 0, :]))
                    dve.wait_ge(w2_loaded, 32)
                    for b in range(NB):
                        dve.wait_ge(out, b + 1)
                        c(v.scalar_tensor_tensor(y[:, b, :], b2[:, :], k.deg[:, b:b + 1], P[0:NP, b, 0:D], ALU.mult,
                                                 ALU.add))
                        c(v.scalar_tensor_tensor(k.x[:, b, :], y[:, b, :], rdeg[:, 1, b:b + 1], k.x[:, b, :],
                                                 ALU.mult, ALU.add))
    k.stack = k.all


def moe3_down(k, hT, tiles):
    nc, P = k.nc, k.psum
    ring = 4
    lead, PT = ring - 2, tiles // 2
    with ExitStack() as st:
        k.stack = st
        raw = [k.sb(f"moe3_raw{s}", [128, PT, D]) for s in range(2)]
        w = [k.sb(f"moe3_wd{s}", [128, 2, D], F32R) for s in range(ring)]
        braw = [k.sb(f"moe3_braw{s}", [1, D]) for s in range(2)]
        bias = [k.sb(f"moe3_bias{s}", [1, 2, 2, D], F32R) for s in range(2)]
        one = k.sb("moe3_one", [1, NP], F32R)
        two = lambda n: [k.sem(f"moe3_{n}{s}") for s in range(2)]
        raw_loaded, raw_used, b_loaded, b_ready, output_given, output_taken = (two(n) for n in (
            "raw_loaded", "raw_used", "bias_loaded", "bias_ready", "output_given", "output_taken"))
        w_high, w_ready, step_done = ([k.sem(f"moe3_{n}{s}") for s in range(ring)] for n in (
            "w_high", "w_ready", "step_done"))
        high_part, cleared = k.sem("moe3_high_part"), k.sem("moe3_cleared")

        def nth(i, s, m):
            return (i * 2 + s) * (tiles // ring) + m // ring

        def acc_of(s, b):
            return P[0:NP, 4 * s + b // 2, (b % 2) * D:(b % 2 + 1) * D]

        with nc.Block() as block:

            @block.sync
            def _(sp):

                def load(e, s, p, i, n_before):
                    sp.wait_ge(raw_used[p], n_before + 1)
                    sp.dma_start(raw[p][:, :, :], k.ins["L3_ffn_Wd"][bass.ds(e, 1)].rearrange(
                        "o (a p) n -> p (o a) n", p=128)[:, p * PT:(p + 1) * PT, :]).then_inc(raw_loaded[p], 16)
                    if p == 0:
                        sp.wait_ge(b_ready[s], i + 1)
                        sp.dma_start(braw[s][:, :], k.ins["L3_ffn_bd"][bass.ds(e, 1), :]).then_inc(b_loaded[s], 16)

                with sp.Fori(0, EXPERTS // 2) as i:
                    for s in range(2):
                        for p in range(2):
                            load(i * 2 + s, s, p, i, i * 2 + s)
                load(0, 0, 0, EXPERTS // 2, EXPERTS)

            @block.gpsimd
            def _(pool):
                open_slots(pool, *raw_used)
                with pool.Fori(0, EXPERTS // 2) as i:
                    for s in range(2):
                        for m in range(tiles):
                            c = m % ring
                            pool.wait_ge(w_high[c], nth(i, s, m) + 1)
                            nc.gpsimd.tensor_tensor(w[c][:, 1, :], raw[m // PT][:, m % PT, :],
                                                    w[c][:, 0, :].bitcast(F32), ALU.subtract).then_inc(w_ready[c], 1)
                            pool.wait_ge(w_ready[c], nth(i, s, m) + 1)
                            if m % PT == PT - 1:
                                pool.sem_inc(raw_used[m // PT], 1)

            @block.tensor
            def _(pe):
                t = nc.tensor

                def frame(s, start):
                    for b in range(3):
                        last = t.matmul(P[0:NP, 4 * s + b, :], k.zeros16[:, 0:NP], k.zeros16[:, :], start=start, stop=not start)
                    return last

                open_slots(pe, *step_done)
                pe.wait_ge(cleared, 1)
                frame(1, True)
                frame(1, False).then_inc(output_given[1], 1)
                with pe.Fori(0, EXPERTS // 2) as i:
                    for s in range(2):
                        pe.wait_ge(output_taken[s], i + 1)
                        pe.wait_ge(b_ready[s], i + 2)
                        for b in range(3):
                            for r in range(2):
                                t.matmul(P[0:NP, 4 * s + b, :], one[:, :], bias[s][:, r, :, :], start=(r == 0),
                                         stop=False)
                        for m in range(tiles):
                            c = m % ring
                            pe.wait_ge(w_ready[c], nth(i, s, m) + 1)
                            for b in range(NB):
                                last = products3(t, acc_of(s, b), [hT[:, r, m, b * NP:(b + 1) * NP] for r in range(2)],
                                                 [w[c][:, r, :] for r in range(2)], False, False)
                            last.then_inc(step_done[c], 1)
                        frame(s, False).then_inc(output_given[s], 1)

            @block.vector
            def _(dve):
                v = nc.vector

                def high_weights(e, m):
                    dve.wait_ge(raw_loaded[m // PT], e * 16 + 16)
                    v.tensor_copy(w[m % ring][:, 0, :], raw[m // PT][:, m % PT, :]).then_inc(w_high[m % ring], 1)

                def cut_bias(s, i, count):
                    dve.wait_ge(b_loaded[s], i * 16 + 16)
                    twice = braw[s][:, :].unsqueeze(1).to_broadcast([1, 2, D])
                    v.tensor_copy(bias[s][:, 0, :, :], twice).then_inc(high_part, 1)
                    dve.wait_ge(high_part, count)
                    v.tensor_tensor(bias[s][:, 1, :, :], twice, bias[s][:, 0, :, :].bitcast(F32),
                                    ALU.subtract).then_inc(b_ready[s], 1)

                def read_output(s, given, column):
                    dve.wait_ge(output_given[s], given)
                    for b in range(NB):
                        last = v.scalar_tensor_tensor(k.x[:, b, :], acc_of(s, b), column(b), k.x[:, b, :], ALU.mult,
                                                      ALU.add)
                    last.then_inc(output_taken[s], 1)

                open_slots(dve, *b_ready, output_taken[0])
                v.tensor_copy(one[:, :], k.ones[0:1, 0:NP]).then_inc(cleared, 1)
                dve.wait_ge(cleared, 1)
                cut_bias(0, 0, 1)
                for m in range(lead):
                    high_weights(0, m)
                with dve.Fori(0, EXPERTS // 2) as i:
                    for s in range(2):
                        e = i * 2 + s
                        for m in range(tiles):
                            far = m + lead
                            dve.wait_ge(step_done[far % ring], nth(i, s, m - 2) + 2)
                            high_weights(e + far // tiles, far % tiles)
                            if m == 1:
                                read_output(1 - s, i + 1, lambda b: k.gate_before[:, b, bass.ds(e, 1)])
                            if m == 5:
                                cut_bias(1 - s, i + s, e + 2)
                read_output(1, EXPERTS // 2 + 1, lambda b: k.gate[:, b, EXPERTS - 1:EXPERTS])
    k.stack = k.all


def moe3(k):
    nc, P = k.nc, k.psum
    tiles = 8
    with ExitStack() as outer:
        k.stack = outer
        hT = k.sb("moe3_hT", [128, tiles, NC])
        hT2 = k.sb("moe3_hT_parts", [128, 2, tiles, NC], F32R)
        with ExitStack() as st:
            k.stack = st
            w1 = k.sb("moe3_w1", [128, KD, tiles * 128])
            loaded = k.sem("moe3_w1_loaded")
            normalize(k, "ln_moe3", k.x, k.xn, k.xT, loads=lambda sp: sp.dma_start(
                w1[:, :, :], k.ins["L3_ffn_W1"].rearrange("(a p) n -> p a n", p=128)).then_inc(loaded, 16))
            k.stack = st
            given, taken = ([k.sem(f"moe3_up_{n}{s}") for s in range(2)] for n in ("given", "taken"))
            with nc.Block() as block:

                @block.tensor
                def _(pe):
                    pe.wait_ge(loaded, 16)
                    for m in range(tiles):
                        q = m % 2
                        if m >= 2:
                            pe.wait_ge(taken[q], m // 2)
                        for a in range(2):
                            for kk in range(KD):
                                ins = nc.tensor.matmul(P[:, 2 * q + a, 0:HC], w1[:, kk, m * 128:(m + 1) * 128],
                                                       k.xT[:, kk, a * HC:(a + 1) * HC], start=(kk == 0),
                                                       stop=(kk == KD - 1))
                        ins.then_inc(given[q], 1)

                @block.scalar
                def _(act):
                    for m in range(tiles):
                        act.wait_ge(given[m % 2], m // 2 + 1)
                        nc.scalar.activation(hT[:, m, :].rearrange("p (a n) -> p a n", a=2),
                                             P[:, 2 * (m % 2):2 * (m % 2) + 2, 0:HC], ACT.Gelu,
                                             bias=col(k, "moe3_b1", m)).then_inc(taken[m % 2], 1)

                @block.vector
                def _(dve):
                    c = Chain(dve, k.sem("moe3_parts"))
                    for m in range(tiles):
                        dve.wait_ge(taken[m % 2], m // 2 + 1)
                        cut(nc.vector, hT[:, m, :], hT2[:, 0, m, :], hT2[:, 1, m, :], c)
        route(k, "moe3_route", hT, tiles, "moe3_router", "L3_ffn_bg", 1, None)
        moe3_down(k, hT2, tiles)
    k.stack = k.all


def store(k):
    done = k.sem("stored")
    with k.nc.Block() as block:

        @block.sync
        def _(sp):
            sp.dma_start(k.out.rearrange("(b p) d -> p b d", b=NB), k.x[:, :, :]).then_inc(done, 16)
            sp.wait_ge(done, 16)
STAGES = [edges, conv_layers, moe0, sage, moe1, rgcn, moe2, edge_conv, moe3, store]


def build(nc, ins, out, stages=None):
    k = Kernel(nc, ins, out)
    with k.all:
        k.const = k.sb("const", [128, C_END])
        k.ones = k.sb("ones", [128, 512])
        k.zeros = k.sb("zeros", [128, 512])
        k.zeros16 = k.sb("zeros16", [1, 512], BF16)
        k.x = k.sb("x_res", [NP, NB, D])
        k.xn = k.sb("xn", [NP, NB, D])
        k.xT = k.sb("xT", [128, KD, NC])
        k.C = k.sb("C", [NP, NB, NC])
        k.CT = k.sb("CT", [NP, NB, NC])
        k.deg = k.sb("deg", [NP, NB])
        k.e_ldst = k.sb("e_ldst", [LANES, ET + AHEAD])
        k.e_src = k.sb("e_src", [LANES, ET])
        k.e_w = k.sb("e_w", [LANES, ET])
        k.e_row = k.sb("e_row", [LANES, ET], U32)
        k.e_srci = k.sb("e_srci", [LANES, ET], U32)
        k.e_blk = k.sb("e_blk", [1, ET // 4 + 4], I32)
        k.negC = k.sb("negC", [NP, NB + 1, NC], BF16)
        k.ident16 = k.sb("ident16", [128, 128], BF16)
        k.wconv = k.sb("wconv", [128, 3, KD, 4 * D])
        k.rgcn_w = k.wconv[:, 0:2].rearrange("p i a n -> p (i a n)").rearrange("p (a r d) -> p a r d", a=KD, r=RELS)
        k.wconv_loaded = k.all.enter_context(nc.semaphore("wconv_loaded"))
        k.coeff = k.sb("rgcn_coeff", [128, 2, RELS * RELS])
        k.basis_loaded = k.all.enter_context(nc.semaphore("rgcn_basis_loaded"))
        k.col = k.sb("columns", [128, sum(COLS.values())])
        k.brow = k.sb("brow", [1, 2 * D])
        k.qT = k.sb("qT", [128, KD, NODES + NP])
        k.kT = k.sb("kT", [128, KD, NC])
        k.v = k.sb("v", [NP, NB, D])
        k.o = k.sb("o", [NP, NB, D])
        k.oT_padded = k.sb("oT", [128, KD, NP + NC])
        k.oT = k.oT_padded[:, :, NP:NP + NC]
        k.gates = k.sb("gates", [NP, 1 + NB * EXPERTS])
        k.gate = k.gates[:, 1:].rearrange("p (b e) -> p b e", b=NB)
        k.gate_before = k.gates[:, 0:NB * EXPERTS].rearrange("p (b e) -> p b e", b=NB)
        k.z = k.sb("z", [NP, NB, D])
        k.picked = k.sb("picked", [1, 2], I32)
        k.picked_b1 = k.sb("picked_b1", [128, 8])
        k.tables = nc.dram_tensor("edge_tables", (NODES, RELS * D), F32).ap()
        k.table_rows = k.tables.rearrange("n (r d) -> (n r) d", d=D)
        k.node_tables = nc.dram_tensor("node_tables", (NODES, 2 * D), F32).ap()
        k.node_rows = k.node_tables
        k.psum = k.all.enter_context(nc.psum_tensor("psum", [128, 8, 512], F32))
        k.psum_flat = k.psum[:, :, :].rearrange("p b n -> p (b n)")
        for s in (stages or STAGES):
            s(k)
            k.end_layer()
    return k


def layout(i):
    a = {"const": constants()}
    a["x"] = i["x"].reshape(NB, NP, D).transpose(1, 0, 2)
    for n in ("src", "dst", "edge_type_8", "edge_weight1"):
        a[n] = i[n].reshape(EP, EC)

    def tiles(v):
        v = v.reshape(*v.shape[:-1], -1, 128)
        return np.moveaxis(v, -1, 0).reshape(128, -1)

    def padded(v):
        v = np.concatenate([v, np.zeros_like(v[:1])]).reshape(EXPERTS + 1, KD, 128)
        return v.transpose(2, 1, 0).reshape(128, -1)

    def router(w):
        return w.reshape(-1, 128, EXPERTS).transpose(1, 0, 2).reshape(128, -1)

    c = {"conv_bias": tiles(np.stack([i["L0_gnn_bq"], i["L0_gnn_bk"], i["L0_gnn_bs"]], 1)),
         "bn_gamma": tiles(i["L0_gnn_bn_gamma"]), "bn_beta": tiles(i["L0_gnn_bn_beta"]),
         "moe0_ln_g": padded(i["L0_ffn_ln_g"]), "moe0_ln_b": padded(i["L0_ffn_ln_b"]),
         "moe0_b1": tiles(i["L0_ffn_b1"]), "moe3_b1": tiles(i["L3_ffn_b1"]),
         "ln1_w": tiles(i["L2_ffn_ln1_w"]), "ln2_w": tiles(i["L2_ffn_ln2_w"]),
         "moe0_router": router(i["L0_ffn_Wr"]), "moe1_router": router(i["L1_ffn_Wr"]),
         "moe2_router": router(i["L2_ffn_router_w"].T), "moe3_router": router(i["L3_ffn_Wg"])}
    a["cols"] = np.concatenate([c[n] for n in COLS], 1)
    a["coeff_rows"] = np.broadcast_to(i["L2_gnn_coeff"].reshape(1, -1), (128, i["L2_gnn_coeff"].size))
    a["moe1_b1"] = i["L1_ffn_b1"].reshape(EXPERTS, -1, 128).transpose(0, 2, 1)
    for n in ("gamma", "beta"):
        a[f"moe1_{n}"] = np.broadcast_to(i[f"L1_ffn_{n}"].reshape(1, D), (NP, D))
    a["edge_b2"] = np.broadcast_to(i["L3_gnn_b2"].reshape(1, D), (NP, D))
    swap = np.arange(D).reshape(-1, 2, 32)[:, ::-1].reshape(-1)
    wq = i["L2_ffn_wq"]
    wk = i["L2_ffn_wk"].reshape(2, 1, 64, D).repeat(2, 1).reshape(D, D)
    a["rope_wq"], a["rope_wq_swapped"] = wq.T, wq[swap].T
    a["rope_wk"], a["rope_wk_swapped"] = wk.T, wk[swap].T
    a["moe2_wv"], a["moe2_wo"] = i["L2_ffn_wv"].T, i["L2_ffn_wo"].T
    a["rope"] = rope_tables()
    wide = lambda w: np.concatenate([w, np.zeros((EXPERTS, HT * HR - HID, D), np.float32)], 1)
    for n, m in (("moe2_w1", "L2_ffn_w1"), ("moe2_w3", "L2_ffn_w3")):
        a[n] = wide(i[m]).transpose(0, 2, 1)
    a["moe2_w2"] = wide(i["L2_ffn_w2"].transpose(0, 2, 1))
    for n in i:
        if n not in a:
            a[n] = i[n]
    return {n: np.ascontiguousarray(v) for n, v in a.items()}


def rope_tables():
    hd = 64
    inv = 1.0 / 10000.0 ** (np.arange(0, hd, 2, dtype=np.float32) / hd)
    f = np.outer(np.arange(NC, dtype=np.float32), inv)
    e = np.concatenate([f, f], -1).T
    sign = np.where(np.arange(hd) < hd // 2, -1.0, 1.0)[:, None]
    both = np.stack([np.cos(e), np.sin(e) * sign], 1)
    return np.concatenate([both, both]).astype(np.float32)


def kernel(**inputs):
    import concourse.bacc as bacc
    from concourse.bass_utils import run_bass_kernel_spmd

    arrays = layout({n: np.asarray(v) for n, v in inputs.items()})
    nc = bacc.Bacc("TRN2", target_bir_lowering=False, num_devices=1)
    ins = {n: nc.dram_tensor(f"in_{n}", a.shape, mybir.dt.from_np(a.dtype), kind="ExternalInput").ap()
           for n, a in arrays.items()}
    out = nc.dram_tensor("out", (NODES, D), F32, kind="ExternalOutput").ap()
    build(nc, ins, out)
    r = run_bass_kernel_spmd(nc, [{f"in_{n}": a for n, a in arrays.items()}], core_ids=[0])
    return r.results[0]["out"]
```
